# Optimizing a Trainium2 kernel written in Bass

```python
import numpy as np
import jax
import jax.numpy as jnp

def _softmax(x, axis=-1):
    return jax.nn.softmax(x, axis=axis)

def _gelu(x):
    return jax.nn.gelu(x, approximate=True)

def _silu(x):
    return jax.nn.silu(x)

def _sigmoid(x):
    return jax.nn.sigmoid(x)

def _layernorm(x, axis=-1, eps=1e-05):
    m = jnp.mean(x, axis=axis, keepdims=True)
    v = jnp.var(x, axis=axis, keepdims=True)
    return (x - m) / jnp.sqrt(v + eps)

def _scatter_add(tgt, idx, src, axis=0):
    return tgt.at[idx].add(src)

def _segment_sum(src, seg, n):
    return jax.ops.segment_sum(src, seg, n)
kernel_name = 'mk_perceiver_d4_seqx_r4_5fe394'

def setup_inputs(seed: int=0):
    np.random.seed(seed)
    _w = jnp.asarray

    def _rec_inputs():
        import jax
        import jax.numpy as jnp
        _rk = jax.random.key(seed)
        x = -0.0002928 + 1 * jax.random.normal(jax.random.fold_in(_rk, 1), (64, 32, 256), jnp.float32)
        _lenS = 32 - jax.random.randint(jax.random.fold_in(_rk, 7), (64,), 0, max(1, 32 // 4) + 1, jnp.int32)
        _lenS2 = 257 - jax.random.randint(jax.random.fold_in(_rk, 8), (64,), 0, max(1, 257 // 4) + 1, jnp.int32)
        _ctx_1024P = jax.random.normal(jax.random.fold_in(_rk, 11), (64, 16, 256), jnp.float32)
        _ctx_1024c = jax.random.dirichlet(jax.random.fold_in(_rk, 511), 0.3 * jnp.ones((16,), jnp.float32), (64, 257))
        _ctx_1024t = jnp.einsum('bsk,bkd->bsd', _ctx_1024c, _ctx_1024P)
        _ctx_1024t = _ctx_1024t * jax.lax.rsqrt(jnp.mean(jnp.square(_ctx_1024t)) + 1e-12) * 0.953939
        ctx_1024 = -1.39393e-06 + 0.999914 * (_ctx_1024t + 0.3 * jax.random.normal(jax.random.fold_in(_rk, 611), (64, 257, 256), jnp.float32))
        fside_BxSxS2_0 = -1.47943e-05 + 1.00017 * jax.random.normal(jax.random.fold_in(_rk, 13), (64, 32, 257), jnp.float32)
        _validS = jnp.arange(32)[None, :] < _lenS[:, None]
        _validS2 = jnp.arange(257)[None, :] < _lenS2[:, None]
        _causal = jnp.tril(jnp.ones((32, 32), dtype=bool))
        mask_Bx1xS2x1_bk0 = jnp.logical_not(jnp.ones((64, 1, 257, 1), dtype=bool))
        return (x, ctx_1024, fside_BxSxS2_0, mask_Bx1xS2x1_bk0)
    x, ctx_1024, fside_BxSxS2_0, mask_Bx1xS2x1_bk0 = _rec_inputs()

    def _L0_xattn_setup():
        import jax, jax.numpy as jnp
        import numpy as np
        import math
        D_MODEL = 256
        N_HEADS = 16
        HEAD_DIM = D_MODEL // N_HEADS
        MLP_DIM = 4 * D_MODEL
        B, L, M = (2, 512, 512)

        def layer_norm(x, g, b, eps=1e-05):
            mu = jnp.mean(x, axis=-1, keepdims=True)
            var = jnp.var(x, axis=-1, keepdims=True)
            return (x - mu) * jax.lax.rsqrt(var + eps) * g + b

        def mha(q_in, k_in, qW, wW, oW, mask=None):
            b, l, _ = q_in.shape
            m = k_in.shape[1]
            q = (q_in @ qW).reshape(b, l, HEAD_DIM, N_HEADS)
            k = (k_in @ wW).reshape(b, m, HEAD_DIM, N_HEADS)
            s = jnp.einsum('bldn,bmdn->blmn', q, k)
            if mask is not None:
                s = jnp.where(mask, -1000000000.0, s)
            s = s / math.sqrt(HEAD_DIM)
            w = jax.nn.softmax(s, axis=2)
            x = jnp.einsum('blmn,bmdn->bldn', w, k)
            x = x.reshape(b, l, HEAD_DIM * N_HEADS)
            return x @ oW
        key = jax.random.key(seed)
        ks = jax.random.split(key, 16)
        sc = 1.0 / math.sqrt(D_MODEL)
        inp = {'x': jax.random.normal(ks[0], (B, L, D_MODEL), jnp.float32), 'enc_output': jax.random.normal(ks[1], (B, M, D_MODEL), jnp.float32), 'mask': jax.random.randint(ks[2], (B, 1, M, 1), 0, 2).astype(bool), 'q1W': jax.random.normal(ks[3], (D_MODEL, D_MODEL), jnp.float32) * sc, 'w1W': jax.random.normal(ks[4], (D_MODEL, D_MODEL), jnp.float32) * sc, 'o1W': jax.random.normal(ks[5], (D_MODEL, D_MODEL), jnp.float32) * sc, 'q2W': jax.random.normal(ks[6], (D_MODEL, D_MODEL), jnp.float32) * sc, 'w2W': jax.random.normal(ks[7], (D_MODEL, D_MODEL), jnp.float32) * sc, 'o2W': jax.random.normal(ks[8], (D_MODEL, D_MODEL), jnp.float32) * sc, 'ffW1': jax.random.normal(ks[9], (D_MODEL, MLP_DIM), jnp.float32) * sc, 'ffb1': jnp.zeros((MLP_DIM,), jnp.float32), 'ffW2': jax.random.normal(ks[10], (MLP_DIM, D_MODEL), jnp.float32) * sc, 'ffb2': jnp.zeros((D_MODEL,), jnp.float32), 'g1': jnp.ones((D_MODEL,), jnp.float32), 'b1': jnp.zeros((D_MODEL,), jnp.float32), 'g2': jnp.ones((D_MODEL,), jnp.float32), 'b2': jnp.zeros((D_MODEL,), jnp.float32), 'g3': jnp.ones((D_MODEL,), jnp.float32), 'b3': jnp.zeros((D_MODEL,), jnp.float32)}
        return inp
    _L0_xattn_all = _L0_xattn_setup()
    _L0_xattn_in = {k: v for k, v in _L0_xattn_all.items() if k in ('q1W', 'w1W', 'o1W', 'q2W', 'w2W', 'o2W', 'ffW1', 'ffb1', 'ffW2', 'ffb2', 'g1', 'b1', 'g2', 'b2', 'g3', 'b3')}
    del _L0_xattn_all

    def _L0_attn_setup():
        import jax, jax.numpy as jnp
        import numpy as np
        B, S, E = (4, 512, 256)
        HIDDEN = 256
        HEADS = 16
        key = jax.random.key(seed)
        k0, k1, k2, k3, k4 = jax.random.split(key, 5)
        inputs = jax.random.normal(k0, (B, S, E), dtype=jnp.float32)
        W_qkv = jax.random.normal(k1, (E, 3 * HIDDEN), dtype=jnp.float32) * 0.02
        b_qkv = jnp.zeros((3 * HIDDEN,), dtype=jnp.float32)
        W_out = jax.random.normal(k2, (HIDDEN, HIDDEN), dtype=jnp.float32) * 0.02
        b_out = jnp.zeros((HIDDEN,), dtype=jnp.float32)
        return {'inputs': inputs, 'W_qkv': W_qkv, 'b_qkv': b_qkv, 'W_out': W_out, 'b_out': b_out}
    _L0_attn_all = _L0_attn_setup()
    _L0_attn_in = {k: v for k, v in _L0_attn_all.items() if k in ('W_qkv', 'b_qkv', 'W_out', 'b_out')}
    del _L0_attn_all

    def _L0_ffn_setup():
        import jax, jax.numpy as jnp
        import numpy as np
        B, T, C = (4, 512, 256)
        E, H, K = (8, 512, 2)
        key = jax.random.key(seed)
        ks = jax.random.split(key, 7)
        s_in = 1.0 / np.sqrt(C)
        s_hid = 1.0 / np.sqrt(H)
        return {'x': jax.random.normal(ks[0], (B, T, C), dtype=jnp.float32), 'gate_w': jax.random.uniform(ks[1], (C, E), jnp.float32, -s_in, s_in), 'gate_b': jnp.zeros((E,), jnp.float32), 'w1': jax.random.uniform(ks[2], (E, C, H), jnp.float32, -s_in, s_in), 'b1': jax.random.uniform(ks[3], (E, H), jnp.float32, -s_in, s_in), 'w2': jax.random.uniform(ks[4], (E, H, C), jnp.float32, -s_hid, s_hid), 'b2': jax.random.uniform(ks[5], (E, C), jnp.float32, -s_hid, s_hid)}
    _L0_ffn_all = _L0_ffn_setup()
    _L0_ffn_in = {k: v for k, v in _L0_ffn_all.items() if k in ('gate_w', 'gate_b', 'w1', 'b1', 'w2', 'b2')}
    del _L0_ffn_all

    def _L1_xattn_setup():
        import jax, jax.numpy as jnp
        import numpy as np
        EMBED_DIM = 256
        NUM_HEADS = 16
        HEAD_DIM = EMBED_DIM // NUM_HEADS
        SCALE = HEAD_DIM ** (-0.5)
        key = jax.random.key(seed)
        k1, k2, k3, k4, k5, k6 = jax.random.split(key, 6)
        B, Tq, Tk = (2, 512, 512)
        std = EMBED_DIM ** (-0.5)
        return {'x_q': jax.random.normal(k1, (B, Tq, EMBED_DIM), jnp.float32), 'x_kv': jax.random.normal(k2, (B, Tk, EMBED_DIM), jnp.float32), 'w_q': jax.random.normal(k3, (EMBED_DIM, EMBED_DIM), jnp.float32) * std, 'w_kv': jax.random.normal(k4, (EMBED_DIM, 2 * EMBED_DIM), jnp.float32) * std, 'w_proj': jax.random.normal(k5, (EMBED_DIM, EMBED_DIM), jnp.float32) * std, 'w_rel': jax.random.normal(k6, (1, NUM_HEADS), jnp.float32) * 0.02}
    _L1_xattn_all = _L1_xattn_setup()
    _L1_xattn_in = {k: v for k, v in _L1_xattn_all.items() if k in ('w_q', 'w_kv', 'w_proj', 'w_rel')}
    del _L1_xattn_all

    def _L1_attn_setup():
        import jax, jax.numpy as jnp
        import numpy as np
        EPS = 1e-08

        def rms_norm_multihead(x, weight):
            x32 = x.astype(jnp.float32)
            normed = x32 * jax.lax.rsqrt(jnp.mean(x32 * x32, axis=-1, keepdims=True) + EPS)
            return normed.astype(x.dtype) * weight
        key = jax.random.key(seed)
        k0, k1, k2 = jax.random.split(key, 3)
        B, L, D, H = (2, 256, 256, 16)
        d = D // H
        X = jax.random.normal(k0, (B, L, D), dtype=jnp.float32)
        Wq = jax.random.normal(k1, (D, D), dtype=jnp.float32) * 0.02
        Wv = jax.random.normal(k2, (D, D), dtype=jnp.float32) * 0.02
        q_norm_w = jnp.ones((H, d), dtype=jnp.float32)
        v_norm_w = jnp.ones((H, d), dtype=jnp.float32)
        return {'X': X, 'Wq': Wq, 'Wv': Wv, 'q_norm_w': q_norm_w, 'v_norm_w': v_norm_w}
    _L1_attn_all = _L1_attn_setup()
    _L1_attn_in = {k: v for k, v in _L1_attn_all.items() if k in ('Wq', 'Wv', 'q_norm_w', 'v_norm_w')}
    del _L1_attn_all

    def _L1_ffn_setup():
        import jax, jax.numpy as jnp
        import numpy as np
        H = 16
        EPS = 1e-05

        def layernorm(x, g, b):
            m = jnp.mean(x, axis=-1, keepdims=True)
            v = jnp.mean((x - m) ** 2, axis=-1, keepdims=True)
            return (x - m) * jax.lax.rsqrt(v + EPS) * g + b
        key = jax.random.key(seed)
        B, S, D, E = (4, 512, 256, 8)
        ks = jax.random.split(key, 16)
        s = 0.02
        inp = {'x': jax.random.normal(ks[0], (B, S, D), jnp.float32), 'Wq': jax.random.normal(ks[1], (D, D), jnp.float32) * s, 'bq': jnp.zeros((D,), jnp.float32), 'Wk': jax.random.normal(ks[2], (D, D), jnp.float32) * s, 'bk': jnp.zeros((D,), jnp.float32), 'Wv': jax.random.normal(ks[3], (D, D), jnp.float32) * s, 'bv': jnp.zeros((D,), jnp.float32), 'Wo': jax.random.normal(ks[4], (D, D), jnp.float32) * s, 'bo': jnp.zeros((D,), jnp.float32), 'g1': jnp.ones((D,), jnp.float32), 'be1': jnp.zeros((D,), jnp.float32), 'g2': jnp.ones((D,), jnp.float32), 'be2': jnp.zeros((D,), jnp.float32), 'Wg': jax.random.normal(ks[5], (D, E), jnp.float32) * s, 'bg': jnp.zeros((E,), jnp.float32), 'We': jax.random.normal(ks[6], (E, D, D), jnp.float32) * s, 'bexp': jnp.zeros((E, D), jnp.float32)}
        return inp
    _L1_ffn_all = _L1_ffn_setup()
    _L1_ffn_in = {k: v for k, v in _L1_ffn_all.items() if k in ('Wq', 'bq', 'Wk', 'bk', 'Wv', 'bv', 'Wo', 'bo', 'g1', 'be1', 'g2', 'be2', 'Wg', 'bg', 'We', 'bexp')}
    del _L1_ffn_all

    def _L2_xattn_setup():
        import jax, jax.numpy as jnp
        import numpy as np
        B, L_ENC, L_DEC, D = (16, 128, 128, 256)
        key = jax.random.key(seed)
        k1, k2, k3, k4, k5, k6 = jax.random.split(key, 6)
        encoder_hc = jax.random.normal(k1, (B, L_ENC, D), dtype=jnp.float32)
        decoder_hq = jax.random.normal(k2, (B, L_DEC, D), dtype=jnp.float32)
        w_sim = jax.random.normal(k3, (3 * D,), dtype=jnp.float32) * 0.02
        b_sim = jax.random.normal(k4, (1,), dtype=jnp.float32) * 0.02
        W_qv = jax.random.normal(k5, (4 * D, D), dtype=jnp.float32) * 0.02
        b_qv = jax.random.normal(k6, (D,), dtype=jnp.float32) * 0.02
        return {'encoder_hc': encoder_hc, 'decoder_hq': decoder_hq, 'w_sim': w_sim, 'b_sim': b_sim, 'W_qv': W_qv, 'b_qv': b_qv}
    _L2_xattn_all = _L2_xattn_setup()
    _L2_xattn_in = {k: v for k, v in _L2_xattn_all.items() if k in ('w_sim', 'b_sim', 'W_qv', 'b_qv')}
    del _L2_xattn_all

    def _L2_attn_setup():
        import jax, jax.numpy as jnp
        import numpy as np
        B, S, D = (4, 512, 256)

        def _xavier(key, shape):
            bound = float(np.sqrt(6.0 / (shape[0] + shape[1])))
            return jax.random.uniform(key, shape, dtype=jnp.float32, minval=-bound, maxval=bound)
        key = jax.random.key(seed)
        k0, k1, k2, k3 = jax.random.split(key, 4)
        return {'embeddings': jax.random.normal(k0, (B, S, D), dtype=jnp.float32), 'W_Q': _xavier(k1, (D, D)), 'W_K': _xavier(k2, (D, D)), 'W_V': _xavier(k3, (D, D))}
    _L2_attn_all = _L2_attn_setup()
    _L2_attn_in = {k: v for k, v in _L2_attn_all.items() if k in ('W_Q', 'W_K', 'W_V')}
    del _L2_attn_all

    def _L2_ffn_setup():
        import jax, jax.numpy as jnp
        import numpy as np
        D_MODEL = 256
        EXPANSION = 4
        D_HIDDEN = D_MODEL * EXPANSION
        NUM_STAGES = int(np.log2(D_HIDDEN))

        def butterfly(y, weights, dim):
            lead = y.shape[:-1]
            for stage in range(weights.shape[0]):
                s = 2 ** stage
                nb = dim // (2 * s)
                yr = y.reshape(*lead, nb, 2, s)
                a = yr[..., 0, :]
                b = yr[..., 1, :]
                w = weights[stage].reshape(nb, s, 2, 2)
                na = w[..., 0, 0] * a + w[..., 0, 1] * b
                nb2 = w[..., 1, 0] * a + w[..., 1, 1] * b
                y = jnp.stack([na, nb2], axis=-2).reshape(*lead, dim)
            return y
        key = jax.random.key(seed)
        ks = jax.random.split(key, 6)
        B, S = (4, 512)
        x = jax.random.normal(ks[0], (B, S, D_MODEL), jnp.float32)
        W_exp = jax.random.normal(ks[1], (D_MODEL, D_HIDDEN), jnp.float32) * 0.02
        b_exp = jnp.zeros((D_HIDDEN,), jnp.float32)
        up_weights = jax.random.normal(ks[2], (NUM_STAGES, D_HIDDEN // 2, 2, 2), jnp.float32) * 0.02
        up_bias = jnp.zeros((D_HIDDEN,), jnp.float32)
        down_weights = jax.random.normal(ks[3], (NUM_STAGES, D_HIDDEN // 2, 2, 2), jnp.float32) * 0.02
        W_con = jax.random.normal(ks[4], (D_HIDDEN, D_MODEL), jnp.float32) * 0.02
        b_con = jnp.zeros((D_MODEL,), jnp.float32)
        down_bias = jnp.zeros((D_MODEL,), jnp.float32)
        return dict(x=x, W_exp=W_exp, b_exp=b_exp, up_weights=up_weights, up_bias=up_bias, down_weights=down_weights, W_con=W_con, b_con=b_con, down_bias=down_bias)
    _L2_ffn_all = _L2_ffn_setup()
    _L2_ffn_in = {k: v for k, v in _L2_ffn_all.items() if k in ('W_exp', 'b_exp', 'up_weights', 'up_bias', 'down_weights', 'W_con', 'b_con', 'down_bias')}
    del _L2_ffn_all

    def _L3_xattn_setup():
        import jax, jax.numpy as jnp
        import numpy as np
        D = 256
        key = jax.random.key(seed)
        ks = jax.random.split(key, 13)
        B, S, d = (4, 512, D)
        inp = {'q_in': jax.random.normal(ks[0], (B, S, d), jnp.float32), 'k_in': jax.random.normal(ks[1], (B, S, d), jnp.float32), 'v_in': jax.random.normal(ks[2], (B, S, d), jnp.float32), 'phi_risk': jax.random.normal(ks[3], (B, S, S), jnp.float32), 'phi_prio': jax.random.normal(ks[4], (B, S, S), jnp.float32), 'phi_impl': jax.random.normal(ks[5], (B, S, S), jnp.float32), 'Wq': jax.random.normal(ks[6], (d, d), jnp.float32) / np.sqrt(d), 'bq': jax.random.normal(ks[7], (d,), jnp.float32) * 0.01, 'Wk': jax.random.normal(ks[8], (d, d), jnp.float32) / np.sqrt(d), 'bk': jax.random.normal(ks[9], (d,), jnp.float32) * 0.01, 'Wv': jax.random.normal(ks[10], (d, d), jnp.float32) / np.sqrt(d), 'bv': jax.random.normal(ks[11], (d,), jnp.float32) * 0.01, 'beta_risk': jnp.float32(0.1), 'beta_prio': jnp.float32(0.1), 'beta_impl': jnp.float32(0.1)}
        return inp
    _L3_xattn_all = _L3_xattn_setup()
    _L3_xattn_in = {k: v for k, v in _L3_xattn_all.items() if k in ('Wq', 'bq', 'Wk', 'bk', 'Wv', 'bv', 'beta_risk', 'beta_prio', 'beta_impl')}
    del _L3_xattn_all

    def _L3_attn_setup():
        import jax, jax.numpy as jnp
        import numpy as np
        B, S, D = (2, 512, 256)
        H, P = (16, 64)
        NUM_OUT = 256
        key = jax.random.key(seed)
        ks = jax.random.split(key, 9)
        sc = 0.05
        return {'x': jax.random.normal(ks[0], (B, S, D), jnp.float32), 'q_w': jax.random.normal(ks[1], (H, P, D), jnp.float32) * sc, 'q_b': jax.random.normal(ks[2], (H, 1, P), jnp.float32) * sc, 'k_w': jax.random.normal(ks[3], (H, P, D), jnp.float32) * sc, 'k_b': jax.random.normal(ks[4], (H, 1, P), jnp.float32) * sc, 'v_w': jax.random.normal(ks[5], (H, P, D), jnp.float32) * sc, 'v_b': jax.random.normal(ks[6], (H, 1, P), jnp.float32) * sc, 'l_w': jax.random.normal(ks[7], (NUM_OUT, P * H), jnp.float32) * sc, 'l_b': jax.random.normal(ks[8], (1, NUM_OUT), jnp.float32) * sc}
    _L3_attn_all = _L3_attn_setup()
    _L3_attn_in = {k: v for k, v in _L3_attn_all.items() if k in ('q_w', 'q_b', 'k_w', 'k_b', 'v_w', 'v_b', 'l_w', 'l_b')}
    del _L3_attn_all

    def _L3_ffn_setup():
        import jax, jax.numpy as jnp
        import numpy as np
        B, S, D = (2, 512, 256)
        E, K, F = (16, 2, 128)
        FS = 256
        key = jax.random.key(seed)
        ks = jax.random.split(key, 8)

        def w(k, shape, fan_in):
            return jax.random.normal(k, shape, jnp.float32) / np.sqrt(fan_in).astype(np.float32)
        return {'x': jax.random.normal(ks[0], (B, S, D), jnp.float32), 'Wr': w(ks[1], (D, E), D), 'Wg': w(ks[2], (E, D, F), D), 'Wu': w(ks[3], (E, D, F), D), 'Wd': w(ks[4], (E, F, D), F), 'Sg': w(ks[5], (D, FS), D), 'Su': w(ks[6], (D, FS), D), 'Sd': w(ks[7], (FS, D), FS)}
    _L3_ffn_all = _L3_ffn_setup()
    _L3_ffn_in = {k: v for k, v in _L3_ffn_all.items() if k in ('Wr', 'Wg', 'Wu', 'Wd', 'Sg', 'Su', 'Sd')}
    del _L3_ffn_all
    return {'x': x, 'ctx_1024': ctx_1024, 'fside_BxSxS2_0': fside_BxSxS2_0, 'mask_Bx1xS2x1_bk0': mask_Bx1xS2x1_bk0, 'L0_xattn_q1W': _L0_xattn_in['q1W'], 'L0_xattn_w1W': _L0_xattn_in['w1W'], 'L0_xattn_o1W': _L0_xattn_in['o1W'], 'L0_xattn_q2W': _L0_xattn_in['q2W'], 'L0_xattn_w2W': _L0_xattn_in['w2W'], 'L0_xattn_o2W': _L0_xattn_in['o2W'], 'L0_xattn_ffW1': _L0_xattn_in['ffW1'], 'L0_xattn_ffb1': _L0_xattn_in['ffb1'], 'L0_xattn_ffW2': _L0_xattn_in['ffW2'], 'L0_xattn_ffb2': _L0_xattn_in['ffb2'], 'L0_xattn_g1': _L0_xattn_in['g1'], 'L0_xattn_b1': _L0_xattn_in['b1'], 'L0_xattn_g2': _L0_xattn_in['g2'], 'L0_xattn_b2': _L0_xattn_in['b2'], 'L0_xattn_g3': _L0_xattn_in['g3'], 'L0_xattn_b3': _L0_xattn_in['b3'], 'L0_attn_W_qkv': _L0_attn_in['W_qkv'], 'L0_attn_b_qkv': _L0_attn_in['b_qkv'], 'L0_attn_W_out': _L0_attn_in['W_out'], 'L0_attn_b_out': _L0_attn_in['b_out'], 'L0_ffn_gate_w': _L0_ffn_in['gate_w'], 'L0_ffn_gate_b': _L0_ffn_in['gate_b'], 'L0_ffn_w1': _L0_ffn_in['w1'], 'L0_ffn_b1': _L0_ffn_in['b1'], 'L0_ffn_w2': _L0_ffn_in['w2'], 'L0_ffn_b2': _L0_ffn_in['b2'], 'L1_xattn_w_q': _L1_xattn_in['w_q'], 'L1_xattn_w_kv': _L1_xattn_in['w_kv'], 'L1_xattn_w_proj': _L1_xattn_in['w_proj'], 'L1_xattn_w_rel': _L1_xattn_in['w_rel'], 'L1_attn_Wq': _L1_attn_in['Wq'], 'L1_attn_Wv': _L1_attn_in['Wv'], 'L1_attn_q_norm_w': _L1_attn_in['q_norm_w'], 'L1_attn_v_norm_w': _L1_attn_in['v_norm_w'], 'L1_ffn_Wq': _L1_ffn_in['Wq'], 'L1_ffn_bq': _L1_ffn_in['bq'], 'L1_ffn_Wk': _L1_ffn_in['Wk'], 'L1_ffn_bk': _L1_ffn_in['bk'], 'L1_ffn_Wv': _L1_ffn_in['Wv'], 'L1_ffn_bv': _L1_ffn_in['bv'], 'L1_ffn_Wo': _L1_ffn_in['Wo'], 'L1_ffn_bo': _L1_ffn_in['bo'], 'L1_ffn_g1': _L1_ffn_in['g1'], 'L1_ffn_be1': _L1_ffn_in['be1'], 'L1_ffn_g2': _L1_ffn_in['g2'], 'L1_ffn_be2': _L1_ffn_in['be2'], 'L1_ffn_Wg': _L1_ffn_in['Wg'], 'L1_ffn_bg': _L1_ffn_in['bg'], 'L1_ffn_We': _L1_ffn_in['We'], 'L1_ffn_bexp': _L1_ffn_in['bexp'], 'L2_xattn_w_sim': _L2_xattn_in['w_sim'], 'L2_xattn_b_sim': _L2_xattn_in['b_sim'], 'L2_xattn_W_qv': _L2_xattn_in['W_qv'], 'L2_xattn_b_qv': _L2_xattn_in['b_qv'], 'L2_attn_W_Q': _L2_attn_in['W_Q'], 'L2_attn_W_K': _L2_attn_in['W_K'], 'L2_attn_W_V': _L2_attn_in['W_V'], 'L2_ffn_W_exp': _L2_ffn_in['W_exp'], 'L2_ffn_b_exp': _L2_ffn_in['b_exp'], 'L2_ffn_up_weights': _L2_ffn_in['up_weights'], 'L2_ffn_up_bias': _L2_ffn_in['up_bias'], 'L2_ffn_down_weights': _L2_ffn_in['down_weights'], 'L2_ffn_W_con': _L2_ffn_in['W_con'], 'L2_ffn_b_con': _L2_ffn_in['b_con'], 'L2_ffn_down_bias': _L2_ffn_in['down_bias'], 'L3_xattn_Wq': _L3_xattn_in['Wq'], 'L3_xattn_bq': _L3_xattn_in['bq'], 'L3_xattn_Wk': _L3_xattn_in['Wk'], 'L3_xattn_bk': _L3_xattn_in['bk'], 'L3_xattn_Wv': _L3_xattn_in['Wv'], 'L3_xattn_bv': _L3_xattn_in['bv'], 'L3_xattn_beta_risk': _L3_xattn_in['beta_risk'], 'L3_xattn_beta_prio': _L3_xattn_in['beta_prio'], 'L3_xattn_beta_impl': _L3_xattn_in['beta_impl'], 'L3_attn_q_w': _L3_attn_in['q_w'], 'L3_attn_q_b': _L3_attn_in['q_b'], 'L3_attn_k_w': _L3_attn_in['k_w'], 'L3_attn_k_b': _L3_attn_in['k_b'], 'L3_attn_v_w': _L3_attn_in['v_w'], 'L3_attn_v_b': _L3_attn_in['v_b'], 'L3_attn_l_w': _L3_attn_in['l_w'], 'L3_attn_l_b': _L3_attn_in['l_b'], 'L3_ffn_Wr': _L3_ffn_in['Wr'], 'L3_ffn_Wg': _L3_ffn_in['Wg'], 'L3_ffn_Wu': _L3_ffn_in['Wu'], 'L3_ffn_Wd': _L3_ffn_in['Wd'], 'L3_ffn_Sg': _L3_ffn_in['Sg'], 'L3_ffn_Su': _L3_ffn_in['Su'], 'L3_ffn_Sd': _L3_ffn_in['Sd']}

def reference(x, ctx_1024, fside_BxSxS2_0, mask_Bx1xS2x1_bk0, L0_xattn_q1W, L0_xattn_w1W, L0_xattn_o1W, L0_xattn_q2W, L0_xattn_w2W, L0_xattn_o2W, L0_xattn_ffW1, L0_xattn_ffb1, L0_xattn_ffW2, L0_xattn_ffb2, L0_xattn_g1, L0_xattn_b1, L0_xattn_g2, L0_xattn_b2, L0_xattn_g3, L0_xattn_b3, L0_attn_W_qkv, L0_attn_b_qkv, L0_attn_W_out, L0_attn_b_out, L0_ffn_gate_w, L0_ffn_gate_b, L0_ffn_w1, L0_ffn_b1, L0_ffn_w2, L0_ffn_b2, L1_xattn_w_q, L1_xattn_w_kv, L1_xattn_w_proj, L1_xattn_w_rel, L1_attn_Wq, L1_attn_Wv, L1_attn_q_norm_w, L1_attn_v_norm_w, L1_ffn_Wq, L1_ffn_bq, L1_ffn_Wk, L1_ffn_bk, L1_ffn_Wv, L1_ffn_bv, L1_ffn_Wo, L1_ffn_bo, L1_ffn_g1, L1_ffn_be1, L1_ffn_g2, L1_ffn_be2, L1_ffn_Wg, L1_ffn_bg, L1_ffn_We, L1_ffn_bexp, L2_xattn_w_sim, L2_xattn_b_sim, L2_xattn_W_qv, L2_xattn_b_qv, L2_attn_W_Q, L2_attn_W_K, L2_attn_W_V, L2_ffn_W_exp, L2_ffn_b_exp, L2_ffn_up_weights, L2_ffn_up_bias, L2_ffn_down_weights, L2_ffn_W_con, L2_ffn_b_con, L2_ffn_down_bias, L3_xattn_Wq, L3_xattn_bq, L3_xattn_Wk, L3_xattn_bk, L3_xattn_Wv, L3_xattn_bv, L3_xattn_beta_risk, L3_xattn_beta_prio, L3_xattn_beta_impl, L3_attn_q_w, L3_attn_q_b, L3_attn_k_w, L3_attn_k_b, L3_attn_v_w, L3_attn_v_b, L3_attn_l_w, L3_attn_l_b, L3_ffn_Wr, L3_ffn_Wg, L3_ffn_Wu, L3_ffn_Wd, L3_ffn_Sg, L3_ffn_Su, L3_ffn_Sd):
    import jax
    import jax.numpy as jnp

    def _L0_xattn_ref(x, enc_output, mask, q1W, w1W, o1W, q2W, w2W, o2W, ffW1, ffb1, ffW2, ffb2, g1, b1, g2, b2, g3, b3):
        import jax, jax.numpy as jnp
        import numpy as np
        import math
        D_MODEL = 256
        N_HEADS = 16
        HEAD_DIM = D_MODEL // N_HEADS
        MLP_DIM = 4 * D_MODEL
        B, L, M = (2, 512, 512)

        def layer_norm(x, g, b, eps=1e-05):
            mu = jnp.mean(x, axis=-1, keepdims=True)
            var = jnp.var(x, axis=-1, keepdims=True)
            return (x - mu) * jax.lax.rsqrt(var + eps) * g + b

        def mha(q_in, k_in, qW, wW, oW, mask=None):
            b, l, _ = q_in.shape
            m = k_in.shape[1]
            q = (q_in @ qW).reshape(b, l, HEAD_DIM, N_HEADS)
            k = (k_in @ wW).reshape(b, m, HEAD_DIM, N_HEADS)
            s = jnp.einsum('bldn,bmdn->blmn', q, k)
            if mask is not None:
                s = jnp.where(mask, -1000000000.0, s)
            s = s / math.sqrt(HEAD_DIM)
            w = jax.nn.softmax(s, axis=2)
            x = jnp.einsum('blmn,bmdn->bldn', w, k)
            x = x.reshape(b, l, HEAD_DIM * N_HEADS)
            return x @ oW
        sa = mha(x, x, q1W, w1W, o1W, mask=None)
        x = layer_norm(x + sa, g1, b1)
        ca = mha(x, enc_output, q2W, w2W, o2W, mask=mask)
        x = layer_norm(x + ca, g2, b2)
        h = jax.nn.gelu(x @ ffW1 + ffb1, approximate=False)
        ff = h @ ffW2 + ffb2
        x = layer_norm(x + ff, g3, b3)
        return x

    def _L0_attn_ref(inputs, W_qkv, b_qkv, W_out, b_out):
        import jax, jax.numpy as jnp
        import numpy as np
        B, S, E = (4, 512, 256)
        HIDDEN = 256
        HEADS = 16
        Bv, Sv, Ev = inputs.shape
        x = inputs @ W_qkv + b_qkv
        x = x.reshape(Bv, HEADS, Sv, -1)
        q, k, v = jnp.split(x, 3, axis=-1)
        scale = (2 * HIDDEN) ** (-0.5)
        qk = jnp.einsum('bhse,bhte->bhst', q, k) * scale
        mask = jnp.triu(jnp.full((Sv, Sv), -jnp.inf, dtype=qk.dtype), k=1)
        attn = jax.nn.softmax(qk + mask, axis=-1)
        sa = jnp.einsum('bhst,bhte->bhse', attn, v).reshape(Bv, Sv, -1)
        return sa @ W_out + b_out

    def _L0_ffn_ref(x, gate_w, gate_b, w1, b1, w2, b2):
        import jax, jax.numpy as jnp
        import numpy as np
        B, T, C = (4, 512, 256)
        E, H, K = (8, 512, 2)
        b, t, c = x.shape
        xf = x.reshape(b * t, c)
        logits = xf @ gate_w + gate_b
        probs = jax.nn.softmax(logits, axis=-1)
        gates, expert_idx = jax.lax.top_k(probs, K)
        h = jax.nn.relu(jnp.einsum('nc,ech->neh', xf, w1) + b1)
        expert_out = jnp.einsum('neh,ehc->nec', h, w2) + b2
        onehot = jax.nn.one_hot(expert_idx, E, dtype=xf.dtype)
        weights = jnp.einsum('nk,nke->ne', gates, onehot)
        out = jnp.einsum('ne,nec->nc', weights, expert_out)
        return out.reshape(b, t, c)

    def _L1_xattn_ref(x_q, x_kv, w_q, w_kv, w_proj, w_rel):
        import jax, jax.numpy as jnp
        import numpy as np
        EMBED_DIM = 256
        NUM_HEADS = 16
        HEAD_DIM = EMBED_DIM // NUM_HEADS
        SCALE = HEAD_DIM ** (-0.5)
        B, Tq, _ = x_q.shape
        Tk = x_kv.shape[1]
        q = x_q @ w_q
        kv = x_kv @ w_kv
        k, v = jnp.split(kv, 2, axis=-1)

        def heads(y, T):
            return y.reshape(B, T, NUM_HEADS, HEAD_DIM).transpose(0, 2, 1, 3)
        q = heads(q, Tq)
        k = heads(k, Tk)
        v = heads(v, Tk)
        logits = jnp.einsum('bhqd,bhkd->bhqk', q, k) * SCALE
        rel = jnp.arange(Tq, dtype=jnp.float32)[:, None] - jnp.arange(Tk, dtype=jnp.float32)[None, :]
        bias = rel[..., None] * w_rel[0]
        bias = bias.transpose(2, 0, 1)[None]
        logits = logits + bias
        attn = jax.nn.softmax(logits, axis=-1)
        out = jnp.einsum('bhqk,bhkd->bhqd', attn, v)
        out = out.transpose(0, 2, 1, 3).reshape(B, Tq, EMBED_DIM)
        return out @ w_proj

    def _L1_attn_ref(X, Wq, Wv, q_norm_w, v_norm_w):
        import jax, jax.numpy as jnp
        import numpy as np
        EPS = 1e-08

        def rms_norm_multihead(x, weight):
            x32 = x.astype(jnp.float32)
            normed = x32 * jax.lax.rsqrt(jnp.mean(x32 * x32, axis=-1, keepdims=True) + EPS)
            return normed.astype(x.dtype) * weight
        B, L, D = X.shape
        H, d = q_norm_w.shape
        K = X.reshape(B, L, H, d)
        Q = rms_norm_multihead((X @ Wq.T).reshape(B, L, H, d), q_norm_w)
        V = rms_norm_multihead((X @ Wv.T).reshape(B, L, H, d), v_norm_w)
        W = jnp.cumsum(jnp.einsum('blhd,blhe->blhde', K, V), axis=1)
        out = jnp.einsum('blhd,blhde->blhe', Q, W).reshape(B, L, D)
        return out

    def _L1_ffn_ref(x, Wq, bq, Wk, bk, Wv, bv, Wo, bo, g1, be1, g2, be2, Wg, bg, We, bexp):
        import jax, jax.numpy as jnp
        import numpy as np
        H = 16
        EPS = 1e-05

        def layernorm(x, g, b):
            m = jnp.mean(x, axis=-1, keepdims=True)
            v = jnp.mean((x - m) ** 2, axis=-1, keepdims=True)
            return (x - m) * jax.lax.rsqrt(v + EPS) * g + b
        B, S, D = x.shape
        Dh = D // H
        TOP_K = 2
        q = (x @ Wq + bq).reshape(B, S, H, Dh)
        k = (x @ Wk + bk).reshape(B, S, H, Dh)
        v = (x @ Wv + bv).reshape(B, S, H, Dh)
        scores = jnp.einsum('bqhd,bkhd->bhqk', q, k) / jnp.sqrt(jnp.float32(Dh))
        attn = jax.nn.softmax(scores, axis=-1)
        ctx = jnp.einsum('bhqk,bkhd->bqhd', attn, v).reshape(B, S, D)
        attn_out = ctx @ Wo + bo
        x = x + layernorm(attn_out, g1, be1)
        gate_probs = jax.nn.softmax(x @ Wg + bg, axis=-1)
        top_vals, top_idx = jax.lax.top_k(gate_probs, TOP_K)
        all_out = jnp.einsum('bsd,edf->bsef', x, We) + bexp
        picked = jnp.take_along_axis(all_out, top_idx[..., None], axis=2)
        moe_out = jnp.sum(top_vals[..., None] * picked, axis=2)
        return x + layernorm(moe_out, g2, be2)

    def _L2_xattn_ref(encoder_hc, decoder_hq, w_sim, b_sim, W_qv, b_qv):
        import jax, jax.numpy as jnp
        import numpy as np
        B, L_ENC, L_DEC, D = (16, 128, 128, 256)
        d = encoder_hc.shape[-1]
        w1, w2, w3 = (w_sim[:d], w_sim[d:2 * d], w_sim[2 * d:])
        Sim = (encoder_hc @ w1)[:, :, None] + (decoder_hq @ w2)[:, None, :] + jnp.einsum('bid,bjd->bij', encoder_hc * w3, decoder_hq) + b_sim[0]
        A = jax.nn.softmax(Sim, axis=2)
        hq_hat = jnp.einsum('bij,bjd->bid', A, decoder_hq)
        Batt = jax.nn.softmax(jnp.max(Sim, axis=2), axis=1)
        hc_bar = jnp.einsum('bi,bid->bd', Batt, encoder_hc)[:, None, :]
        hc_hat = jnp.broadcast_to(hc_bar, encoder_hc.shape)
        feats = jnp.concatenate([encoder_hc, hq_hat, encoder_hc * hq_hat, encoder_hc * hc_hat], axis=-1)
        hcq = feats @ W_qv + b_qv
        return hcq

    def _L2_attn_ref(embeddings, W_Q, W_K, W_V):
        import jax, jax.numpy as jnp
        import numpy as np
        B, S, D = (4, 512, 256)

        def _xavier(key, shape):
            bound = float(np.sqrt(6.0 / (shape[0] + shape[1])))
            return jax.random.uniform(key, shape, dtype=jnp.float32, minval=-bound, maxval=bound)
        _, seq_len, d = embeddings.shape
        Q = embeddings @ W_Q
        K = embeddings @ W_K
        V = embeddings @ W_V
        scale = 1.0 / jnp.sqrt(jnp.float32(d))
        scores = jnp.einsum('bqd,bkd->bqk', Q, K) * scale
        causal = jnp.tril(jnp.ones((seq_len, seq_len), dtype=bool))
        scores = jnp.where(causal[None, :, :], scores, -jnp.inf)
        probs = jax.nn.softmax(scores, axis=-1)
        return jnp.einsum('bqk,bkd->bqd', probs, V)

    def _L2_ffn_ref(x, W_exp, b_exp, up_weights, up_bias, down_weights, W_con, b_con, down_bias):
        import jax, jax.numpy as jnp
        import numpy as np
        D_MODEL = 256
        EXPANSION = 4
        D_HIDDEN = D_MODEL * EXPANSION
        NUM_STAGES = int(np.log2(D_HIDDEN))

        def butterfly(y, weights, dim):
            lead = y.shape[:-1]
            for stage in range(weights.shape[0]):
                s = 2 ** stage
                nb = dim // (2 * s)
                yr = y.reshape(*lead, nb, 2, s)
                a = yr[..., 0, :]
                b = yr[..., 1, :]
                w = weights[stage].reshape(nb, s, 2, 2)
                na = w[..., 0, 0] * a + w[..., 0, 1] * b
                nb2 = w[..., 1, 0] * a + w[..., 1, 1] * b
                y = jnp.stack([na, nb2], axis=-2).reshape(*lead, dim)
            return y
        h = jnp.einsum('bsd,dh->bsh', x, W_exp) + b_exp
        h = butterfly(h, up_weights, D_HIDDEN)
        h = jax.nn.gelu(h + up_bias, approximate=False)
        h = butterfly(h, down_weights, D_HIDDEN)
        y = jnp.einsum('bsh,hd->bsd', h, W_con) + b_con
        return y + down_bias

    def _L3_xattn_ref(q_in, k_in, v_in, phi_risk, phi_prio, phi_impl, Wq, bq, Wk, bk, Wv, bv, beta_risk, beta_prio, beta_impl):
        import jax, jax.numpy as jnp
        import numpy as np
        D = 256
        d = q_in.shape[-1]
        scale = jnp.asarray(d, q_in.dtype) ** (-0.5)
        Q = q_in @ Wq.T + bq
        K = k_in @ Wk.T + bk
        V = v_in @ Wv.T + bv
        att = jnp.einsum('bsd,btd->bst', Q, K) * scale
        att = att + beta_risk * phi_risk + beta_prio * phi_prio - beta_impl * phi_impl
        w = jax.nn.softmax(att, axis=-1)
        return jnp.einsum('bst,btd->bsd', w, V)

    def _L3_attn_ref(x, q_w, q_b, k_w, k_b, v_w, v_b, l_w, l_b):
        import jax, jax.numpy as jnp
        import numpy as np
        B, S, D = (2, 512, 256)
        H, P = (16, 64)
        NUM_OUT = 256
        q = jnp.einsum('bsd,hpd->bhsp', x, q_w) + q_b
        k = jnp.einsum('bsd,hpd->bhsp', x, k_w) + k_b
        v = jnp.einsum('bsd,hpd->bhsp', x, v_w) + v_b
        scores = jnp.einsum('bhqp,bhkp->bhqk', q, k) / jnp.sqrt(jnp.float32(P))
        attn = jax.nn.softmax(scores, axis=2)
        ctx = jnp.einsum('bhqk,bhkp->bqhp', attn, v)
        concat = ctx.reshape(ctx.shape[0], ctx.shape[1], H * P)
        out = concat @ l_w.T + l_b
        return out

    def _L3_ffn_ref(x, Wr, Wg, Wu, Wd, Sg, Su, Sd):
        import jax, jax.numpy as jnp
        import numpy as np
        B, S, D = (2, 512, 256)
        E, K, F = (16, 2, 128)
        FS = 256
        b, s, d = x.shape
        T = b * s
        xf = x.reshape(T, d)
        shared = jax.nn.silu(xf @ Sg) * (xf @ Su) @ Sd
        probs = jax.nn.softmax(xf @ Wr, axis=-1)
        topk_p, topk_i = jax.lax.top_k(probs, K)
        n_exp = Wr.shape[1]
        cw = jnp.zeros((T, n_exp), x.dtype).at[jnp.arange(T)[:, None], topk_i].add(topk_p)

        def step(acc, ew):
            wg, wu, wd, c = ew
            y = jax.nn.silu(xf @ wg) * (xf @ wu) @ wd
            return (acc + y * c[:, None], None)
        routed, _ = jax.lax.scan(step, jnp.zeros_like(xf), (Wg, Wu, Wd, cw.T))
        return (routed + shared).reshape(b, s, d)
    x = x + _L0_xattn_ref(_layernorm(x, axis=-1), ctx_1024, mask_Bx1xS2x1_bk0, L0_xattn_q1W, L0_xattn_w1W, L0_xattn_o1W, L0_xattn_q2W, L0_xattn_w2W, L0_xattn_o2W, L0_xattn_ffW1, L0_xattn_ffb1, L0_xattn_ffW2, L0_xattn_ffb2, L0_xattn_g1, L0_xattn_b1, L0_xattn_g2, L0_xattn_b2, L0_xattn_g3, L0_xattn_b3)
    x = x + _L0_attn_ref(_layernorm(x, axis=-1), L0_attn_W_qkv, L0_attn_b_qkv, L0_attn_W_out, L0_attn_b_out)
    x = x + _L0_ffn_ref(_layernorm(x, axis=-1), L0_ffn_gate_w, L0_ffn_gate_b, L0_ffn_w1, L0_ffn_b1, L0_ffn_w2, L0_ffn_b2)
    x = x + _L1_xattn_ref(_layernorm(x, axis=-1), ctx_1024, L1_xattn_w_q, L1_xattn_w_kv, L1_xattn_w_proj, L1_xattn_w_rel)
    x = x + _L1_attn_ref(_layernorm(x, axis=-1), L1_attn_Wq, L1_attn_Wv, L1_attn_q_norm_w, L1_attn_v_norm_w)
    x = x + _L1_ffn_ref(_layernorm(x, axis=-1), L1_ffn_Wq, L1_ffn_bq, L1_ffn_Wk, L1_ffn_bk, L1_ffn_Wv, L1_ffn_bv, L1_ffn_Wo, L1_ffn_bo, L1_ffn_g1, L1_ffn_be1, L1_ffn_g2, L1_ffn_be2, L1_ffn_Wg, L1_ffn_bg, L1_ffn_We, L1_ffn_bexp)
    x = x + _L2_xattn_ref(_layernorm(x, axis=-1), ctx_1024, L2_xattn_w_sim, L2_xattn_b_sim, L2_xattn_W_qv, L2_xattn_b_qv)
    x = x + _L2_attn_ref(_layernorm(x, axis=-1), L2_attn_W_Q, L2_attn_W_K, L2_attn_W_V)
    x = x + _L2_ffn_ref(_layernorm(x, axis=-1), L2_ffn_W_exp, L2_ffn_b_exp, L2_ffn_up_weights, L2_ffn_up_bias, L2_ffn_down_weights, L2_ffn_W_con, L2_ffn_b_con, L2_ffn_down_bias)
    x = x + _L3_xattn_ref(_layernorm(x, axis=-1), ctx_1024, ctx_1024, fside_BxSxS2_0, fside_BxSxS2_0, fside_BxSxS2_0, L3_xattn_Wq, L3_xattn_bq, L3_xattn_Wk, L3_xattn_bk, L3_xattn_Wv, L3_xattn_bv, L3_xattn_beta_risk, L3_xattn_beta_prio, L3_xattn_beta_impl)
    x = x + _L3_attn_ref(_layernorm(x, axis=-1), L3_attn_q_w, L3_attn_q_b, L3_attn_k_w, L3_attn_k_b, L3_attn_v_w, L3_attn_v_b, L3_attn_l_w, L3_attn_l_b)
    x = x + _L3_ffn_ref(_layernorm(x, axis=-1), L3_ffn_Wr, L3_ffn_Wg, L3_ffn_Wu, L3_ffn_Wd, L3_ffn_Sg, L3_ffn_Su, L3_ffn_Sd)
    return x

_drawn_inputs = setup_inputs


def setup_inputs(seed=0):
    import zlib

    import numpy as np

    out = dict(_drawn_inputs(seed))
    spreads = {'L0_xattn_ffb1': (0.0, 0.1),
     'L0_xattn_ffb2': (0.0, 0.1),
     'L0_xattn_g1': (1.0, 0.2),
     'L0_xattn_b1': (0.0, 0.1),
     'L0_xattn_g2': (1.0, 0.2),
     'L0_xattn_b2': (0.0, 0.1),
     'L0_xattn_g3': (1.0, 0.2),
     'L0_xattn_b3': (0.0, 0.1),
     'L0_attn_b_qkv': (0.0, 0.348),
     'L0_attn_b_out': (0.0, 0.1),
     'L0_ffn_gate_b': (0.0, 0.321),
     'L1_attn_q_norm_w': (1.0, 0.2),
     'L1_attn_v_norm_w': (1.0, 0.2),
     'L1_ffn_bq': (0.0, 0.8),
     'L1_ffn_bk': (0.0, 2.0),
     'L1_ffn_bv': (0.0, 0.4),
     'L1_ffn_bo': (0.0, 0.1),
     'L1_ffn_g1': (1.0, 0.6),
     'L1_ffn_be1': (0.0, 0.679),
     'L1_ffn_g2': (1.0, 0.6),
     'L1_ffn_be2': (0.0, 0.8),
     'L1_ffn_bg': (0.0, 0.372),
     'L1_ffn_bexp': (0.0, 0.8),
     'L2_ffn_b_exp': (0.0, 0.1),
     'L2_ffn_up_bias': (0.0, 0.1),
     'L2_ffn_b_con': (0.0, 0.8),
     'L2_ffn_down_bias': (0.0, 0.8)}
    factors = {'fside_BxSxS2_0': 22.268,
     'L0_ffn_b1': 8.0,
     'L0_ffn_b2': 6.207,
     'L1_ffn_Wq': 8.0,
     'L1_ffn_Wk': 8.0,
     'L2_xattn_w_sim': 8.0,
     'L2_xattn_W_qv': 3.122,
     'L2_xattn_b_qv': 8.0,
     'L2_attn_W_Q': 5.137,
     'L2_attn_W_K': 5.218,
     'L3_xattn_Wq': 6.693,
     'L3_xattn_bq': 29.282,
     'L3_xattn_Wk': 6.733,
     'L3_xattn_bk': 200.0,
     'L3_xattn_bv': 22.413,
     'L3_attn_q_w': 6.566,
     'L3_attn_q_b': 200.0,
     'L3_attn_k_w': 6.614,
     'L3_attn_k_b': 8.0,
     'L3_attn_v_b': 8.0,
     'L3_attn_l_b': 8.0,
     'L3_ffn_Wr': 7.937,
     'L3_ffn_Wg': 8.0,
     'L3_ffn_Wu': 7.542,
     'L3_ffn_Wd': 7.537,
     'L3_ffn_Sg': 8.0,
     'L3_ffn_Su': 8.0,
     'L3_ffn_Sd': 8.0}
    for name, (base, spread) in spreads.items():
        noise = np.random.default_rng([zlib.crc32(name.encode()), seed]).standard_normal(out[name].shape)
        drawn = base * np.exp(spread * noise) if base else spread * noise
        out[name] = jnp.asarray(drawn.astype(out[name].dtype))
    for name, factor in factors.items():
        out[name] = (out[name] * factor).astype(out[name].dtype)
    return out
```

```python
import concourse.bass as bass
from concourse import mybir
from contextlib import ExitStack, contextmanager

P = 128
D = 256
KC = D // P
B = 64
S = 32
N = B * S
M = 257
BLK = 512
NB = N // BLK
GT = 128
NG = N // GT
KCH = [(0, 128), (128, 128), (256, 1)]
HALF = BLK // 2

START = 1

F32 = mybir.dt.float32
U32 = mybir.dt.uint32
U8 = mybir.dt.uint8
ALU = mybir.AluOpType
ACT = mybir.ActivationFunctionType
AX = mybir.AxisListType.X


CONSTS = ["ident", "mask_block", "mask_causal", "mask_lower", "mask_segments", "head_of_8", "head_of_2",
          "own_head", "query_sel", "same_head",
          "iota16", "ones", "positions"]




class Core:

    BANK = 20

    def __init__(self, nc, ctx, dram):
        self.nc, self.ctx, self.dram = nc, ctx, dram
        self.banks = [[ctx.enter_context(nc.semaphore(f"bank{b}_{i}")) for i in range(self.BANK)]
                      for b in range(2)]
        self.turn = 0
        self.used = [self.BANK, self.BANK]
        with nc.Block(no_gpsimd_drain=True) as block:
            @block.gpsimd
            def _(pool):
                for s in self.banks[0]:
                    pool.sem_inc(s, START)
        self.banks8 = ctx.enter_context(nc.psum_tensor("banks8", [P, 8, BLK], F32))
        self.psum = [self.banks8[:, i, :] for i in range(8)]
        self.x = self.keep("x_T", [P, KC, N])
        self.consts = {name: self.keep(name, list(dram[name].shape)) for name in CONSTS}
        self.ident = self.consts["ident"]
        self.mean_w = self.keep("mean_w", [P, P])
        self.eps = self.keep("eps", [P, 2])

    def keep(self, name, shape, dt=F32):
        return self.ctx.enter_context(self.nc.sbuf_tensor(f"sb_{name}", shape, dt))


@contextmanager
def phase(core, *names):
    nc = core.nc
    assert len(names) <= core.BANK
    bank, old = core.banks[core.turn % 2], core.banks[(core.turn + 1) % 2]
    stale = old if core.turn == 0 else old[:core.used[(core.turn + 1) % 2]]
    core.used[core.turn % 2] = max(len(names), 1)
    with nc.Block(no_gpsimd_drain=True) as block:
        @block.gpsimd
        def _(pool):
            for s in stale:
                if core.turn:
                    pool.sem_clear(s)
                pool.sem_inc(s, START)
        yield (block, *bank[:len(names)])
    core.turn += 1


def bcast(ap, n, at=1):
    a = ap.unsqueeze(at)
    shape = list(a.shape)
    shape[at] = n
    return a.broadcast_to(shape)


def blk(t, width=BLK):
    return bass.ds(t * width, width)


def layer_norm(core, src, dst, scale_shift=None, add=None):
    nc = core.nc
    var_bank = core.psum[2]
    with ExitStack() as mem:
        def sb(name, shape):
            return mem.enter_context(nc.sbuf_tensor(f"{name}_{core.turn}", shape, F32))
        cen, sq, diag = sb("cen", [P, KC, N]), sb("sq", [P, 2, KC, BLK]), sb("diag", [P, 2, 4, P])
        std, rstd = sb("std", [P, NG]), sb("rstd", [P, NG])
        (block, mean_ready, centred, squared, var_ready, std_ready, rstd_ready, diag_ready, spread, scaled,
         done) = mem.enter_context(
            phase(core, "mean_ready", "centred", "squared", "var_ready", "std_ready", "rstd_ready",
                  "diag_ready", "spread", "scaled", "done"))

        @block.tensor
        def _(pe):
            def variance(t):
                pe.wait_ge(squared, START + t + 1)
                for g in range(4):
                    for k in range(KC):
                        ins = pe.matmul(var_bank[:, 4 * t + g:4 * t + g + 1], sq[:, t % 2, k, g * P:(g + 1) * P],
                                        core.mean_w[:, 0:1], start=(k == 0), stop=(k == KC - 1))
                ins.then_inc(var_ready, 1)

            for t in range(NB):
                if t >= 2:
                    pe.wait_ge(centred, START + t - 1)
                for k in range(KC):
                    ins = pe.matmul(core.psum[t % 2], core.mean_w[:, :], src[:, k, blk(t)], start=(k == 0),
                                    stop=(k == KC - 1))
                ins.then_inc(mean_ready, 1)
                if t >= 1:
                    variance(t - 1)
            variance(NB - 1)
            for t in range(NB):
                pe.wait_ge(diag_ready, START + t + 1)
                pe.matmul(core.psum[4 + t], core.consts["ones"][:, :],
                          diag[:, t % 2, :, :].rearrange("p g w -> p (g w)"), start=True, stop=True)\
                  .then_inc(spread, 1)

        @block.scalar
        def _(act):
            for t in range(NB):
                act.wait_ge(centred, START + t + 1)
                if t >= 2:
                    act.wait_ge(var_ready, START + t - 1)
                nc.scalar.activation(sq[:, t % 2, :, :], cen[:, :, blk(t)], ACT.Square).then_inc(squared, 1)
            act.wait_ge(var_ready, START + NB)
            nc.scalar.activation(std[:, :], var_bank[:, 0:NG], ACT.Sqrt, bias=core.eps[:, 0:1])\
              .then_inc(std_ready, 1)
            if scale_shift is not None and add is None:
                for t in range(NB):
                    for k in range(KC):
                        act.wait_ge(scaled, START + t * KC + k + 1)
                        nc.scalar.activation(dst[:, k, blk(t)], cen[:, k, blk(t)], ACT.Identity,
                                             bias=scale_shift[1][:, k:k + 1]).then_inc(done, 1)

        @block.gpsimd
        def _(pool):
            pool.wait_ge(rstd_ready, START + 1)
            for t in range(NB):
                if t >= 2:
                    pool.wait_ge(spread, START + t - 1)
                nc.gpsimd.tensor_tensor(diag[:, t % 2, :, :], bcast(core.ident[:, :], 4),
                                        bcast(rstd[:, 4 * t:4 * t + 4], P, 2), ALU.mult).then_inc(diag_ready, 1)

        @block.vector
        def _(dve):
            for t in range(NB):
                dve.wait_ge(mean_ready, START + t + 1)
                nc.vector.tensor_tensor(cen[:, :, blk(t)], src[:, :, blk(t)], bcast(core.psum[t % 2], KC),
                                        ALU.subtract).then_inc(centred, 1)
            dve.wait_ge(std_ready, START + 1)
            nc.vector.reciprocal(rstd[:, :], std[:, :]).then_inc(rstd_ready, 1)
            dve.wait_ge(centred, START + NB)
            for t in range(NB):
                dve.wait_ge(spread, START + t + 1)
                if scale_shift is None:
                    out = dst if add is None else cen
                    nc.vector.tensor_tensor(out[:, :, blk(t)], cen[:, :, blk(t)], bcast(core.psum[4 + t], KC),
                                            ALU.mult).then_inc(scaled, 1)
                    continue
                g, b = scale_shift
                for k in range(KC):
                    nc.vector.scalar_tensor_tensor(out=cen[:, k, blk(t)], in0=core.psum[4 + t],
                                                   scalar=g[:, k:k + 1], in1=cen[:, k, blk(t)], op0=ALU.mult,
                                                   op1=ALU.mult).then_inc(scaled, 1)
                    if add is not None:
                        dve.wait_ge(scaled, START + t * KC + k + 1)
                        nc.vector.scalar_tensor_tensor(out=dst[:, k, blk(t)], in0=cen[:, k, blk(t)],
                                                       scalar=b[:, k:k + 1], in1=add[:, k, blk(t)], op0=ALU.add,
                                                       op1=ALU.add).then_inc(done, 1)


def linear(core, w, src, dst, bias=None, kind="copy", kc=KC, mc=KC):
    nc = core.nc
    takers = {"copy": 2, "gelu": 1, "residual": 1}[kind]
    unroll = 2 if mc <= 4 else 1
    per = unroll * mc // takers
    with phase(core, "product_ready", "free_act", "free_dve") as (block, ready, free_act, free_dve):
        @block.tensor
        def _(pe):
            with pe.Fori(0, NB // unroll) as r:
                for n in range(unroll * mc):
                    u, m = n // mc, n % mc
                    free = free_act if kind == "gelu" or (takers == 2 and n % 2 == 0) else free_dve
                    pe.wait_ge(free, START + r * per + n // takers + 1)
                    for k in range(kc):
                        ins = pe.matmul(core.psum[n][:, :], w[:, k, m * P:(m + 1) * P],
                                        src[:, k, blk(r * unroll + u)], start=(k == 0), stop=(k == kc - 1))
                    ins.then_inc(ready, 1)

        def take(eng, which, free):
            eng.sem_inc(free, per)
            with eng.Fori(0, NB // unroll) as r:
                for n in range(unroll * mc):
                    u, m = n // mc, n % mc
                    if takers == 2 and n % 2 != which:
                        continue
                    eng.wait_ge(ready, START + r * unroll * mc + n + 1)
                    out, got = dst[:, m, blk(r * unroll + u)], core.psum[n][:, :]
                    b = 0.0 if bias is None else bias[:, m:m + 1]
                    if which == 0:
                        f = ACT.Gelu if kind == "gelu" else ACT.Identity
                        ins = nc.scalar.activation(out, got, f, bias=b)
                    elif kind == "residual":
                        ins = nc.vector.scalar_tensor_tensor(out=out, in0=got, scalar=b, in1=out,
                                                             op0=ALU.add, op1=ALU.add)
                    else:
                        ins = nc.vector.tensor_scalar(out, got, b, None, ALU.add)
                    ins.then_inc(free, 1)

        if kind != "residual":
            @block.scalar
            def _(act):
                take(act, 0, free_act)
        if kind != "gelu":
            @block.vector
            def _(dve):
                take(dve, 1, free_dve)


def start(core):
    nc = core.nc
    with phase(core, "loaded", "set") as (block, loaded, done):
        @block.sync
        def _(sp):
            sp.dma_start(core.x[:, :, :], core.dram["x"].rearrange("(k p) n -> p k n", p=P)).then_inc(loaded, 16)
            for i, (name, tile) in enumerate(core.consts.items()):
                sp.dma_start(tile[:, :], core.dram[name]).then_inc(loaded, 16)
            sp.wait_ge(loaded, START + 16 * (1 + len(core.consts)))

        @block.gpsimd
        def _(pool):
            nc.gpsimd.memset(core.mean_w[:, :], 1.0 / D).then_inc(done, 1)
            nc.gpsimd.memset(core.eps[:, 0:1], 1e-5).then_inc(done, 1)
            nc.gpsimd.memset(core.eps[:, 1:2], 1e-8).then_inc(done, 1)
            pool.wait_ge(done, START + 3)


def load(core, *pairs):
    with phase(core, "loaded") as (block, loaded):
        @block.sync
        def _(sp):
            for tile, source in pairs:
                sp.dma_start(tile, source).then_inc(loaded, 16)
            sp.wait_ge(loaded, START + 16 * len(pairs))


def chunks(ap):
    return ap.rearrange("(k p) n -> p k n", p=P)


def store(core, src, out):
    with phase(core, "stored") as (block, stored):
        @block.sync
        def _(sp):
            sp.dma_start(chunks(out), src[:, :, :]).then_inc(stored, 16)
            sp.wait_ge(stored, START + 16)


def self_attention(core, kind, still, moving, v, out, chunk_n, scale=1.0, mask=None, wv=None):
    nc = core.nc
    seg, single = kind == "segments", kind == "single"
    dh = {"heads": 16, "linear": 16, "columns": 64}.get(kind, 0)
    hp = P // dh if dh else 0
    units = 16 if seg else 4 if single else chunk_n * hp
    quads = units // 4
    iters = NB if single else NG
    rows = BLK if single else GT
    softmax, turns = kind != "linear", kind != "columns"
    outs = chunk_n if dh else quads
    with ExitStack() as mem:
        def sb(name, shape):
            return mem.enter_context(nc.sbuf_tensor(f"{name}_{core.turn}", shape, F32))
        if seg:
            q_e, b_st, v_e, o_st = (sb(n, [16, 16, GT]) for n in ("q_e", "k_e", "v_e", "o_e"))
            a_st, v_st = (sb(n, [16, 16, 16, 8]) for n in ("q_rows", "v_cols"))
            v_use = sb("v_rows", [P, 16, 16])
        elif single:
            a_st, v_st = sb("a_st", [P, KC, BLK]), sb("v_st", [P, KC, BLK])
            v_use = sb("v_tok", [P, 4, D])
        else:
            a_st = sb("a_pad", [P, units, GT])
            v_st = sb("v_st", [P, chunk_n, GT])
            v_use = sb("v_pad", [P, chunk_n, hp, P + dh])
            v_flat = v_use[:, :, :, :].rearrange("p c h w -> p (c h w)")
        s = sb("s", [P, 2, 4, P])
        p = sb("p", [P, 2, 4, P])
        pt = sb("pt", [P, 2, 4, P]) if turns else p
        top, neg, total, inv = (sb(n, [P, 2, 4]) for n in ("top", "neg", "total", "inv"))
        (block, staged, v_turned, v_ready, scores_ready, masked, topped, negated, exped, inverted,
         normed, p_turned, pt_ready, out_ready, out_taken, stored, arrived, passed) = mem.enter_context(
            phase(core, "staged", "v_turned", "v_ready", "scores_ready", "masked", "topped", "negated",
                  "exped", "inverted", "normed", "p_turned", "pt_ready", "out_ready", "out_taken", "stored", "arrived",
                  "passed"))
        n_staged = 2 if seg else 2 if single else chunk_n + 1
        heads_of = core.consts["head_of_8" if dh == 16 else "head_of_2"]

        def scores_bank(n):
            return core.psum[n % 2]

        def turned_bank(n):
            return core.psum[2 + n % 2]

        v_bank = core.psum[4]

        def out_bank(o):
            return core.psum[5 + o % 2] if not single else core.psum[5 + o]

        if seg:
            q_d, k_d, v_d, o_d = still, moving, v, out

            @block.sync
            def _(sp):
                def part(d, i):
                    return d.rearrange("(s e) n -> e s n", e=16)[:, :, blk(i, GT)]

                with sp.Fori(0, iters) as i:
                    sp.wait_ge(scores_ready, START + i * quads)
                    sp.sem_inc(passed, 1)
                    sp.wait_ge(v_turned, START + i)
                    sp.sem_inc(passed, 1)
                    for tile, d in ((q_e, q_d), (b_st, k_d), (v_e, v_d)):
                        sp.dma_start(tile[:, :, :], part(d, i)).then_inc(arrived, 16)
                    sp.wait_ge(out_taken, START + (i + 1) * quads)
                    sp.sem_inc(passed, 1)
                    sp.dma_start(part(o_d, i), o_st[:, :, :]).then_inc(stored, 16)
                sp.wait_ge(stored, START + 16 * iters)

            @block.gpsimd
            def _(pool):
                with pool.Fori(0, iters) as i:
                    pool.wait_ge(arrived, START + (i + 1) * 48)
                    pool.wait_ge(v_turned, START + i)
                    pool.wait_ge(scores_ready, START + i * quads)
                    pool.sem_inc(passed, 1)
                    for rows_of, e in ((v_st, v_e), (a_st, q_e)):
                        nc.gpsimd.tensor_copy(rows_of[:, :, :, :],
                                              e[:, :, :].rearrange("e s (u t) -> e u s t", t=8)).then_inc(staged, 1)
        else:
            @block.gpsimd
            def _(pool):
                if not single:
                    nc.gpsimd.memset(v_use[:, :, :, :], 0.0).then_inc(stored, 1)
                with pool.Fori(0, iters) as i:
                    pool.wait_ge(v_turned, START + i)
                    pool.sem_inc(passed, 1)
                    nc.gpsimd.tensor_copy(v_st[:, :, :], v[:, :, blk(i, rows)]).then_inc(staged, 1)
                    pool.wait_ge(scores_ready, START + i * quads)
                    pool.sem_inc(passed, 1)
                    if single:
                        nc.gpsimd.tensor_copy(a_st[:, :, :], still[:, :, blk(i, rows)]).then_inc(staged, 1)
                    else:
                        for c in range(chunk_n):
                            nc.gpsimd.tensor_tensor(
                                a_st[:, c * hp:(c + 1) * hp, :], bcast(still[:, c, blk(i, rows)], hp),
                                bcast(heads_of[:, 0:hp], GT, 2), ALU.mult).then_inc(staged, 1)

        @block.tensor
        def _(pe):
            def values(i):
                pe.wait_ge(staged, START + i * n_staged + 1)
                pe.wait_ge(v_ready, START + i)
                if seg:
                    for u in range(units):
                        ins = pe.matmul(v_bank[:, u * 16:(u + 1) * 16],
                                        v_st[:, u, :, :].rearrange("e s t -> e (s t)"), core.ident[0:16, 0:16],
                                        start=True, stop=True)
                elif single:
                    for u in range(units):
                        vb = core.psum[4 + 3 * (u // 2)][:, (u % 2) * D:(u % 2 + 1) * D]
                        for k in range(KC):
                            ins = pe.matmul(vb, v_st[:, k, u * P:(u + 1) * P], wv[:, k, :], start=(k == 0),
                                            stop=(k == KC - 1))
                else:
                    for c in range(chunk_n):
                        ins = pe.transpose(v_bank[:, c * P:(c + 1) * P], v_st[:, c, :], core.ident[:, :])
                ins.then_inc(v_turned, 1)

            def scores(i, n):
                pe.wait_ge(staged, START + (i + 1) * n_staged)
                if n >= 2:
                    pe.wait_ge(masked, START + i * quads + n - 1)
                else:
                    pe.wait_ge(masked, START + i * quads)
                for u in range(4 * n, 4 * n + 4):
                    to = scores_bank(n)[:, (u % 4) * P:(u % 4 + 1) * P]
                    if seg:
                        ins = pe.matmul(to, a_st[:, u, :, :].rearrange("e s t -> e (s t)"), b_st[:, :, 8 * u:8 * u + 8],
                                        start=True, stop=True)
                    elif single:
                        for k in range(KC):
                            ins = pe.matmul(to, a_st[:, k, u * P:(u + 1) * P],
                                            moving[:, k, bass.ds(i * BLK + u * P, P)], start=(k == 0),
                                            stop=(k == KC - 1))
                    else:
                        ins = pe.matmul(to, a_st[:, u, :], moving[:, u // hp, blk(i, GT)], start=True,
                                        stop=True)
                ins.then_inc(scores_ready, 1)

            def turn(i, n):
                pe.wait_ge(normed, START + i * quads + n + 1)
                if n >= 2:
                    pe.wait_ge(pt_ready, START + i * quads + n - 1)
                else:
                    pe.wait_ge(pt_ready, START + i * quads)
                for u in range(4):
                    ins = pe.transpose(turned_bank(n)[:, u * P:(u + 1) * P], p[:, n % 2, u, :], core.ident[:, :])
                ins.then_inc(p_turned, 1)

            def result(i, n):
                if turns:
                    pe.wait_ge(pt_ready, START + i * quads + n + 1)
                else:
                    pe.wait_ge(normed, START + i * quads + n + 1)
                if n == 0:
                    pe.wait_ge(v_ready, START + i + 1)
                for u in range(4 * n, 4 * n + 4):
                    pu = pt[:, n % 2, u % 4, :]
                    if seg:
                        if u % 4 == 0:
                            pe.wait_ge(out_taken, START + i * quads + max(0, n - 1))
                        ins = pe.matmul(out_bank(n)[0:16, (u % 4) * P:(u % 4 + 1) * P], v_use[:, u, :], pu,
                                        start=True, stop=True)
                        if u % 4 == 3:
                            ins.then_inc(out_ready, 1)
                    elif single:
                        if u == 0:
                            pe.wait_ge(out_taken, START + i)
                        for c in range(KC):
                            ins = pe.matmul(out_bank(c)[:, u * P:(u + 1) * P], v_use[:, u, c * P:(c + 1) * P],
                                            pu, start=True, stop=True)
                        if u == 3:
                            ins.then_inc(out_ready, 1)
                    else:
                        c, h = u // hp, u % hp
                        if h == 0:
                            pe.wait_ge(out_taken, START + i * outs + max(0, c - 1))
                        at = c * hp * (P + dh) + h * P
                        ins = pe.matmul(out_bank(c)[:, 0:GT], v_flat[:, at:at + P], pu, start=(h == 0),
                                        stop=(h == hp - 1))
                        if h == hp - 1:
                            ins.then_inc(out_ready, 1)

            with pe.Fori(0, iters) as i:
                values(i)
                scores(i, 0)
                for n in range(quads):
                    if n + 1 < quads:
                        scores(i, n + 1)
                    if turns:
                        turn(i, n)
                    if n >= 1:
                        result(i, n - 1)
                result(i, quads - 1)

        @block.scalar
        def _(act):
            if not (seg or single):
                act.wait_ge(stored, START + 1)

            def exps(i, n):
                act.wait_ge(negated, START + i * quads + n + 1)
                if turns:
                    act.wait_ge(p_turned, START + i * quads + max(0, n - 1))
                else:
                    act.wait_ge(out_ready, START + i * outs + max(0, n - 1) * (4 // hp))
                for u in range(4):
                    ins = nc.scalar.activation(p[:, n % 2, u, :], s[:, n % 2, u, :], ACT.Exp,
                                               bias=neg[:, n % 2, u:u + 1], scale=scale,
                                               accum_out=total[:, n % 2, u:u + 1])
                ins.then_inc(exped, 1)

            def turned(i, n):
                act.wait_ge(p_turned, START + i * quads + n + 1)
                if seg or single:
                    act.wait_ge(out_ready, START + i * outs + max(0, n - 1))
                else:
                    act.wait_ge(out_ready, START + i * outs + max(0, n - 1) // 2)
                nc.scalar.copy(pt[:, n % 2, :, :], turned_bank(n).rearrange("p (u w) -> p u w", u=4))\
                  .then_inc(pt_ready, 1)

            with act.Fori(0, iters) as i:
                act.wait_ge(v_turned, START + i + 1)
                act.wait_ge(out_ready, START + (i * outs if not single else i))
                if seg:
                    ins = nc.scalar.copy(v_use[:, :, :], v_bank[:, 0:256].rearrange("p (u e) -> p u e", u=16))
                elif single:
                    for half in range(2):
                        ins = nc.scalar.copy(v_use[:, 2 * half:2 * half + 2, :],
                                             core.psum[4 + 3 * half].rearrange("p (u f) -> p u f", u=2))
                else:
                    for c in range(chunk_n):
                        ins = nc.scalar.copy(v_use[:, c, :, 0:dh],
                                             v_bank[:, c * P:(c + 1) * P].rearrange("p (h f) -> p h f", h=hp))
                ins.then_inc(v_ready, 1)
                for n in range(quads):
                    if softmax:
                        exps(i, n)
                    if turns and n >= 1:
                        turned(i, n - 1)
                if turns:
                    turned(i, quads - 1)

        @block.vector
        def _(dve):
            def mask_quad(i, n):
                dve.wait_ge(scores_ready, START + i * quads + n + 1)
                sc = scores_bank(n).rearrange("p (u w) -> p u w", u=4)
                if not softmax:
                    dve.wait_ge(p_turned, START + i * quads + max(0, n - 1))
                    nc.vector.tensor_tensor(p[:, n % 2, :, :], sc, bcast(mask[:, :], 4), ALU.mult)\
                      .then_inc(masked, 1)
                    dve.wait_ge(masked, START + i * quads + n + 1)
                    dve.sem_inc(normed, 1)
                    return
                dve.wait_ge(exped, START + i * quads + max(0, n - 1))
                nc.vector.tensor_tensor(s[:, n % 2, :, :], sc, bcast(mask[:, :], 4), ALU.add).then_inc(masked, 1)
                dve.wait_ge(masked, START + i * quads + n + 1)
                nc.vector.tensor_reduce(top[:, n % 2, :], s[:, n % 2, :, :], AX, ALU.max).then_inc(topped, 1)
                dve.wait_ge(topped, START + i * quads + n + 1)
                nc.vector.tensor_scalar(neg[:, n % 2, :], top[:, n % 2, :], -scale, None, ALU.mult)\
                  .then_inc(negated, 1)

            def norm(i, n):
                dve.wait_ge(exped, START + i * quads + n + 1)
                nc.vector.reciprocal(inv[:, n % 2, :], total[:, n % 2, :]).then_inc(inverted, 1)
                dve.wait_ge(inverted, START + i * quads + n + 1)
                nc.vector.tensor_tensor(p[:, n % 2, :, :], p[:, n % 2, :, :], bcast(inv[:, n % 2, :], P, 2),
                                        ALU.mult).then_inc(normed, 1)

            def take(i, o):
                if single:
                    dve.wait_ge(out_ready, START + i + 1)
                    nc.vector.tensor_copy(out[:, :, blk(i)], core.banks8[:, 5:7, :]).then_inc(out_taken, 1)
                    return
                dve.wait_ge(out_ready, START + i * outs + o + 1)
                if seg:
                    dve.wait_ge(stored, START + 16 * i)
                    nc.vector.tensor_copy(
                        o_st[:, :, 32 * o:32 * o + 32].rearrange("e s (u t) -> e u s t", u=4),
                        out_bank(o)[0:16, :].rearrange("e (u s t) -> e u s t", u=4, t=8)).then_inc(out_taken, 1)
                else:
                    nc.vector.tensor_copy(out[:, o, blk(i, GT)], out_bank(o)[:, 0:GT]).then_inc(out_taken, 1)

            with dve.Fori(0, iters) as i:
                taken = 0
                for n in range(quads + 2):
                    if n < quads:
                        mask_quad(i, n)
                    if softmax and 1 <= n <= quads:
                        norm(i, n - 1)
                    while n >= 2 and not single and (taken + 1) * (1 if seg else hp) <= (n - 1) * (1 if seg else 4):
                        take(i, taken)
                        taken += 1
                if single:
                    take(i, 0)
                else:
                    assert taken == outs


def cross_attention(core, q, wk, wv, out, ctx_t, mask=None, rel=None):
    nc = core.nc
    SC = 0.25
    LAST = B - 1
    with ExitStack() as mem:
        def sb(name, shape, dt=F32):
            return mem.enter_context(nc.sbuf_tensor(f"{name}_{core.turn}", shape, dt))
        ctx_sb = [sb(f"ctx{j}", [P, KC, M]) for j in range(2)]
        hide8 = [sb(f"hide8{j}", [P, M], U8) for j in range(2)]
        show, hidden = sb("show", [P, M]), sb("hidden", [P, M])
        q_pad = [sb(f"q_pad{j}", [P, 16, S]) for j in range(2)]
        k_t = [sb(f"k_t{j}", [P, KC, M]) for j in range(2)]
        v_tok = [sb(f"v_tok{j}", [P, 3, D]) for j in range(2)]
        s, p = sb("s", [P, 4, M]), sb("p", [P, 4, M])
        pt = sb("pt", [P, 3, 4 * P])
        om = sb("om", [P, 4, 64])
        top, neg, total, inv = (sb(n, [P, 4]) for n in ("top", "neg", "total", "inv"))
        (block, loaded, padded, kv_made, k_ready, v_ready, scores_ready, biased, topped, negated, exped,
         inverted, p_turned, pt_act, pt_dve, result_ready, owned, out_made, out_taken, loaded1,
         passed) = mem.enter_context(
            phase(core, "loaded", "padded", "kv_made", "k_ready", "v_ready", "scores_ready", "biased",
                  "topped", "negated", "exped", "inverted", "p_turned", "pt_act", "pt_dve", "result_ready",
                  "owned", "out_made", "out_taken", "loaded1", "passed"))
        arrived = [loaded, loaded1]
        loads = 32 if mask is not None else 16
        bias_steps = 4 if mask is not None else 1
        banks = core.banks8

        @block.sync
        def _(sp):
            def fetch(b, j):
                sp.dma_start(ctx_sb[j][:, :, :], ctx_t[b, :, :].rearrange("(k p) m -> p k m", p=P))\
                  .then_inc(arrived[j], 16)
                if mask is not None:
                    sp.dma_start(hide8[j][:, :], mask[b, :, :].broadcast_to([P, M])).then_inc(arrived[j], 16)

            for j in range(2):
                fetch(j, j)
            with sp.Fori(0, B // 2 - 1) as r:
                for j in range(2):
                    sp.wait_ge(kv_made, START + 2 * r + j + 1)
                    sp.sem_inc(passed, 1)
                    sp.wait_ge(biased, START + (2 * r + j + 1) * bias_steps)
                    sp.sem_inc(passed, 1)
                    fetch(2 * r + j + 2, j)

        @block.gpsimd
        def _(pool):
            with pool.Fori(0, B // 2) as r:
                for j in range(2):
                    b = 2 * r + j
                    pool.wait_ge(scores_ready, START + (b - j) * 4)
                    for c in range(KC):
                        nc.gpsimd.tensor_tensor(q_pad[j][:, c * 8:c * 8 + 8, :],
                                                bcast(q[:, c, blk(b, S)], 8),
                                                bcast(core.consts["head_of_8"][:, :], S, 2), ALU.mult)\
                          .then_inc(padded, 1)

        @block.tensor
        def _(pe):
            def keys_values(b, j, first=False):
                pe.wait_ge(arrived[j], START + (b - j) * (loads // 2) + loads)
                if not first:
                    pe.wait_ge(pt_act, START + b - 1)
                    pe.wait_ge(pt_dve, START + b - 1)
                    pe.wait_ge(out_taken, START + b - 1)
                    pe.wait_ge(v_ready, START + b)
                for m in range(KC):
                    for k in range(KC):
                        pe.matmul(banks[:, 4 + m, 0:M], wk[:, k, m * P:(m + 1) * P], ctx_sb[j][:, k, :],
                                  start=(k == 0), stop=(k == KC - 1))
                for c, (at, n) in enumerate(KCH):
                    for k in range(KC):
                        ins = pe.matmul(banks[0:n, 6 + c // 2, (c % 2) * D:(c % 2 + 1) * D],
                                        ctx_sb[j][:, k, at:at + n], wv[:, k, :], start=(k == 0),
                                        stop=(k == KC - 1))
                ins.then_inc(kv_made, 1)

            def scores(b, j):
                pe.wait_ge(padded, START + 2 * b + 2)
                pe.wait_ge(k_ready, START + b + 1)
                pe.wait_ge(biased, START + b * bias_steps)
                for n in range(4):
                    ins = pe.matmul(banks[:, n, 0:M],
                                    q_pad[j][:, 4 * n:4 * n + 4, :].rearrange("p h s -> p (h s)"),
                                    k_t[j][:, n // 2, :], start=True, stop=True)
                    ins.then_inc(scores_ready, 1)

            def turn(b, ahead):
                pe.wait_ge(exped, START + b + 1)
                pe.wait_ge(k_ready, START + b + 1 + ahead)
                pe.wait_ge(v_ready, START + b + 1 + ahead)
                for c, (at, m) in enumerate(KCH):
                    for n in range(4):
                        ins = pe.transpose(banks[0:m, (4, 5, 7)[c], n * P:(n + 1) * P], p[:, n, at:at + m],
                                           core.ident[:, :])
                ins.then_inc(p_turned, 1)

            def results(b, j):
                pe.wait_ge(pt_act, START + b + 1)
                pe.wait_ge(pt_dve, START + b + 1)
                for n in range(4):
                    for c, (at, m) in enumerate(KCH):
                        ins = pe.matmul(banks[:, 6, n * 64:(n + 1) * 64], pt[0:m, c, n * P:(n + 1) * P],
                                        v_tok[j][0:m, c, n * 64:(n + 1) * 64], start=(c == 0), stop=(c == 2))
                ins.then_inc(result_ready, 1)
                pe.wait_ge(owned, START + (b + 1) * 4)
                for c in range(KC):
                    ins = pe.matmul(banks[:, 6, 256 + c * S:256 + (c + 1) * S],
                                    om[:, 2 * c:2 * c + 2, :].rearrange("p n f -> p (n f)"),
                                    core.consts["query_sel"][:, :], start=True, stop=True)
                ins.then_inc(out_made, 1)

            keys_values(0, 0, first=True)
            scores(0, 0)

            def batch(b, j, ahead=1):
                if ahead:
                    keys_values(b + 1, 1 - j)
                turn(b, ahead)
                if ahead:
                    scores(b + 1, 1 - j)
                results(b, j)

            with pe.Fori(0, B // 2 - 1) as r:
                for j in range(2):
                    batch(2 * r + j, j)
            batch(LAST - 1, 0)
            batch(LAST, 1, 0)

        def copy_keys(b, j):
            nc.scalar.copy(k_t[j][:, :, :], banks[:, 4:6, 0:M]).then_inc(k_ready, 1)

        @block.scalar
        def _(act):
            def keys(b, j):
                act.wait_ge(kv_made, START + b + 1)
                copy_keys(b, j)

            def batch(b, j, ahead=1):
                if ahead:
                    keys(b + 1, 1 - j)
                act.wait_ge(negated, START + b + 1)
                act.wait_ge(p_turned, START + b)
                for n in range(4):
                    ins = nc.scalar.activation(p[:, n, :], s[:, n, :], ACT.Exp, bias=neg[:, n:n + 1],
                                               scale=SC if rel is None else 1.0, accum_out=total[:, n:n + 1])
                ins.then_inc(exped, 1)
                act.wait_ge(p_turned, START + b + 1)
                act.wait_ge(result_ready, START + b)
                nc.scalar.copy(pt[:, 0, :], banks[:, 4, :])
                nc.scalar.copy(pt[0:1, 2, :], banks[0:1, 7, :]).then_inc(pt_act, 1)

            keys(0, 0)
            with act.Fori(0, B // 2 - 1) as r:
                for j in range(2):
                    batch(2 * r + j, j)
            batch(LAST - 1, 0)
            batch(LAST, 1, 0)

        @block.vector
        def _(dve):
            def values(b, j):
                dve.wait_ge(kv_made, START + b + 1)
                nc.vector.tensor_copy(v_tok[j][:, 0:2, :], banks[:, 6, :].rearrange("p (c f) -> p c f", c=2))
                nc.vector.tensor_copy(v_tok[j][0:1, 2, :], banks[0:1, 7, 0:D]).then_inc(v_ready, 1)

            def softmax(b, j):
                done = 0
                if mask is not None:
                    dve.wait_ge(arrived[j], START + (b - j) * (loads // 2) + loads)
                    dve.wait_ge(biased, START + b * bias_steps)
                    nc.vector.tensor_scalar(show[:, :], hide8[j][:, :], -1.0, 1.0, ALU.mult, ALU.add)\
                      .then_inc(biased, 1)
                    nc.vector.tensor_scalar(hidden[:, :], hide8[j][:, :], -1e9, None, ALU.mult)\
                      .then_inc(biased, 1)
                    done = 2
                dve.wait_ge(scores_ready, START + (b + 1) * 4)
                dve.wait_ge(exped, START + b)
                if mask is not None:
                    dve.wait_ge(biased, START + b * bias_steps + 2)
                    nc.vector.tensor_tensor(s[:, :, :], banks[:, 0:4, 0:M], bcast(show[:, :], 4), ALU.mult)\
                      .then_inc(biased, 1)
                    dve.wait_ge(biased, START + b * bias_steps + 3)
                    nc.vector.tensor_tensor(s[:, :, :], s[:, :, :], bcast(hidden[:, :], 4), ALU.add)\
                      .then_inc(biased, 1)
                else:
                    nc.vector.scalar_tensor_tensor(out=s[:, :, :], in0=banks[:, 0:4, 0:M], scalar=SC,
                                                   in1=rel[:, :, :], op0=ALU.mult, op1=ALU.add)\
                      .then_inc(biased, 1)
                dve.wait_ge(biased, START + (b + 1) * bias_steps)
                nc.vector.tensor_reduce(top[:, :], s[:, :, :], AX, ALU.max).then_inc(topped, 1)
                dve.wait_ge(topped, START + b + 1)
                nc.vector.tensor_scalar(neg[:, :], top[:, :], -SC if rel is None else -1.0, None, ALU.mult)\
                  .then_inc(negated, 1)

            def batch(b, j, ahead=1):
                if ahead:
                    values(b + 1, 1 - j)
                dve.wait_ge(exped, START + b + 1)
                nc.vector.reciprocal(inv[:, :], total[:, :]).then_inc(inverted, 1)
                dve.wait_ge(p_turned, START + b + 1)
                nc.vector.tensor_copy(pt[:, 1, :], banks[:, 5, :]).then_inc(pt_dve, 1)
                if ahead:
                    softmax(b + 1, 1 - j)
                dve.wait_ge(inverted, START + b + 1)
                dve.wait_ge(result_ready, START + b + 1)
                for n in range(4):
                    nc.vector.scalar_tensor_tensor(out=om[:, n, :], in0=banks[:, 6, n * 64:(n + 1) * 64],
                                                   scalar=inv[:, n:n + 1], in1=core.consts["own_head"][:, :],
                                                   op0=ALU.mult, op1=ALU.mult).then_inc(owned, 1)
                dve.wait_ge(out_made, START + b + 1)
                nc.vector.tensor_copy(out[:, :, blk(b, S)],
                                      banks[:, 6, 256:256 + KC * S].rearrange("p (c s) -> p c s", c=KC))\
                  .then_inc(out_taken, 1)

            values(0, 0)
            softmax(0, 0)
            with dve.Fori(0, B // 2 - 1) as r:
                for j in range(2):
                    batch(2 * r + j, j)
            batch(LAST - 1, 0)
            batch(LAST, 1, 0)


def cross_single(core, q, out, ctx_t, ctx_rows, row_w, row_src, row_bias, phi=None, phi_w=None, tops=None):
    nc = core.nc
    with ExitStack() as mem:
        def sb(name, shape):
            return mem.enter_context(nc.sbuf_tensor(f"{name}_{core.turn}", shape, F32))
        ctx_sb = [sb(f"ctx{j}", [P, KC, M]) for j in range(4)]
        rows_sb = [sb(f"rows{j}", [P, 3, D]) for j in range(4)]
        q_st, src_st = sb("q_st", [P, KC, GT]), sb("src_st", [P, KC, GT])
        phi_sb = sb("phi", [P, M])
        s, p = sb("s", [P, M]), sb("p", [P, M])
        pt = sb("pt", [P, 3, P])
        top, neg, total, inv, const = (sb(n, [P, 1]) for n in ("top", "neg", "total", "inv", "const"))
        (block, loaded_t, loaded_rows, loaded_phi, staged, scores_ready, summed, topped, negated, exped,
         inverted, normed, p_turned, pt_ready, out_ready, out_taken, passed) = mem.enter_context(
            phase(core, "loaded_t", "loaded_rows", "loaded_phi", "staged", "scores_ready", "summed", "topped",
                  "negated", "exped", "inverted", "normed", "p_turned", "pt_ready", "out_ready", "out_taken",
                  "passed"))
        sums = 3
        banks = core.banks8

        @block.sync
        def _(sp):
            with sp.Fori(0, NG) as g:
                sp.wait_ge(scores_ready, START + g)
                sp.sem_inc(passed, 1)
                for j in range(4):
                    sp.dma_start(ctx_sb[j][:, :, :], ctx_t[4 * g + j, :, :].rearrange("(k p) m -> p k m", p=P))\
                      .then_inc(loaded_t, 16)
                if phi is not None:
                    sp.wait_ge(summed, START + g * sums)
                    sp.sem_inc(passed, 1)
                    sp.dma_start(phi_sb[:, :], phi[blk(g, GT), :]).then_inc(loaded_phi, 16)
                sp.wait_ge(out_ready, START + g)
                sp.sem_inc(passed, 1)
                for j in range(4):
                    sp.dma_start(rows_sb[j][:, 0:2, :], ctx_rows[4 * g + j, 0:2 * P, :]
                                 .rearrange("(c p) f -> p c f", p=P)).then_inc(loaded_rows, 16)
                    sp.dma_start(rows_sb[j][0:1, 2, :], ctx_rows[4 * g + j, 2 * P:M, :]).then_inc(loaded_rows, 16)

        @block.gpsimd
        def _(pool):
            with pool.Fori(0, NG) as g:
                pool.wait_ge(scores_ready, START + g)
                pool.sem_inc(passed, 1)
                nc.gpsimd.tensor_copy(q_st[:, :, :], q[:, :, blk(g, GT)]).then_inc(staged, 1)
                nc.gpsimd.tensor_copy(src_st[:, :, :], row_src[:, :, blk(g, GT)]).then_inc(staged, 1)

        @block.tensor
        def _(pe):
            with pe.Fori(0, NG) as g:
                pe.wait_ge(loaded_t, START + (g + 1) * 64)
                pe.wait_ge(staged, START + 2 * g + 2)
                pe.wait_ge(summed, START + g * sums)
                for k in range(KC):
                    pe.matmul(banks[:, 1, 0:1], src_st[:, k, :], row_w[:, k:k + 1], start=(k == 0),
                              stop=(k == KC - 1))
                for j in range(4):
                    for k in range(KC):
                        ins = pe.matmul(banks[32 * j:32 * j + 32, 0, 0:M], q_st[:, k, 32 * j:32 * j + 32],
                                        ctx_sb[j][:, k, :], start=(k == 0), stop=(k == KC - 1))
                ins.then_inc(scores_ready, 1)
                pe.wait_ge(normed, START + g + 1)
                pe.wait_ge(pt_ready, START + g)
                for c, (at, m) in enumerate(KCH):
                    ins = pe.transpose(banks[0:m, 2, c * P:(c + 1) * P], p[:, at:at + m], core.ident[:, :])
                ins.then_inc(p_turned, 1)
                pe.wait_ge(pt_ready, START + g + 1)
                pe.wait_ge(loaded_rows, START + (g + 1) * 128)
                pe.wait_ge(out_taken, START + g)
                for j in range(4):
                    for f in range(KC):
                        for c, (at, m) in enumerate(KCH):
                            ins = pe.matmul(banks[:, 3, f * P + 32 * j:f * P + 32 * j + 32],
                                            rows_sb[j][0:m, c, f * P:(f + 1) * P], pt[0:m, c, 32 * j:32 * j + 32],
                                            start=(c == 0), stop=(c == 2))
                ins.then_inc(out_ready, 1)

        @block.scalar
        def _(act):
            with act.Fori(0, NG) as g:
                act.wait_ge(negated, START + g + 1)
                act.wait_ge(p_turned, START + g)
                nc.scalar.activation(p[:, :], s[:, :], ACT.Exp, bias=neg[:, 0:1], accum_out=total[:, 0:1])\
                  .then_inc(exped, 1)
                act.wait_ge(p_turned, START + g + 1)
                act.wait_ge(out_ready, START + g)
                nc.scalar.copy(pt[:, 0:2, :], banks[:, 2, 0:2 * P].rearrange("p (c w) -> p c w", c=2))
                nc.scalar.copy(pt[0:1, 2, :], banks[0:1, 2, 2 * P:3 * P]).then_inc(pt_ready, 1)

        @block.vector
        def _(dve):
            with dve.Fori(0, NG) as g:
                dve.wait_ge(scores_ready, START + g + 1)
                dve.wait_ge(exped, START + g)
                nc.vector.tensor_scalar(const[:, :], banks[:, 1, 0:1], row_bias, None, ALU.add).then_inc(summed, 1)
                if phi is not None:
                    dve.wait_ge(loaded_phi, START + (g + 1) * 16)
                    nc.vector.scalar_tensor_tensor(out=s[:, :], in0=phi_sb[:, :], scalar=phi_w,
                                                   in1=banks[:, 0, 0:M], op0=ALU.mult, op1=ALU.add).then_inc(summed, 1)
                else:
                    nc.vector.tensor_copy(s[:, :], banks[:, 0, 0:M]).then_inc(summed, 1)
                dve.wait_ge(summed, START + g * sums + 2)
                nc.vector.tensor_scalar(s[:, :], s[:, :], const[:, 0:1], None, ALU.add).then_inc(summed, 1)
                dve.wait_ge(summed, START + g * sums + 3)
                nc.vector.tensor_reduce(top[:, :], s[:, :], AX, ALU.max).then_inc(topped, 1)
                dve.wait_ge(topped, START + g + 1)
                if tops is not None:
                    nc.vector.tensor_copy(tops[:, bass.ds(g, 1)], top[:, :])
                nc.vector.tensor_scalar(neg[:, :], top[:, :], -1.0, None, ALU.mult).then_inc(negated, 1)
                dve.wait_ge(exped, START + g + 1)
                nc.vector.reciprocal(inv[:, :], total[:, :]).then_inc(inverted, 1)
                dve.wait_ge(inverted, START + g + 1)
                nc.vector.tensor_scalar(p[:, :], p[:, :], inv[:, 0:1], None, ALU.mult).then_inc(normed, 1)
                dve.wait_ge(out_ready, START + g + 1)
                nc.vector.tensor_copy(out[:, :, blk(g, GT)],
                                      banks[:, 3, 0:KC * P].rearrange("p (f n) -> p f n", f=KC)).then_inc(out_taken, 1)


def gates(core, x, w, bias, gate_rows, experts, shared=0):
    nc = core.nc
    E = experts
    with ExitStack() as mem:
        def sb(name, shape, dt=F32):
            return mem.enter_context(nc.sbuf_tensor(f"{name}_{core.turn}", shape, dt))
        z, e = sb("z", [P, NG, E]), sb("e", [P, NG, E])
        top, total, inv = (sb(n, [P, NG]) for n in ("top", "total", "inv"))
        best, which = sb("best", [P, NG, 8]), sb("which", [P, NG, 8], U32)
        at = sb("at", [P, NG, 8])
        first, second = sb("first", [P, NG, E]), sb("second", [P, NG, E])
        gate_t = sb("gate_t", [E, N])
        ones = sb("ones", [1, N])
        experts_at = core.consts["iota16"]
        (block, logits_ready, step, exped, found, turned, taken, kept, filled) = mem.enter_context(
            phase(core, "logits_ready", "step", "exped", "found", "turned", "taken", "kept", "filled"))

        @block.tensor
        def _(pe):
            for g in range(NG):
                for k in range(KC):
                    ins = pe.matmul(core.psum[0][:, g * E:(g + 1) * E], x[:, k, g * GT:(g + 1) * GT], w[:, k, :],
                                    start=(k == 0), stop=(k == KC - 1))
            ins.then_inc(logits_ready, 1)
            pe.wait_ge(found, START + 1)
            for g in range(NG):
                ins = pe.transpose(core.psum[4 + g // 4][0:E, (g % 4) * P:(g % 4 + 1) * P], second[:, g, :],
                                   core.ident[:, :])
            ins.then_inc(turned, 1)

        @block.scalar
        def _(act):
            act.wait_ge(step, START + 3)
            nc.scalar.activation(e[:, :, :], z[:, :, :], ACT.Exp).then_inc(exped, 1)

        @block.gpsimd
        def _(pool):
            nc.gpsimd.memset(ones[:, :], 1.0).then_inc(filled, 1)

        @block.sync
        def _(sp):
            sp.wait_ge(filled, START + 1)
            sp.wait_ge(taken, START + 1)
            sp.dma_start(gate_rows[0:E, :], gate_t[:, :]).then_inc(kept, 16)
            for j in range(shared):
                sp.dma_start(gate_rows[E + j:E + j + 1, :], ones[:, :]).then_inc(kept, 16)
            sp.wait_ge(kept, START + 16 * (1 + shared))

        @block.vector
        def _(dve):
            n = 0

            def then(ins):
                nonlocal n
                n += 1
                ins.then_inc(step, 1)
                dve.wait_ge(step, START + n)

            dve.wait_ge(logits_ready, START + 1)
            logits = core.psum[0][:, 0:NG * E].rearrange("p (g e) -> p g e", e=E)
            then(nc.vector.tensor_tensor(z[:, :, :], logits, bcast(bias[:, :], NG), ALU.add))
            then(nc.vector.tensor_reduce(top[:, :], z[:, :, :], AX, ALU.max))
            then(nc.vector.tensor_tensor(z[:, :, :], z[:, :, :], bcast(top[:, :], E, 2), ALU.subtract))
            dve.wait_ge(exped, START + 1)
            then(nc.vector.tensor_reduce(total[:, :], e[:, :, :], AX, ALU.add))
            then(nc.vector.reciprocal(inv[:, :], total[:, :]))
            then(nc.vector.tensor_tensor(e[:, :, :], e[:, :, :], bcast(inv[:, :], E, 2), ALU.mult))
            for g in range(NG):
                ins = nc.vector.max(best[:, g, :], e[:, g, :])
            then(ins)
            for g in range(NG):
                ins = nc.vector.max_index(which[:, g, :], best[:, g, :], e[:, g, :])
            then(ins)
            then(nc.vector.tensor_copy(at[:, :, :], which[:, :, :]))
            for g in range(NG):
                nc.vector.tensor_scalar(first[:, g, :], experts_at[:, 0:E], at[:, g, 0:1], best[:, g, 0:1],
                                        ALU.is_equal, ALU.mult)
                ins = nc.vector.tensor_scalar(second[:, g, :], experts_at[:, 0:E], at[:, g, 1:2],
                                              best[:, g, 1:2], ALU.is_equal, ALU.mult)
            then(ins)
            nc.vector.tensor_tensor(second[:, :, :], second[:, :, :], first[:, :, :], ALU.add).then_inc(found, 1)
            dve.wait_ge(turned, START + 1)
            nc.vector.tensor_copy(gate_t[:, :].rearrange("e (b n) -> e b n", b=4),
                                  core.banks8[0:E, 4:8, :]).then_inc(taken, 1)


def experts_sum(core, kind, x, acc, gate_rows, experts, w1, w2, b1=None, b2=None, hidden=None):
    nc = core.nc
    hc = hidden // P if hidden else 0
    hp = 2 * hc if kind == "glu" else hc
    with ExitStack() as mem:
        def sb(name, shape):
            return mem.enter_context(nc.sbuf_tensor(f"{name}_{core.turn}", shape, F32))
        w1_sb = [sb(f"w1_{j}", [P, KC, hp * P if hp else D]) for j in range(2)]
        w2_sb = [sb(f"w2_{j}", [P, hc, D]) for j in range(2)] if hc else None
        b1_sb = [sb(f"b1_{j}", [P, hc]) for j in range(2)] if b1 is not None else None
        b2_sb = [sb(f"b2_{j}", [P, KC]) for j in range(2)] if b2 is not None else None
        gate = [sb(f"gate_{j}", [P, N]) for j in range(2)]
        h = sb("h", [P, 2, hc, BLK]) if hc else None
        act_g = sb("act_g", [P, 2, BLK]) if kind == "glu" else None
        y = sb("y", [P, 2, KC, BLK])
        (block, loaded, h_made, h_ready, y_made, y_gated, added, glu_ready, loaded1, passed) = mem.enter_context(
            phase(core, "loaded", "h_made", "h_ready", "y_made", "y_gated", "added", "glu_ready", "loaded1",
                  "passed"))
        arrived = [loaded, loaded1]
        loads = 16 * (2 + bool(hc) + (b1 is not None) + (b2 is not None))
        banks = core.banks8
        y_at = 4
        credit = {"relu": hc, "plain": 0, "glu": 2}[kind]

        @block.sync
        def _(sp):
            def fetch(e, j):
                sp.dma_start(w1_sb[j][:, :, :], w1[e, :, :].rearrange("(k p) m -> p k m", p=P)).then_inc(arrived[j], 16)
                if hc:
                    sp.dma_start(w2_sb[j][:, :, :], w2[e, :, :].rearrange("(k p) m -> p k m", p=P))\
                      .then_inc(arrived[j], 16)
                if b1 is not None:
                    sp.dma_start(b1_sb[j][:, :], b1[e, :, :]).then_inc(arrived[j], 16)
                if b2 is not None:
                    sp.dma_start(b2_sb[j][:, :], b2[e, :, :]).then_inc(arrived[j], 16)
                sp.dma_start(gate[j][:, :], gate_rows[bass.ds(e, 1), :].broadcast_to([P, N])).then_inc(arrived[j], 16)

            fetch(0, 0)
            fetch(1, 1)
            if experts > 2:
                with sp.Fori(0, experts // 2 - 1) as r:
                    for j in range(2):
                        sp.wait_ge(y_gated, START + (2 * r + j + 1) * NB * KC)
                        sp.sem_inc(passed, 1)
                        fetch(2 * r + j + 2, j)

        @block.tensor
        def _(pe):
            def first(e, j, t):
                n = e * NB + t
                pe.wait_ge(arrived[j], START + (e - j) * (loads // 2) + loads)
                for m in range(hp):
                    bank = m if hc == 4 else 2 * (t % 2) + m
                    pe.wait_ge(h_ready, START + (n * hc + (m + 1 if kind == "relu" else 1)))
                    for k in range(KC):
                        ins = pe.matmul(banks[:, bank, :], w1_sb[j][:, k, m * P:(m + 1) * P], x[:, k, blk(t)],
                                        start=(k == 0), stop=(k == KC - 1))
                    ins.then_inc(h_made, 1)

            def second(e, j, t):
                n = e * NB + t
                if hc:
                    pe.wait_ge(h_ready, START + (n + 1) * hc + credit)
                else:
                    pe.wait_ge(arrived[j], START + (e - j) * (loads // 2) + loads)
                for m in range(KC):
                    pe.wait_ge(added, START + n * KC + m + 1)
                    bank = y_at + 2 * (t % 2) + m
                    if hc:
                        for k in range(hc):
                            ins = pe.matmul(banks[:, bank, :], w2_sb[j][:, k, m * P:(m + 1) * P],
                                            h[:, t % 2, k, :], start=(k == 0), stop=(k == hc - 1))
                    else:
                        for k in range(KC):
                            ins = pe.matmul(banks[:, bank, :], w1_sb[j][:, k, m * P:(m + 1) * P], x[:, k, blk(t)],
                                            start=(k == 0), stop=(k == KC - 1))
                    ins.then_inc(y_made, 1)

            if hc:
                first(0, 0, 0)
            with pe.Fori(0, experts // 2 - 1) as r:
                for j in range(2):
                    for t in range(NB):
                        if hc:
                            if t + 1 < NB:
                                first(2 * r + j, j, t + 1)
                            else:
                                first(2 * r + j + 1, 1 - j, 0)
                        second(2 * r + j, j, t)
            for j in range(2):
                for t in range(NB):
                    if hc:
                        if t + 1 < NB:
                            first(experts - 2 + j, j, t + 1)
                        elif j == 0:
                            first(experts - 1, 1, 0)
                    second(experts - 2 + j, j, t)

        @block.scalar
        def _(act):
            if kind == "plain":
                return
            act.sem_inc(h_ready, credit)
            with act.Fori(0, experts // 2) as r:
                for j in range(2):
                    for t in range(NB):
                        n = (2 * r + j) * NB + t
                        if kind == "relu":
                            for m in range(hc):
                                act.wait_ge(h_made, START + n * hp + m + 1)
                                act.wait_ge(y_made, START + (((n - 1) * KC) if t >= 1 else (2 * r + j) * NB * KC - KC * j))
                                nc.scalar.activation(h[:, t % 2, m, :], banks[:, m, :], ACT.Relu,
                                                     bias=b1_sb[j][:, m:m + 1]).then_inc(h_ready, 1)
                        else:
                            act.wait_ge(h_made, START + n * 2 + 1)
                            act.wait_ge(h_ready, START + n - 1 + credit)
                            nc.scalar.activation(act_g[:, t % 2, :], banks[:, 2 * (t % 2), :], ACT.Silu)\
                              .then_inc(glu_ready, 1)

        @block.vector
        def _(dve):
            dve.sem_inc(added, 4)
            with dve.Fori(0, experts // 2) as r:
                for j in range(2):
                    for t in range(NB):
                        n = (2 * r + j) * NB + t

                        def glu(n, t):
                            dve.wait_ge(glu_ready, START + n + 1)
                            dve.wait_ge(h_made, START + n * 2 + 2)
                            nc.vector.tensor_tensor(h[:, t % 2, 0, :], act_g[:, t % 2, :],
                                                    banks[:, 2 * (t % 2) + 1, :], ALU.mult).then_inc(h_ready, 1)

                        if kind == "glu":
                            glu(n, t)
                        for m in range(KC):
                            dve.wait_ge(y_made, START + n * KC + m + 1)
                            dve.wait_ge(arrived[j], START + (r + 1) * loads)
                            dve.wait_ge(added, START + n * KC + m + 1)
                            nc.vector.scalar_tensor_tensor(
                                out=y[:, t % 2, m, :], in0=banks[:, y_at + 2 * (t % 2) + m, :],
                                scalar=b2_sb[j][:, m:m + 1] if b2 is not None else 0.0,
                                in1=gate[j][:, blk(t)], op0=ALU.add, op1=ALU.mult).then_inc(y_gated, 1)
                            dve.wait_ge(y_gated, START + n * KC + m + 1)
                            nc.vector.tensor_tensor(acc[:, m, blk(t)], acc[:, m, blk(t)], y[:, t % 2, m, :],
                                                    ALU.add).then_inc(added, 1)


def rms_norm(core, t, w):
    nc = core.nc
    with ExitStack() as mem:
        def sb(name, shape):
            return mem.enter_context(nc.sbuf_tensor(f"{name}_{core.turn}", shape, F32))
        sq, std, inv = sb("sq", [P, 2, KC, BLK]), sb("std", [P, 2, KC, BLK]), sb("inv", [P, 2, KC, BLK])
        block, squared, mean_ready, std_ready, inverted, done = mem.enter_context(
            phase(core, "squared", "mean_ready", "std_ready", "inverted", "done"))

        @block.gpsimd
        def _(pool):
            for n in range(NB):
                if n >= 2:
                    pool.wait_ge(mean_ready, START + n - 1)
                nc.gpsimd.tensor_tensor(sq[:, n % 2, :, :], t[:, :, blk(n)], t[:, :, blk(n)], ALU.mult)\
                  .then_inc(squared, 1)

        @block.tensor
        def _(pe):
            for n in range(NB):
                pe.wait_ge(squared, START + n + 1)
                if n >= 2:
                    pe.wait_ge(std_ready, START + n - 1)
                for k in range(KC):
                    ins = pe.matmul(core.psum[2 * (n % 2) + k], core.consts["same_head"][:, :],
                                    sq[:, n % 2, k, :], start=True, stop=True)
                ins.then_inc(mean_ready, 1)

        @block.scalar
        def _(act):
            for n in range(NB):
                act.wait_ge(mean_ready, START + n + 1)
                if n >= 2:
                    act.wait_ge(inverted, START + n - 1)
                nc.scalar.activation(std[:, n % 2, :, :], core.banks8[:, 2 * (n % 2):2 * (n % 2) + 2, :], ACT.Sqrt,
                                     bias=core.eps[:, 1:2]).then_inc(std_ready, 1)

        @block.vector
        def _(dve):
            for n in range(NB):
                dve.wait_ge(std_ready, START + n + 1)
                nc.vector.reciprocal(inv[:, n % 2, :, :], std[:, n % 2, :, :]).then_inc(inverted, 1)
                dve.wait_ge(inverted, START + n + 1)
                dve.wait_ge(squared, START + n + 1)
                for k in range(KC):
                    nc.vector.scalar_tensor_tensor(out=t[:, k, blk(n)], in0=inv[:, n % 2, k, :],
                                                   scalar=w[:, k:k + 1], in1=t[:, k, blk(n)], op0=ALU.mult,
                                                   op1=ALU.mult).then_inc(done, 1)


def elementwise(core, *steps):
    with phase(core, "step") as (block, step):
        @block.vector
        def _(dve):
            for n, f in enumerate(steps):
                f().then_inc(step, 1)
                dve.wait_ge(step, START + n + 1)


def butterfly(core, w, row, stage_w, backwards):
    nc = core.nc
    hidden, stages = 4 * D, 10
    with ExitStack() as mem:
        def sb(name, shape):
            return mem.enter_context(nc.sbuf_tensor(f"{name}_{core.turn}", shape, F32))
        sw = [sb(f"sw{j}", [P, hidden * 2]) for j in range(2)]
        t = [sb(f"t{j}", [P, KC, hidden // 2]) for j in range(4)]
        tr = [sb(f"tr{j}", [1, hidden // 2]) for j in range(4)]
        block, loaded0, loaded1, step, used = mem.enter_context(phase(core, "loaded0", "loaded1", "step", "used"))
        arrived = [loaded0, loaded1]
        order = range(stages - 1, -1, -1) if backwards else range(stages)

        @block.sync
        def _(sp):
            for n, st in enumerate(order):
                if n >= 2:
                    sp.wait_ge(used, START + n - 1)
                sp.dma_start(sw[n % 2][:, :], stage_w[st:st + 1, :].broadcast_to([P, 2 * hidden]))\
                  .then_inc(arrived[n % 2], 16)

        @block.vector
        def _(dve):
            done = 0
            for n, st in enumerate(order):
                half = 2 ** st
                dve.wait_ge(arrived[n % 2], START + 16 * (n // 2 + 1))
                wv = sw[n % 2][:, :].rearrange("p (b s q) -> p b s q", s=half, q=4)
                both = []
                for c in range(KC):
                    v = w[:, c, :].rearrange("p (b h s) -> p b h s", h=2, s=half)
                    both.append((v[:, :, 0, :], v[:, :, 1, :], wv, [x[:, c, :] for x in t]))
                if row is not None:
                    v = row[:, :].rearrange("p (b h s) -> p b h s", h=2, s=half)
                    both.append((v[:, :, 0, :], v[:, :, 1, :], wv[0:1], [x[:, :] for x in tr]))
                order4 = [(0, 0), (2, 1), (1, 0), (3, 1)] if backwards else [(0, 0), (1, 1), (2, 0), (3, 1)]
                for a, b, ww, tt in both:
                    for i, (q, which) in enumerate(order4):
                        ins = nc.vector.tensor_tensor(tt[i].rearrange("p (b s) -> p b s", s=half),
                                                      (a, b)[which], ww[:, :, :, q], ALU.mult)
                        ins.then_inc(step, 1)
                        done += 1
                dve.wait_ge(step, START + done)
                for a, b, ww, tt in both:
                    for o, i in ((a, 0), (b, 2)):
                        tv = [x.rearrange("p (b s) -> p b s", s=half) for x in tt[i:i + 2]]
                        nc.vector.tensor_tensor(o, tv[0], tv[1], ALU.add).then_inc(step, 1)
                        done += 1
                dve.wait_ge(step, START + done)
                dve.sem_inc(used, 1)


def turn_weights(core, src, dst, row=None, row_dst=None):
    nc = core.nc
    with phase(core, "turned", "taken") as (block, turned, taken):
        @block.tensor
        def _(pe):
            for h in range(8):
                for c in range(KC):
                    ins = pe.transpose(core.psum[h % 4][:, c * P:(c + 1) * P] if h < 4 else
                                       core.psum[h % 4][:, (2 + c) * P:(3 + c) * P],
                                       src[:, c, h * P:(h + 1) * P], core.ident[:, :])
            if row is not None:
                for h in range(8):
                    ins = pe.transpose(core.psum[4][:, h:h + 1], row[:, h * P:(h + 1) * P], core.ident[0:1, 0:1])
            ins.then_inc(turned, 1)

        @block.vector
        def _(dve):
            dve.wait_ge(turned, START + 1)
            for half in range(2):
                nc.vector.tensor_copy(dst[:, 4 * half:4 * half + 4, :],
                                      core.banks8[:, 0:4, half * D:(half + 1) * D]).then_inc(taken, 1)
            if row is not None:
                nc.vector.tensor_copy(row_dst[:, :], core.psum[4][:, 0:8]).then_inc(taken, 1)


def context_mean(core, x, tops, mixed):
    nc = core.nc
    nb = BLK // S
    with ExitStack() as mem:
        def sb(name, shape):
            return mem.enter_context(nc.sbuf_tensor(f"{name}_{core.turn}", shape, F32))
        diag = sb("diag", [P, 4, P])
        z, e = sb("z", [P, nb, S]), sb("e", [P, nb, S])
        top, total, inv = (sb(n, [P, nb]) for n in ("top", "total", "inv"))
        wx, bar = sb("wx", [P, KC, BLK]), sb("bar", [P, KC * nb])
        block, diag_ready, spread, centred, exped, step = mem.enter_context(
            phase(core, "diag_ready", "spread", "centred", "exped", "step"))

        @block.tensor
        def _(pe):
            for t in range(NB):
                pe.wait_ge(diag_ready, START + t + 1)
                pe.matmul(core.psum[t], core.consts["ones"][:, :], diag[:, :, :].rearrange("p g w -> p (g w)"),
                          start=True, stop=True).then_inc(spread, 1)

        @block.gpsimd
        def _(pool):
            for t in range(NB):
                if t >= 1:
                    pool.wait_ge(spread, START + t)
                nc.gpsimd.tensor_tensor(diag[:, :, :], bcast(core.ident[:, :], 4),
                                        bcast(tops[:, 4 * t:4 * t + 4], P, 2), ALU.mult).then_inc(diag_ready, 1)

        @block.scalar
        def _(act):
            for t in range(NB):
                act.wait_ge(centred, START + t + 1)
                nc.scalar.activation(e[:, :, :], z[:, :, :], ACT.Exp).then_inc(exped, 1)

        @block.vector
        def _(dve):
            n = 0

            def then(ins):
                nonlocal n
                n += 1
                ins.then_inc(step, 1)
                dve.wait_ge(step, START + n)

            for t in range(NB):
                dve.wait_ge(spread, START + t + 1)
                m = core.psum[t].rearrange("p (b s) -> p b s", s=S)
                then(nc.vector.tensor_reduce(top[:, :], m, AX, ALU.max))
                nc.vector.tensor_tensor(z[:, :, :], m, bcast(top[:, :], S, 2), ALU.subtract).then_inc(centred, 1)
                dve.wait_ge(exped, START + t + 1)
                then(nc.vector.tensor_reduce(total[:, :], e[:, :, :], AX, ALU.add))
                then(nc.vector.reciprocal(inv[:, :], total[:, :]))
                then(nc.vector.tensor_tensor(e[:, :, :], e[:, :, :], bcast(inv[:, :], S, 2), ALU.mult))
                then(nc.vector.tensor_tensor(wx[:, :, :], x[:, :, blk(t)],
                                             bcast(e[:, :, :].rearrange("p b s -> p (b s)"), KC), ALU.mult))
                then(nc.vector.tensor_reduce(bar[:, :], wx[:, :, :].rearrange("p k (b s) -> p (k b) s", s=S), AX,
                                             ALU.add))
                for k in range(KC):
                    then(nc.vector.tensor_tensor(
                        mixed[:, k, blk(t)].rearrange("p (b s) -> p b s", s=S),
                        x[:, k, blk(t)].rearrange("p (b s) -> p b s", s=S),
                        bcast(bar[:, k * nb:(k + 1) * nb], S, 2), ALU.mult))


def perceiver(nc, dram, out, scratch, layers=12):
    with ExitStack() as ctx:
        core = Core(nc, ctx, dram)
        start(core)
        steps = [l0_xattn, l0_attn, l0_ffn, l1_xattn, l1_attn, l1_ffn, l2_xattn, l2_attn, l2_ffn, l3_xattn,
                 l3_attn, l3_ffn]
        for step in steps[:layers]:
            with ExitStack() as mem:
                turn = core.turn

                def sb(name, *shape):
                    return mem.enter_context(nc.sbuf_tensor(f"{name}_{turn}", list(shape), F32))
                step(core, sb, scratch)
        store(core, core.x, out)


def weights(core, sb, layer, mats, vecs=()):
    got, pairs = [], []
    for name in mats:
        d = core.dram[f"{layer}_{name}"]
        tile = sb(name, P, d.shape[0] // P, d.shape[1])
        pairs.append((tile[:, :, :], chunks(d)))
        got.append(tile)
    for name in vecs:
        d = core.dram[f"{layer}_{name}"]
        tile = sb(name, P, d.shape[1])
        pairs.append((tile[:, :], d if d.shape[0] == P else d.broadcast_to([P, d.shape[1]])))
        got.append(tile)
    load(core, *pairs)
    return got


def l0_xattn(core, sb, scratch):
    q1, k1, o1, q2, k2, o2, f1, f2, fb1, fb2, g1, b1, g2, b2, g3, b3 = weights(
        core, sb, "L0_xattn", ["q1W", "w1W", "o1W", "q2W", "w2W", "o2W", "ffW1", "ffW2"],
        ["ffb1", "ffb2", "g1", "b1", "g2", "b2", "g3", "b3"])
    xn, q, k, o = (sb(n, P, KC, N) for n in ("xn", "q", "k", "o"))
    layer_norm(core, core.x, xn)
    linear(core, q1, xn, q)
    linear(core, k1, xn, k)
    self_attention(core, "heads", q, k, k, o, KC, 0.25, core.consts["mask_block"])
    linear(core, o1, o, xn, kind="residual")
    layer_norm(core, xn, xn, (g1, b1))
    linear(core, q2, xn, q)
    cross_attention(core, q, k2, k2, o, core.dram["ctx_t"], mask=core.dram["mask"])
    linear(core, o2, o, xn, kind="residual")
    layer_norm(core, xn, xn, (g2, b2))
    mlp(core, xn, f1, fb1, f2, fb2, xn)
    layer_norm(core, xn, core.x, (g3, b3), add=core.x)


def mlp(core, x, w1, b1, w2, b2, out):
    nc = core.nc
    HC = 8
    with ExitStack() as mem:
        h = mem.enter_context(nc.sbuf_tensor(f"h_{core.turn}", [P, 2, HC, BLK], F32))
        block, h_made, h_ready, y_made, y_taken = mem.enter_context(
            phase(core, "h_made", "h_ready", "y_made", "y_taken"))

        @block.tensor
        def _(pe):
            def first(t):
                for m in range(HC):
                    n = t * HC + m
                    if n >= 4:
                        pe.wait_ge(h_ready, START + n - 3)
                    for k in range(KC):
                        ins = pe.matmul(core.psum[m % 4], w1[:, k, m * P:(m + 1) * P], x[:, k, blk(t)],
                                        start=(k == 0), stop=(k == KC - 1))
                    ins.then_inc(h_made, 1)

            def second(t):
                pe.wait_ge(h_ready, START + (t + 1) * HC)
                for m in range(KC):
                    if t >= 2:
                        pe.wait_ge(y_taken, START + (t - 2) * KC + m + 1)
                    for k in range(HC):
                        ins = pe.matmul(core.psum[4 + 2 * (t % 2) + m], w2[:, k, m * P:(m + 1) * P],
                                        h[:, t % 2, k, :], start=(k == 0), stop=(k == HC - 1))
                    ins.then_inc(y_made, 1)

            first(0)
            for t in range(NB):
                if t + 1 < NB:
                    first(t + 1)
                second(t)

        @block.scalar
        def _(act):
            for t in range(NB):
                for m in range(HC):
                    act.wait_ge(h_made, START + t * HC + m + 1)
                    if t >= 2:
                        act.wait_ge(y_made, START + (t - 1) * KC)
                    nc.scalar.activation(h[:, t % 2, m, :], core.psum[m % 4], ACT.Gelu, bias=b1[:, m:m + 1])\
                      .then_inc(h_ready, 1)

        @block.vector
        def _(dve):
            for t in range(NB):
                dve.wait_ge(h_made, START + (t + 1) * HC)
                for m in range(KC):
                    dve.wait_ge(y_made, START + t * KC + m + 1)
                    nc.vector.scalar_tensor_tensor(out=out[:, m, blk(t)], in0=core.psum[4 + 2 * (t % 2) + m],
                                                   scalar=b2[:, m:m + 1], in1=out[:, m, blk(t)], op0=ALU.add,
                                                   op1=ALU.add).then_inc(y_taken, 1)


def l0_attn(core, sb, scratch):
    wqkv, wo, bqkv, bo = weights(core, sb, "L0_attn", ["W_qkv", "W_out"], ["b_qkv", "b_out"])
    xn, o, qkv = sb("xn", P, KC, N), sb("o", P, KC, N), sb("qkv", P, 6, N)
    layer_norm(core, core.x, xn)
    linear(core, wqkv, xn, qkv, bias=bqkv, mc=6)
    parts = [scratch["qkv"][i * D:(i + 1) * D, :] for i in range(3)]
    load(core, *[(chunks(parts[i]), qkv[:, 2 * i:2 * i + 2, :]) for i in range(3)])
    self_attention(core, "segments", *parts, scratch["seg_out"], KC, 512 ** -0.5, core.consts["mask_segments"])
    load(core, (o[:, :, :], chunks(scratch["seg_out"])))
    linear(core, wo, o, core.x, bias=bo, kind="residual")


def l0_ffn(core, sb, scratch):
    gw, gb = weights(core, sb, "L0_ffn", ["gate_w"], ["gate_b"])
    d = core.dram
    xn = sb("xn", P, KC, N)
    layer_norm(core, core.x, xn)
    gates(core, xn, gw, gb, scratch["gates"], 8)
    experts_sum(core, "relu", xn, core.x, scratch["gates"], 8, d["L0_ffn_w1"], d["L0_ffn_w2"], d["L0_ffn_b1"],
                d["L0_ffn_b2"], hidden=512)


def l1_xattn(core, sb, scratch):
    nc = core.nc
    wq, wk, wv, wo, w_rel = weights(core, sb, "L1_xattn", ["w_q", "w_k", "w_v", "w_proj"], ["w_rel"])
    xn, q, o, rel = sb("xn", P, KC, N), sb("q", P, KC, N), sb("o", P, KC, N), sb("rel", P, 4, M)
    layer_norm(core, core.x, xn)
    linear(core, wq, xn, q)
    elementwise(core, *[lambda n=n: nc.vector.tensor_scalar(rel[:, n, :], core.consts["positions"][:, :],
                                                            w_rel[:, n:n + 1], None, ALU.mult) for n in range(4)])
    cross_attention(core, q, wk, wv, o, core.dram["ctx_t"], rel=rel)
    linear(core, wo, o, core.x, kind="residual")


def l1_attn(core, sb, scratch):
    wq, wv, qw, vw = weights(core, sb, "L1_attn", ["Wq", "Wv"], ["q_norm_w", "v_norm_w"])
    xn, q, v, o = (sb(n, P, KC, N) for n in ("xn", "q", "v", "o"))
    layer_norm(core, core.x, xn)
    linear(core, wq, xn, q)
    linear(core, wv, xn, v)
    rms_norm(core, q, qw)
    rms_norm(core, v, vw)
    self_attention(core, "linear", q, xn, v, o, KC, mask=core.consts["mask_lower"])
    elementwise(core, lambda: core.nc.vector.tensor_tensor(core.x[:, :, :], core.x[:, :, :], o[:, :, :], ALU.add))


def l1_ffn(core, sb, scratch):
    nc = core.nc
    wq, wk, wv, wo, wg, bq, bk, bv, bo, g1, be1, g2, be2, bg = weights(
        core, sb, "L1_ffn", ["Wq", "Wk", "Wv", "Wo", "Wg"],
        ["bq", "bk", "bv", "bo", "g1", "be1", "g2", "be2", "bg"])
    xn, q, k, v, o = (sb(n, P, KC, N) for n in ("xn", "q", "k", "v", "o"))
    d = core.dram
    layer_norm(core, core.x, xn)
    linear(core, wq, xn, q, bias=bq)
    linear(core, wk, xn, k, bias=bk)
    linear(core, wv, xn, v, bias=bv)
    self_attention(core, "heads", q, k, v, o, KC, 0.25, core.consts["mask_block"])
    linear(core, wo, o, q, bias=bo)
    layer_norm(core, q, xn, (g1, be1), add=xn)
    gates(core, xn, wg, bg, scratch["gates"], 8)
    elementwise(core, lambda: nc.vector.memset(k[:, :, :], 0.0))
    experts_sum(core, "plain", xn, k, scratch["gates"], 8, d["L1_ffn_We"], None, b2=d["L1_ffn_bexp"])
    layer_norm(core, k, xn, (g2, be2), add=xn)
    elementwise(core, lambda: nc.vector.tensor_tensor(core.x[:, :, :], core.x[:, :, :], xn[:, :, :], ALU.add))


def l2_xattn(core, sb, scratch):
    nc = core.nc
    wqv, w_sim, b_sim, bqv = weights(core, sb, "L2_xattn", ["W_qv"], ["w_sim", "b_sim", "b_qv"])
    xn, q, hat, mixed, tops = (sb("xn", P, KC, N), sb("q", P, KC, N), sb("hat", P, KC, N),
                               sb("mixed", P, KC, N), sb("tops", P, NG))
    d = core.dram
    layer_norm(core, core.x, xn)
    elementwise(core, *[lambda k=k: nc.vector.tensor_scalar(q[:, k, :], xn[:, k, :], w_sim[:, 4 + k:5 + k],
                                                            w_sim[:, 2 + k:3 + k], ALU.mult, ALU.add)
                        for k in range(KC)])
    cross_single(core, q, hat, d["ctx_t"], d["ctx"], w_sim, xn, b_sim[:, 0:1], tops=tops)
    linear(core, wqv[:, 0:2, :], xn, core.x, bias=bqv, kind="residual")
    linear(core, wqv[:, 2:4, :], hat, core.x, kind="residual")
    elementwise(core, lambda: nc.vector.tensor_tensor(hat[:, :, :], hat[:, :, :], xn[:, :, :], ALU.mult))
    linear(core, wqv[:, 4:6, :], hat, core.x, kind="residual")
    context_mean(core, xn, tops, mixed)
    linear(core, wqv[:, 6:8, :], mixed, core.x, kind="residual")


def l2_attn(core, sb, scratch):
    wq, wk, wv = weights(core, sb, "L2_attn", ["W_Q", "W_K", "W_V"])
    xn, q, k, o = (sb(n, P, KC, N) for n in ("xn", "q", "k", "o"))
    layer_norm(core, core.x, xn)
    linear(core, wq, xn, q)
    linear(core, wk, xn, k)
    self_attention(core, "single", q, k, xn, o, KC, D ** -0.5, core.consts["mask_causal"], wv=wv)
    elementwise(core, lambda: core.nc.vector.tensor_tensor(core.x[:, :, :], core.x[:, :, :], o[:, :, :], ALU.add))


def l2_ffn(core, sb, scratch):
    nc = core.nc
    w_up, w_con_t, up_bias, b_con, down_bias = weights(
        core, sb, "L2_ffn", ["W_exp", "W_con_t"], ["up_bias", "b_con", "down_bias"])
    xn, w_down = sb("xn", P, KC, N), sb("w_down", P, 8, D)
    row, hb = sb("row", 1, 4 * D), sb("hb", P, 8)
    d = core.dram
    load(core, (row[:, :], d["L2_ffn_b_exp"]))
    butterfly(core, w_up, row, d["L2_ffn_up_weights"], False)
    butterfly(core, w_con_t, None, d["L2_ffn_down_weights"], True)
    turn_weights(core, w_con_t, w_down, row, hb)
    elementwise(core, lambda: nc.vector.tensor_tensor(hb[:, :], hb[:, :], up_bias[:, :], ALU.add),
                lambda: nc.vector.tensor_tensor(b_con[:, :], b_con[:, :], down_bias[:, :], ALU.add))
    layer_norm(core, core.x, xn)
    mlp(core, xn, w_up, hb, w_down, b_con, core.x)


def l3_xattn(core, sb, scratch):
    nc = core.nc
    wq, wk, wv, bq, bk, bv, betas = weights(core, sb, "L3_xattn", ["Wq", "Wk", "Wv"], ["bq", "bk", "bv", "betas"])
    xn, q, qk, o, phi_w, zero = (sb("xn", P, KC, N), sb("q", P, KC, N), sb("qk", P, KC, N), sb("o", P, KC, N),
                                 sb("phi_w", P, 1), sb("zero", P, 1))
    d = core.dram
    layer_norm(core, core.x, xn)
    linear(core, wq, xn, q, bias=bq)
    elementwise(core, lambda: nc.vector.tensor_scalar(q[:, :, :], q[:, :, :], D ** -0.5, None, ALU.mult),
                lambda: nc.vector.memset(zero[:, :], 0.0),
                lambda: nc.vector.tensor_tensor(phi_w[:, :], betas[:, 0:1], betas[:, 1:2], ALU.add),
                lambda: nc.vector.tensor_tensor(phi_w[:, :], phi_w[:, :], betas[:, 2:3], ALU.subtract))
    linear(core, wk, q, qk)
    cross_single(core, qk, o, d["ctx_t"], d["ctx"], bk, q, zero[:, 0:1], phi=d["fside"], phi_w=phi_w[:, 0:1])
    linear(core, wv, o, core.x, bias=bv, kind="residual")


def l3_attn(core, sb, scratch):
    lb, bq, bk, bv = weights(core, sb, "L3_attn", [], ["l_b", "q_b", "k_b", "v_b"])
    d = core.dram
    wq, wk, wv = (sb(n, P, KC, 512) for n in ("wq", "wk", "wv"))
    wl = sb("wl", P, 4, D)
    xn = sb("xn", P, KC, N)
    layer_norm(core, core.x, xn)
    q, k, v = (sb(n, P, 4, N) for n in ("q", "k", "v"))
    for half in range(2):
        cols = slice(half * 512, (half + 1) * 512)
        load(core, *[(t[:, :, :], chunks(d[f"L3_attn_{n}"][:, cols]))
                     for n, t in (("q_w", wq), ("k_w", wk), ("v_w", wv))],
             (wl[:, :, :], chunks(d["L3_attn_l_w"][cols, :])))
        for w, b, t in ((wq, bq, q), (wk, bk, k), (wv, bv, v)):
            linear(core, w, xn, t, bias=b[:, 4 * half:4 * half + 4], mc=4)
        self_attention(core, "columns", k, q, v, q, 4, 0.125, core.consts["mask_block"])
        linear(core, wl, q, core.x, bias=lb if half == 0 else None, kind="residual", kc=4)


def l3_ffn(core, sb, scratch):
    nc = core.nc
    (wr,) = weights(core, sb, "L3_ffn", ["Wr"])
    d = core.dram
    xn, no_bias = sb("xn", P, KC, N), sb("no_bias", P, 16)
    layer_norm(core, core.x, xn)
    elementwise(core, lambda: nc.vector.memset(no_bias[:, :], 0.0))
    gates(core, xn, wr, no_bias, scratch["gates"], 16, shared=2)
    experts_sum(core, "glu", xn, core.x, scratch["gates"], 18, d["L3_ffn_Wgu"], d["L3_ffn_Wd"], hidden=P)


def shape_constants():
    import numpy as np
    f, r = np.float32, np.arange(128)
    same = r[:, None] // 32 == r[None, :] // 32
    lower = same & (r[:, None] >= r[None, :])
    seg, tok = r // 8, r % 8
    at = tok % 2 * 16 + seg
    own = (tok[:, None] // 2 == tok[None, :] // 2) & (at[:, None] >= at[None, :])
    hide = f(-1e30)
    return {
        "ident": np.eye(128, dtype=f),
        "mask_block": np.where(same, f(0), hide),
        "mask_causal": np.where(lower, f(0), hide),
        "mask_lower": lower.astype(f),
        "mask_segments": np.where(own, f(0), hide),
        "head_of_8": (r[:, None] // 16 == np.arange(8)[None, :]).astype(f),
        "head_of_2": (r[:, None] // 64 == np.arange(2)[None, :]).astype(f),
        "own_head": (r[:, None] // 32 == np.arange(64)[None, :] // 16).astype(f),
        "query_sel": (r[:, None] % 32 == np.arange(32)[None, :]).astype(f),
        "same_head": (r[:, None] // 16 == r[None, :] // 16).astype(f) / 16,
        "iota16": np.tile(np.arange(16, dtype=f), (128, 1)),
        "ones": np.ones((128, 128), f),
        "positions": (r[:, None] % 32 - np.arange(257)[None, :]).astype(f),
    }


def laid_out(inputs):
    import numpy as np
    a = {k: np.asarray(v) for k, v in inputs.items()}

    def vec(b):
        return b.reshape(-1, 128).T

    def heads_cols(w):
        return w.reshape(-1, 16, 16).transpose(0, 2, 1).reshape(-1, 256)

    out = {"x": a["x"].reshape(2048, 256).T, "ctx": a["ctx_1024"], "ctx_t": a["ctx_1024"].transpose(0, 2, 1),
           "fside": a["fside_BxSxS2_0"].reshape(2048, 257),
           "mask": a["mask_Bx1xS2x1_bk0"].reshape(64, 1, 257)}
    n = "L0_xattn_"
    for w in ("q1W", "w1W", "q2W", "w2W"):
        out[n + w] = heads_cols(a[n + w])
    for w in ("o1W", "o2W"):
        out[n + w] = heads_cols(a[n + w].T).T
    for w in ("ffW1", "ffW2"):
        out[n + w] = a[n + w]
    for b in ("ffb1", "ffb2", "g1", "b1", "g2", "b2", "g3", "b3"):
        out[n + b] = vec(a[n + b])
    n = "L0_attn_"
    parts = a[n + "W_qkv"].reshape(256, 16, 3, 16).transpose(0, 2, 1, 3).reshape(256, 768)
    out[n + "W_qkv"] = parts
    out[n + "b_qkv"] = vec(a[n + "b_qkv"].reshape(16, 3, 16).transpose(1, 0, 2).reshape(768))
    out[n + "W_out"], out[n + "b_out"] = a[n + "W_out"], vec(a[n + "b_out"])
    n = "L0_ffn_"
    out[n + "gate_w"], out[n + "gate_b"] = a[n + "gate_w"], a[n + "gate_b"].reshape(1, 8)
    out[n + "w1"], out[n + "w2"] = a[n + "w1"], a[n + "w2"]
    out[n + "b1"] = a[n + "b1"].reshape(8, 4, 128).transpose(0, 2, 1)
    out[n + "b2"] = a[n + "b2"].reshape(8, 2, 128).transpose(0, 2, 1)
    n = "L1_xattn_"
    out[n + "w_q"], out[n + "w_proj"] = a[n + "w_q"], a[n + "w_proj"]
    out[n + "w_k"], out[n + "w_v"] = a[n + "w_kv"][:, :256], a[n + "w_kv"][:, 256:]
    out[n + "w_rel"] = np.repeat(a[n + "w_rel"].reshape(4, 4).T, 32, axis=0)
    n = "L1_attn_"
    out[n + "Wq"], out[n + "Wv"] = a[n + "Wq"].T, a[n + "Wv"].T
    out[n + "q_norm_w"], out[n + "v_norm_w"] = vec(a[n + "q_norm_w"].reshape(-1)), vec(a[n + "v_norm_w"].reshape(-1))
    n = "L1_ffn_"
    for w in ("Wq", "Wk", "Wv", "Wo", "Wg", "We"):
        out[n + w] = a[n + w]
    for b in ("bq", "bk", "bv", "bo", "g1", "be1", "g2", "be2"):
        out[n + b] = vec(a[n + b])
    out[n + "bg"] = a[n + "bg"].reshape(1, 8)
    out[n + "bexp"] = a[n + "bexp"].reshape(8, 2, 128).transpose(0, 2, 1)
    n = "L2_xattn_"
    out[n + "W_qv"], out[n + "w_sim"] = a[n + "W_qv"], vec(a[n + "w_sim"])
    out[n + "b_sim"], out[n + "b_qv"] = a[n + "b_sim"].reshape(1, 1), vec(a[n + "b_qv"])
    n = "L2_attn_"
    for w in ("W_Q", "W_K", "W_V"):
        out[n + w] = a[n + w]
    n = "L2_ffn_"
    out[n + "W_exp"], out[n + "W_con_t"] = a[n + "W_exp"], a[n + "W_con"].T
    out[n + "b_exp"] = a[n + "b_exp"].reshape(1, 1024)
    for w in ("up_weights", "down_weights"):
        out[n + w] = a[n + w].reshape(10, 2048)
    for b in ("up_bias", "b_con", "down_bias"):
        out[n + b] = vec(a[n + b])
    n = "L3_xattn_"
    out[n + "Wq"], out[n + "Wk"], out[n + "Wv"] = a[n + "Wq"].T, a[n + "Wk"], a[n + "Wv"].T
    for b in ("bq", "bk", "bv"):
        out[n + b] = vec(a[n + b])
    out[n + "betas"] = np.stack([a[n + "beta_risk"], a[n + "beta_prio"], a[n + "beta_impl"]]).reshape(1, 3)
    n = "L3_attn_"
    for w in "qkv":
        out[n + w + "_w"] = a[n + w + "_w"].reshape(1024, 256).T
        out[n + w + "_b"] = vec(a[n + w + "_b"].reshape(-1))
    out[n + "l_w"], out[n + "l_b"] = a[n + "l_w"].T, vec(a[n + "l_b"].reshape(-1))
    n = "L3_ffn_"
    out[n + "Wr"] = a[n + "Wr"]
    gate = np.concatenate([a[n + "Wg"], a[n + "Sg"].reshape(256, 2, 128).transpose(1, 0, 2)])
    up = np.concatenate([a[n + "Wu"], a[n + "Su"].reshape(256, 2, 128).transpose(1, 0, 2)])
    out[n + "Wgu"] = np.concatenate([gate, up], axis=2)
    out[n + "Wd"] = np.concatenate([a[n + "Wd"], a[n + "Sd"].reshape(2, 128, 256)])
    return {k: np.ascontiguousarray(v) for k, v in out.items()}


def kernel(**inputs):
    import numpy as np
    import concourse.bacc as bacc
    from concourse.bass_utils import run_bass_kernel_spmd

    arrays = {**laid_out(inputs), **shape_constants()}
    nc = bacc.Bacc("TRN2", target_bir_lowering=False, num_devices=1)
    dram = {k: nc.dram_tensor(f"in_{k}", v.shape, mybir.dt.from_np(v.dtype), kind="ExternalInput").ap()
            for k, v in arrays.items()}
    out = nc.dram_tensor("out_0_dram", (D, N), F32, kind="ExternalOutput").ap()
    scratch = {k: nc.dram_tensor(f"scratch_{k}", shape, F32, kind="Internal").ap()
               for k, shape in {"qkv": (3 * D, N), "seg_out": (D, N), "gates": (18, N)}.items()}
    perceiver(nc, dram, out, scratch)
    r = run_bass_kernel_spmd(nc, [{f"in_{k}": v for k, v in arrays.items()}], core_ids=[0])
    return r.results[0]["out_0_dram"].T.reshape(B, S, D)
```

```python
import concourse.bass as bass
from concourse import mybir
from contextlib import ExitStack, contextmanager

P = 128
D = 256
KC = D // P
B = 64
S = 32
N = B * S
M = 257
BLK = 512
NB = N // BLK
GT = 128
NG = N // GT
KCH = [(0, 128), (128, 128), (256, 1)]
HALF = BLK // 2

START = 1

F32 = mybir.dt.float32
U32 = mybir.dt.uint32
U8 = mybir.dt.uint8
ALU = mybir.AluOpType
ACT = mybir.ActivationFunctionType
AX = mybir.AxisListType.X


CONSTS = ["ident", "mask_block", "mask_causal", "mask_lower", "mask_segments", "head_of_8", "head_of_2",
          "own_head", "query_sel", "same_head",
          "iota16", "ones", "positions"]




class Core:

    BANK = 30

    def __init__(self, nc, ctx, dram):
        self.nc, self.ctx, self.dram = nc, ctx, dram
        self.banks = [[ctx.enter_context(nc.semaphore(f"bank{b}_{i}")) for i in range(self.BANK)]
                      for b in range(2)]
        self.turn = 0
        self.used = [self.BANK, self.BANK]
        with nc.Block(no_gpsimd_drain=True) as block:
            @block.gpsimd
            def _(pool):
                for s in self.banks[0]:
                    pool.sem_inc(s, START)
        self.banks8 = ctx.enter_context(nc.psum_tensor("banks8", [P, 8, BLK], F32))
        self.psum = [self.banks8[:, i, :] for i in range(8)]
        self.x = self.keep("x_T", [P, KC, N])
        self.consts = {name: self.keep(name, list(dram[name].shape)) for name in CONSTS}
        self.ident = self.consts["ident"]
        self.mean_w = self.keep("mean_w", [P, P])
        self.eps = self.keep("eps", [P, 2])

    def keep(self, name, shape, dt=F32):
        return self.ctx.enter_context(self.nc.sbuf_tensor(f"sb_{name}", shape, dt))


@contextmanager
def phase(core, *names):
    nc = core.nc
    assert len(names) <= core.BANK
    bank, old = core.banks[core.turn % 2], core.banks[(core.turn + 1) % 2]
    stale = old if core.turn == 0 else old[:core.used[(core.turn + 1) % 2]]
    core.used[core.turn % 2] = max(len(names), 1)
    with nc.Block(no_gpsimd_drain=True) as block:
        @block.gpsimd
        def _(pool):
            for s in stale:
                if core.turn:
                    pool.sem_clear(s)
                pool.sem_inc(s, START)
        yield (block, *bank[:len(names)])
    core.turn += 1


def bcast(ap, n, at=1):
    a = ap.unsqueeze(at)
    shape = list(a.shape)
    shape[at] = n
    return a.broadcast_to(shape)


def blk(t, width=BLK):
    return bass.ds(t * width, width)


def layer_norm(core, src, dst, scale_shift=None, add=None):
    nc = core.nc
    var_bank = core.psum[2]
    with ExitStack() as mem:
        def sb(name, shape):
            return mem.enter_context(nc.sbuf_tensor(f"{name}_{core.turn}", shape, F32))
        cen, sq, diag = sb("cen", [P, KC, N]), sb("sq", [P, 2, KC, BLK]), sb("diag", [P, 2, 4, P])
        std, rstd = sb("std", [P, NG]), sb("rstd", [P, NG])
        (block, mean_ready, centred, squared, var_ready, std_ready, rstd_ready, diag_ready, spread, scaled,
         done) = mem.enter_context(
            phase(core, "mean_ready", "centred", "squared", "var_ready", "std_ready", "rstd_ready",
                  "diag_ready", "spread", "scaled", "done"))

        @block.tensor
        def _(pe):
            def variance(t):
                pe.wait_ge(squared, START + t + 1)
                for g in range(4):
                    for k in range(KC):
                        ins = pe.matmul(var_bank[:, 4 * t + g:4 * t + g + 1], sq[:, t % 2, k, g * P:(g + 1) * P],
                                        core.mean_w[:, 0:1], start=(k == 0), stop=(k == KC - 1))
                ins.then_inc(var_ready, 1)

            for t in range(NB):
                if t >= 2:
                    pe.wait_ge(centred, START + t - 1)
                for k in range(KC):
                    ins = pe.matmul(core.psum[t % 2], core.mean_w[:, :], src[:, k, blk(t)], start=(k == 0),
                                    stop=(k == KC - 1))
                ins.then_inc(mean_ready, 1)
                if t >= 1:
                    variance(t - 1)
            variance(NB - 1)
            for t in range(NB):
                pe.wait_ge(diag_ready, START + t + 1)
                pe.matmul(core.psum[4 + t], core.consts["ones"][:, :],
                          diag[:, t % 2, :, :].rearrange("p g w -> p (g w)"), start=True, stop=True)\
                  .then_inc(spread, 1)

        @block.scalar
        def _(act):
            for t in range(NB):
                act.wait_ge(centred, START + t + 1)
                if t >= 2:
                    act.wait_ge(var_ready, START + t - 1)
                nc.scalar.activation(sq[:, t % 2, :, :], cen[:, :, blk(t)], ACT.Square).then_inc(squared, 1)
            act.wait_ge(var_ready, START + NB)
            nc.scalar.activation(std[:, :], var_bank[:, 0:NG], ACT.Sqrt, bias=core.eps[:, 0:1])\
              .then_inc(std_ready, 1)
            if scale_shift is not None and add is None:
                for t in range(NB):
                    for k in range(KC):
                        act.wait_ge(scaled, START + t * KC + k + 1)
                        nc.scalar.activation(dst[:, k, blk(t)], cen[:, k, blk(t)], ACT.Identity,
                                             bias=scale_shift[1][:, k:k + 1]).then_inc(done, 1)

        @block.gpsimd
        def _(pool):
            pool.wait_ge(rstd_ready, START + 1)
            for t in range(NB):
                if t >= 2:
                    pool.wait_ge(spread, START + t - 1)
                nc.gpsimd.tensor_tensor(diag[:, t % 2, :, :], bcast(core.ident[:, :], 4),
                                        bcast(rstd[:, 4 * t:4 * t + 4], P, 2), ALU.mult).then_inc(diag_ready, 1)

        @block.vector
        def _(dve):
            for t in range(NB):
                dve.wait_ge(mean_ready, START + t + 1)
                nc.vector.tensor_tensor(cen[:, :, blk(t)], src[:, :, blk(t)], bcast(core.psum[t % 2], KC),
                                        ALU.subtract).then_inc(centred, 1)
            dve.wait_ge(std_ready, START + 1)
            nc.vector.reciprocal(rstd[:, :], std[:, :]).then_inc(rstd_ready, 1)
            dve.wait_ge(centred, START + NB)
            for t in range(NB):
                dve.wait_ge(spread, START + t + 1)
                if scale_shift is None:
                    out = dst if add is None else cen
                    nc.vector.tensor_tensor(out[:, :, blk(t)], cen[:, :, blk(t)], bcast(core.psum[4 + t], KC),
                                            ALU.mult).then_inc(scaled, 1)
                    continue
                g, b = scale_shift
                for k in range(KC):
                    nc.vector.scalar_tensor_tensor(out=cen[:, k, blk(t)], in0=core.psum[4 + t],
                                                   scalar=g[:, k:k + 1], in1=cen[:, k, blk(t)], op0=ALU.mult,
                                                   op1=ALU.mult).then_inc(scaled, 1)
                    if add is not None:
                        dve.wait_ge(scaled, START + t * KC + k + 1)
                        nc.vector.scalar_tensor_tensor(out=dst[:, k, blk(t)], in0=cen[:, k, blk(t)],
                                                       scalar=b[:, k:k + 1], in1=add[:, k, blk(t)], op0=ALU.add,
                                                       op1=ALU.add).then_inc(done, 1)


def linear(core, w, src, dst, bias=None, kind="copy", kc=KC, mc=KC):
    nc = core.nc
    takers = {"copy": 2, "gelu": 1, "residual": 1}[kind]
    unroll = 2 if mc <= 4 else 1
    per = unroll * mc // takers
    with phase(core, "product_ready", "free_act", "free_dve") as (block, ready, free_act, free_dve):
        @block.tensor
        def _(pe):
            with pe.Fori(0, NB // unroll) as r:
                for n in range(unroll * mc):
                    u, m = n // mc, n % mc
                    free = free_act if kind == "gelu" or (takers == 2 and n % 2 == 0) else free_dve
                    pe.wait_ge(free, START + r * per + n // takers + 1)
                    for k in range(kc):
                        ins = pe.matmul(core.psum[n][:, :], w[:, k, m * P:(m + 1) * P],
                                        src[:, k, blk(r * unroll + u)], start=(k == 0), stop=(k == kc - 1))
                    ins.then_inc(ready, 1)

        def take(eng, which, free):
            eng.sem_inc(free, per)
            with eng.Fori(0, NB // unroll) as r:
                for n in range(unroll * mc):
                    u, m = n // mc, n % mc
                    if takers == 2 and n % 2 != which:
                        continue
                    eng.wait_ge(ready, START + r * unroll * mc + n + 1)
                    out, got = dst[:, m, blk(r * unroll + u)], core.psum[n][:, :]
                    b = 0.0 if bias is None else bias[:, m:m + 1]
                    if which == 0:
                        f = ACT.Gelu if kind == "gelu" else ACT.Identity
                        ins = nc.scalar.activation(out, got, f, bias=b)
                    elif kind == "residual":
                        ins = nc.vector.scalar_tensor_tensor(out=out, in0=got, scalar=b, in1=out,
                                                             op0=ALU.add, op1=ALU.add)
                    else:
                        ins = nc.vector.tensor_scalar(out, got, b, None, ALU.add)
                    ins.then_inc(free, 1)

        if kind != "residual":
            @block.scalar
            def _(act):
                take(act, 0, free_act)
        if kind != "gelu":
            @block.vector
            def _(dve):
                take(dve, 1, free_dve)


def start(core):
    nc = core.nc
    with phase(core, "loaded", "set") as (block, loaded, done):
        @block.sync
        def _(sp):
            sp.dma_start(core.x[:, :, :], core.dram["x"].rearrange("(k p) n -> p k n", p=P)).then_inc(loaded, 16)
            for i, (name, tile) in enumerate(core.consts.items()):
                sp.dma_start(tile[:, :], core.dram[name]).then_inc(loaded, 16)
            sp.wait_ge(loaded, START + 16 * (1 + len(core.consts)))

        @block.gpsimd
        def _(pool):
            nc.gpsimd.memset(core.mean_w[:, :], 1.0 / D).then_inc(done, 1)
            nc.gpsimd.memset(core.eps[:, 0:1], 1e-5).then_inc(done, 1)
            nc.gpsimd.memset(core.eps[:, 1:2], 1e-8).then_inc(done, 1)
            pool.wait_ge(done, START + 3)


def load(core, *pairs):
    with phase(core, "loaded") as (block, loaded):
        @block.sync
        def _(sp):
            for tile, source in pairs:
                sp.dma_start(tile, source).then_inc(loaded, 16)
            sp.wait_ge(loaded, START + 16 * len(pairs))


def chunks(ap):
    return ap.rearrange("(k p) n -> p k n", p=P)


def store(core, src, out):
    with phase(core, "stored") as (block, stored):
        @block.sync
        def _(sp):
            sp.dma_start(chunks(out), src[:, :, :]).then_inc(stored, 16)
            sp.wait_ge(stored, START + 16)


def self_attention(core, kind, still, moving, v, out, chunk_n, scale=1.0, mask=None):
    nc = core.nc
    seg = kind == "segments"
    dh = {"heads": 16, "linear": 16, "columns": 64}.get(kind, 0)
    hp = P // dh if dh else 0
    units = 16 if seg else chunk_n * hp
    Q = units // 4
    softmax, turns = kind != "linear", kind != "columns"
    outs = Q if seg else chunk_n
    AHEAD, TOTAL = 3, NG * Q
    with ExitStack() as mem:
        def sb(name, shape):
            return mem.enter_context(nc.sbuf_tensor(f"{name}_{core.turn}", shape, F32))
        if seg:
            q_e, v_e = sb("q_e", [16, 16, GT]), sb("v_e", [16, 16, GT])
            k_e, o_e = ([sb(f"{n}{j}", [16, 16, GT]) for j in range(2)] for n in ("k_e", "o_e"))
            a_st, v_st = ([sb(f"{n}{j}", [16, 16, 16, 8]) for j in range(2)] for n in ("q_rows", "v_cols"))
            v_use = [sb(f"v_rows{j}", [P, 16, 16]) for j in range(2)]
        else:
            a_st = [sb(f"a_pad{j}", [P, units, GT]) for j in range(2)]
            v_st = [sb(f"v_st{j}", [P, chunk_n, GT]) for j in range(2)]
            v_use = [sb(f"v_pad{j}", [P, chunk_n, hp, P + dh]) for j in range(2)]
        s = sb("s", [P, 4, 4, P]) if softmax else None
        p = sb("p", [P, 4, 4, P])
        pt = sb("pt", [P, 2, 4, P]) if turns else None
        top, neg, total, inv = (sb(n, [P, 4, 4]) for n in ("top", "neg", "total", "inv"))
        (block, staged, v_staged, zeroed, v_turned, v_ready, scores_ready, masked, topped, negated, exped,
         inverted, normed, p_turned, pt_ready, out_ready, out_taken, stored0, stored1, arrived, passed) = \
            mem.enter_context(phase(
                core, "staged", "v_staged", "zeroed", "v_turned", "v_ready", "scores_ready", "masked",
                "topped", "negated", "exped", "inverted", "normed", "p_turned", "pt_ready", "out_ready",
                "out_taken", "stored0", "stored1", "arrived", "passed"))
        stored = [stored0, stored1]
        n_staged = 1 if seg else chunk_n
        heads_of = core.consts["head_of_8" if dh == 16 else "head_of_2"]
        normal = masked if kind == "linear" else normed
        v_bank = core.psum[7]

        def rounds(eng, step):
            with eng.Fori(0, NG // 2 - 1) as r:
                for j in range(2):
                    for n in range(Q):
                        step(2 * r + j, j, n, False)
            for j in range(2):
                for n in range(Q):
                    step(NG - 2 + j, j, n, True)

        def ahead(i, j, n, by, last):
            d, n2 = (n + by) // Q, (n + by) % Q
            return None if last and i + d >= NG else (i + d, (j + d) % 2, n2)

        def slot(j, n, of=4):
            return (j * Q + n) % of

        def finished(n):
            return [n] if seg else [c for c in range(chunk_n) if (c + 1) * hp - 1 in range(4 * n, 4 * n + 4)]

        if seg:
            @block.sync
            def _(sp):
                def part(d, g):
                    return d.rearrange("(s e) n -> e s n", e=16)[:, :, blk(g, GT)]

                def fetch(g, j):
                    for tile, d in ((q_e, still), (k_e[j], moving), (v_e, v)):
                        sp.dma_start(tile[:, :, :], part(d, g)).then_inc(arrived, 16)

                def keep(g, j):
                    sp.wait_ge(out_taken, START + (g + 1) * Q)
                    sp.sem_inc(passed, 1)
                    sp.dma_start(part(out, g), o_e[j][:, :, :]).then_inc(stored[j], 16)

                fetch(0, 0)
                sp.wait_ge(staged, START + 1)
                sp.wait_ge(v_staged, START + 1)
                fetch(1, 1)
                with sp.Fori(0, NG // 2 - 1) as r:
                    for j in range(2):
                        g = 2 * r + j
                        sp.wait_ge(staged, START + g + 2)
                        sp.sem_inc(passed, 1)
                        sp.wait_ge(v_staged, START + g + 2)
                        sp.sem_inc(passed, 1)
                        sp.wait_ge(scores_ready, START + (g + 1) * Q)
                        sp.sem_inc(passed, 1)
                        fetch(g + 2, j)
                        keep(g, j)
                for j in range(2):
                    keep(NG - 2 + j, j)
                for j in range(2):
                    sp.wait_ge(stored[j], START + 16 * (NG // 2))

            @block.gpsimd
            def _(pool):
                def stage(g, j):
                    pool.wait_ge(arrived, START + (g + 1) * 48)
                    pool.sem_inc(passed, 1)
                    nc.gpsimd.tensor_copy(a_st[j][:, :, :, :],
                                          q_e[:, :, :].rearrange("e s (u t) -> e u s t", t=8)).then_inc(staged, 1)

                for j in range(2):
                    stage(j, j)
                with pool.Fori(0, NG // 2 - 1) as r:
                    for j in range(2):
                        pool.wait_ge(scores_ready, START + (2 * r + j + 1) * Q)
                        stage(2 * r + j + 2, j)
        else:
            @block.gpsimd
            def _(pool):
                def stage(g, j):
                    nc.gpsimd.tensor_copy(v_st[j][:, :, :], v[:, :, blk(g, GT)]).then_inc(v_staged, 1)
                    for c in range(chunk_n):
                        nc.gpsimd.tensor_tensor(
                            a_st[j][:, c * hp:(c + 1) * hp, :], bcast(still[:, c, blk(g, GT)], hp),
                            bcast(heads_of[:, 0:hp], GT, 2), ALU.mult).then_inc(staged, 1)

                stage(0, 0)
                for j in range(2):
                    nc.gpsimd.memset(v_use[j][:, :, :, :], 0.0).then_inc(zeroed, 1)
                stage(1, 1)
                with pool.Fori(0, NG // 2 - 1) as r:
                    for j in range(2):
                        pool.wait_ge(scores_ready, START + (2 * r + j + 1) * Q)
                        pool.wait_ge(v_turned, START + 2 * r + j + 1)
                        pool.sem_inc(passed, 1)
                        stage(2 * r + j + 2, j)

        @block.tensor
        def _(pe):
            def values(g, j):
                pe.wait_ge(v_staged, START + g + 1)
                pe.wait_ge(v_ready, START + g)
                if seg:
                    for u in range(units):
                        ins = pe.matmul(v_bank[:, u * 16:(u + 1) * 16],
                                        v_st[j][:, u, :, :].rearrange("e s t -> e (s t)"),
                                        core.ident[0:16, 0:16], start=True, stop=True)
                else:
                    for c in range(chunk_n):
                        ins = pe.transpose(v_bank[:, c * P:(c + 1) * P], v_st[j][:, c, :], core.ident[:, :])
                ins.then_inc(v_turned, 1)

            def scores(g, j, n):
                pe.wait_ge(staged, START + (g + 1) * n_staged)
                for u in range(4 * n, 4 * n + 4):
                    to = core.psum[slot(j, n)][:, (u % 4) * P:(u % 4 + 1) * P]
                    if seg:
                        ins = pe.matmul(to, a_st[j][:, u, :, :].rearrange("e s t -> e (s t)"),
                                        k_e[j][:, :, 8 * u:8 * u + 8], start=True, stop=True)
                    else:
                        ins = pe.matmul(to, a_st[j][:, u, :], moving[:, u // hp, blk(g, GT)], start=True,
                                        stop=True)
                ins.then_inc(scores_ready, 1)

            def result(g, j, n, last):
                if turns:
                    pe.wait_ge(pt_ready, START + g * Q + n + 1)
                else:
                    pe.wait_ge(normal, START + g * Q + n + 1)
                if n == 0:
                    pe.wait_ge(v_ready, START + g + 1)
                for u in range(4 * n, 4 * n + 4):
                    pu = pt[:, slot(j, n, 2), u % 4, :] if turns else p[:, slot(j, n), u % 4, :]
                    o = n if seg else u // hp
                    first = u % 4 == 0 if seg else u % hp == 0
                    if first:
                        pe.wait_ge(out_taken, START + g * outs + max(0, o - 1))
                        if o == 1 and not (last and g == NG - 1):
                            pe.wait_ge(v_ready, START + g + 2)
                    if seg:
                        ins = pe.matmul(core.psum[6 + o % 2][0:16, (u % 4) * P:(u % 4 + 1) * P],
                                        v_use[j][:, u, :], pu, start=True, stop=True)
                        done = u % 4 == 3
                    else:
                        h = u % hp
                        at = o * hp * (P + dh) + h * P
                        flat = v_use[j][:, :, :, :].rearrange("p c h w -> p (c h w)")
                        ins = pe.matmul(core.psum[6 + o % 2][:, 0:GT], flat[:, at:at + P], pu, start=(h == 0),
                                        stop=(h == hp - 1))
                        done = h == hp - 1
                    if done:
                        ins.then_inc(out_ready, 1)

            def step(i, j, n, last):
                if turns:
                    pe.wait_ge(normal, START + i * Q + n + 1)
                    for u in range(4):
                        ins = pe.transpose(core.psum[4 + slot(j, n, 2)][:, u * P:(u + 1) * P],
                                           p[:, slot(j, n), u, :], core.ident[:, :])
                    ins.then_inc(p_turned, 1)
                later = ahead(i, j, n, AHEAD, last)
                if later:
                    pe.wait_ge(masked, START + i * Q + n)
                    scores(*later)
                if n == 0 and not (last and i == NG - 1):
                    pe.wait_ge(out_taken, START + i * outs)
                    values(i + 1, 1 - j)
                result(i, j, n, last)

            values(0, 0)
            for m in range(AHEAD):
                scores(m // Q, m // Q % 2, m % Q)
            rounds(pe, step)

        @block.scalar
        def _(act):
            def values(g, j):
                act.wait_ge(v_turned, START + g + 1)
                if seg:
                    ins = nc.scalar.copy(v_use[j][:, :, :], v_bank[:, 0:256].rearrange("p (u e) -> p u e", u=16))
                else:
                    for c in range(chunk_n):
                        ins = nc.scalar.copy(v_use[j][:, c, :, 0:dh],
                                             v_bank[:, c * P:(c + 1) * P].rearrange("p (h f) -> p h f", h=hp))
                ins.then_inc(v_ready, 1)

            def arrange(g, j):
                act.wait_ge(arrived, START + (g + 1) * 48)
                nc.scalar.copy(v_st[j][:, :, :, :], v_e[:, :, :].rearrange("e s (u t) -> e u s t", t=8))\
                  .then_inc(v_staged, 1)

            def exps(g, j, n):
                act.wait_ge(negated, START + g * Q + n + 1)
                sl = slot(j, n)
                for u in range(4):
                    ins = nc.scalar.activation(p[:, sl, u, :], s[:, sl, u, :], ACT.Exp, bias=neg[:, sl, u:u + 1],
                                               scale=scale, accum_out=total[:, sl, u:u + 1])
                ins.then_inc(exped, 1)

            def step(i, j, n, last):
                if turns:
                    act.wait_ge(p_turned, START + i * Q + n + 1)
                    nc.scalar.copy(pt[:, slot(j, n, 2), :, :],
                                   core.psum[4 + slot(j, n, 2)].rearrange("p (u w) -> p u w", u=4))\
                      .then_inc(pt_ready, 1)
                if n == 0 and not (last and i == NG - 1):
                    values(i + 1, 1 - j)
                later = ahead(i, j, n, 2, last)
                if softmax and later:
                    exps(*later)
                if seg and n == 2 and not last:
                    arrange(i + 2, j)

            if seg:
                arrange(0, 0)
            else:
                act.wait_ge(zeroed, START + 2)
            values(0, 0)
            if seg:
                arrange(1, 1)
            if softmax:
                for m in range(2):
                    exps(m // Q, m // Q % 2, m % Q)
            rounds(act, step)

        @block.vector
        def _(dve):
            def mask_quad(g, j, n):
                dve.wait_ge(scores_ready, START + g * Q + n + 1)
                sl = slot(j, n)
                sc = core.psum[sl].rearrange("p (u w) -> p u w", u=4)
                if not softmax:
                    nc.vector.tensor_tensor(p[:, sl, :, :], sc, bcast(mask[:, :], 4), ALU.mult)\
                      .then_inc(masked, 1)
                    return
                nc.vector.tensor_tensor(s[:, sl, :, :], sc, bcast(mask[:, :], 4), ALU.add).then_inc(masked, 1)
                dve.wait_ge(masked, START + g * Q + n + 1)
                nc.vector.tensor_reduce(top[:, sl, :], s[:, sl, :, :], AX, ALU.max).then_inc(topped, 1)
                dve.wait_ge(topped, START + g * Q + n + 1)
                nc.vector.tensor_scalar(neg[:, sl, :], top[:, sl, :], -scale, None, ALU.mult)\
                  .then_inc(negated, 1)

            def norm(g, j, n):
                sl = slot(j, n)
                dve.wait_ge(exped, START + g * Q + n + 1)
                nc.vector.reciprocal(inv[:, sl, :], total[:, sl, :]).then_inc(inverted, 1)
                dve.wait_ge(inverted, START + g * Q + n + 1)
                nc.vector.tensor_tensor(p[:, sl, :, :], p[:, sl, :, :], bcast(inv[:, sl, :], P, 2), ALU.mult)\
                  .then_inc(normed, 1)

            def take(g, j, o):
                dve.wait_ge(out_ready, START + g * outs + o + 1)
                bank = core.psum[6 + o % 2]
                if seg:
                    if o == 0:
                        dve.wait_ge(stored[j], START + (g - j) * 8)
                    nc.vector.tensor_copy(
                        o_e[j][:, :, 32 * o:32 * o + 32].rearrange("e s (u t) -> e u s t", u=4),
                        bank[0:16, :].rearrange("e (u s t) -> e u s t", u=4, t=8)).then_inc(out_taken, 1)
                else:
                    nc.vector.tensor_copy(out[:, o, blk(g, GT)], bank[:, 0:GT]).then_inc(out_taken, 1)

            def step(i, j, n, last):
                later = ahead(i, j, n, 2, last)
                if later:
                    mask_quad(*later)
                later = ahead(i, j, n, 1, last)
                if softmax and later:
                    norm(*later)
                for o in finished(n):
                    take(i, j, o)

            for m in range(2):
                mask_quad(m // Q, m // Q % 2, m % Q)
            if softmax:
                norm(0, 0, 0)
            rounds(dve, step)


def single_attention_old(core, kind, still, moving, v, out, chunk_n, scale=1.0, mask=None, wv=None):
    nc = core.nc
    seg, single = kind == "segments", kind == "single"
    dh = {"heads": 16, "linear": 16, "columns": 64}.get(kind, 0)
    hp = P // dh if dh else 0
    units = 16 if seg else 4 if single else chunk_n * hp
    quads = units // 4
    iters = NB if single else NG
    rows = BLK if single else GT
    softmax, turns = kind != "linear", kind != "columns"
    outs = chunk_n if dh else quads
    with ExitStack() as mem:
        def sb(name, shape):
            return mem.enter_context(nc.sbuf_tensor(f"{name}_{core.turn}", shape, F32))
        if seg:
            q_e, b_st, v_e, o_st = (sb(n, [16, 16, GT]) for n in ("q_e", "k_e", "v_e", "o_e"))
            a_st, v_st = (sb(n, [16, 16, 16, 8]) for n in ("q_rows", "v_cols"))
            v_use = sb("v_rows", [P, 16, 16])
        elif single:
            a_st, v_st = sb("a_st", [P, KC, BLK]), sb("v_st", [P, KC, BLK])
            v_use = sb("v_tok", [P, 4, D])
        else:
            a_st = sb("a_pad", [P, units, GT])
            v_st = sb("v_st", [P, chunk_n, GT])
            v_use = sb("v_pad", [P, chunk_n, hp, P + dh])
            v_flat = v_use[:, :, :, :].rearrange("p c h w -> p (c h w)")
        s = sb("s", [P, 2, 4, P])
        p = sb("p", [P, 2, 4, P])
        pt = sb("pt", [P, 2, 4, P]) if turns else p
        top, neg, total, inv = (sb(n, [P, 2, 4]) for n in ("top", "neg", "total", "inv"))
        (block, staged, v_turned, v_ready, scores_ready, masked, topped, negated, exped, inverted,
         normed, p_turned, pt_ready, out_ready, out_taken, stored, arrived, passed) = mem.enter_context(
            phase(core, "staged", "v_turned", "v_ready", "scores_ready", "masked", "topped", "negated",
                  "exped", "inverted", "normed", "p_turned", "pt_ready", "out_ready", "out_taken", "stored", "arrived",
                  "passed"))
        n_staged = 2 if seg else 2 if single else chunk_n + 1
        heads_of = core.consts["head_of_8" if dh == 16 else "head_of_2"]

        def scores_bank(n):
            return core.psum[n % 2]

        def turned_bank(n):
            return core.psum[2 + n % 2]

        v_bank = core.psum[4]

        def out_bank(o):
            return core.psum[5 + o % 2] if not single else core.psum[5 + o]

        if seg:
            q_d, k_d, v_d, o_d = still, moving, v, out

            @block.sync
            def _(sp):
                def part(d, i):
                    return d.rearrange("(s e) n -> e s n", e=16)[:, :, blk(i, GT)]

                with sp.Fori(0, iters) as i:
                    sp.wait_ge(scores_ready, START + i * quads)
                    sp.sem_inc(passed, 1)
                    sp.wait_ge(v_turned, START + i)
                    sp.sem_inc(passed, 1)
                    for tile, d in ((q_e, q_d), (b_st, k_d), (v_e, v_d)):
                        sp.dma_start(tile[:, :, :], part(d, i)).then_inc(arrived, 16)
                    sp.wait_ge(out_taken, START + (i + 1) * quads)
                    sp.sem_inc(passed, 1)
                    sp.dma_start(part(o_d, i), o_st[:, :, :]).then_inc(stored, 16)
                sp.wait_ge(stored, START + 16 * iters)

            @block.gpsimd
            def _(pool):
                with pool.Fori(0, iters) as i:
                    pool.wait_ge(arrived, START + (i + 1) * 48)
                    pool.wait_ge(v_turned, START + i)
                    pool.wait_ge(scores_ready, START + i * quads)
                    pool.sem_inc(passed, 1)
                    for rows_of, e in ((v_st, v_e), (a_st, q_e)):
                        nc.gpsimd.tensor_copy(rows_of[:, :, :, :],
                                              e[:, :, :].rearrange("e s (u t) -> e u s t", t=8)).then_inc(staged, 1)
        else:
            @block.gpsimd
            def _(pool):
                if not single:
                    nc.gpsimd.memset(v_use[:, :, :, :], 0.0).then_inc(stored, 1)
                with pool.Fori(0, iters) as i:
                    pool.wait_ge(v_turned, START + i)
                    pool.sem_inc(passed, 1)
                    nc.gpsimd.tensor_copy(v_st[:, :, :], v[:, :, blk(i, rows)]).then_inc(staged, 1)
                    pool.wait_ge(scores_ready, START + i * quads)
                    pool.sem_inc(passed, 1)
                    if single:
                        nc.gpsimd.tensor_copy(a_st[:, :, :], still[:, :, blk(i, rows)]).then_inc(staged, 1)
                    else:
                        for c in range(chunk_n):
                            nc.gpsimd.tensor_tensor(
                                a_st[:, c * hp:(c + 1) * hp, :], bcast(still[:, c, blk(i, rows)], hp),
                                bcast(heads_of[:, 0:hp], GT, 2), ALU.mult).then_inc(staged, 1)

        @block.tensor
        def _(pe):
            def values(i):
                pe.wait_ge(staged, START + i * n_staged + 1)
                pe.wait_ge(v_ready, START + i)
                if seg:
                    for u in range(units):
                        ins = pe.matmul(v_bank[:, u * 16:(u + 1) * 16],
                                        v_st[:, u, :, :].rearrange("e s t -> e (s t)"), core.ident[0:16, 0:16],
                                        start=True, stop=True)
                elif single:
                    for u in range(units):
                        vb = core.psum[4 + 3 * (u // 2)][:, (u % 2) * D:(u % 2 + 1) * D]
                        for k in range(KC):
                            ins = pe.matmul(vb, v_st[:, k, u * P:(u + 1) * P], wv[:, k, :], start=(k == 0),
                                            stop=(k == KC - 1))
                else:
                    for c in range(chunk_n):
                        ins = pe.transpose(v_bank[:, c * P:(c + 1) * P], v_st[:, c, :], core.ident[:, :])
                ins.then_inc(v_turned, 1)

            def scores(i, n):
                pe.wait_ge(staged, START + (i + 1) * n_staged)
                if n >= 2:
                    pe.wait_ge(masked, START + i * quads + n - 1)
                else:
                    pe.wait_ge(masked, START + i * quads)
                for u in range(4 * n, 4 * n + 4):
                    to = scores_bank(n)[:, (u % 4) * P:(u % 4 + 1) * P]
                    if seg:
                        ins = pe.matmul(to, a_st[:, u, :, :].rearrange("e s t -> e (s t)"), b_st[:, :, 8 * u:8 * u + 8],
                                        start=True, stop=True)
                    elif single:
                        for k in range(KC):
                            ins = pe.matmul(to, a_st[:, k, u * P:(u + 1) * P],
                                            moving[:, k, bass.ds(i * BLK + u * P, P)], start=(k == 0),
                                            stop=(k == KC - 1))
                    else:
                        ins = pe.matmul(to, a_st[:, u, :], moving[:, u // hp, blk(i, GT)], start=True,
                                        stop=True)
                ins.then_inc(scores_ready, 1)

            def turn(i, n):
                pe.wait_ge(normed, START + i * quads + n + 1)
                if n >= 2:
                    pe.wait_ge(pt_ready, START + i * quads + n - 1)
                else:
                    pe.wait_ge(pt_ready, START + i * quads)
                for u in range(4):
                    ins = pe.transpose(turned_bank(n)[:, u * P:(u + 1) * P], p[:, n % 2, u, :], core.ident[:, :])
                ins.then_inc(p_turned, 1)

            def result(i, n):
                if turns:
                    pe.wait_ge(pt_ready, START + i * quads + n + 1)
                else:
                    pe.wait_ge(normed, START + i * quads + n + 1)
                if n == 0:
                    pe.wait_ge(v_ready, START + i + 1)
                for u in range(4 * n, 4 * n + 4):
                    pu = pt[:, n % 2, u % 4, :]
                    if seg:
                        if u % 4 == 0:
                            pe.wait_ge(out_taken, START + i * quads + max(0, n - 1))
                        ins = pe.matmul(out_bank(n)[0:16, (u % 4) * P:(u % 4 + 1) * P], v_use[:, u, :], pu,
                                        start=True, stop=True)
                        if u % 4 == 3:
                            ins.then_inc(out_ready, 1)
                    elif single:
                        if u == 0:
                            pe.wait_ge(out_taken, START + i)
                        for c in range(KC):
                            ins = pe.matmul(out_bank(c)[:, u * P:(u + 1) * P], v_use[:, u, c * P:(c + 1) * P],
                                            pu, start=True, stop=True)
                        if u == 3:
                            ins.then_inc(out_ready, 1)
                    else:
                        c, h = u // hp, u % hp
                        if h == 0:
                            pe.wait_ge(out_taken, START + i * outs + max(0, c - 1))
                        at = c * hp * (P + dh) + h * P
                        ins = pe.matmul(out_bank(c)[:, 0:GT], v_flat[:, at:at + P], pu, start=(h == 0),
                                        stop=(h == hp - 1))
                        if h == hp - 1:
                            ins.then_inc(out_ready, 1)

            with pe.Fori(0, iters) as i:
                values(i)
                scores(i, 0)
                for n in range(quads):
                    if n + 1 < quads:
                        scores(i, n + 1)
                    if turns:
                        turn(i, n)
                    if n >= 1:
                        result(i, n - 1)
                result(i, quads - 1)

        @block.scalar
        def _(act):
            if not (seg or single):
                act.wait_ge(stored, START + 1)

            def exps(i, n):
                act.wait_ge(negated, START + i * quads + n + 1)
                if turns:
                    act.wait_ge(p_turned, START + i * quads + max(0, n - 1))
                else:
                    act.wait_ge(out_ready, START + i * outs + max(0, n - 1) * (4 // hp))
                for u in range(4):
                    ins = nc.scalar.activation(p[:, n % 2, u, :], s[:, n % 2, u, :], ACT.Exp,
                                               bias=neg[:, n % 2, u:u + 1], scale=scale,
                                               accum_out=total[:, n % 2, u:u + 1])
                ins.then_inc(exped, 1)

            def turned(i, n):
                act.wait_ge(p_turned, START + i * quads + n + 1)
                if seg or single:
                    act.wait_ge(out_ready, START + i * outs + max(0, n - 1))
                else:
                    act.wait_ge(out_ready, START + i * outs + max(0, n - 1) // 2)
                nc.scalar.copy(pt[:, n % 2, :, :], turned_bank(n).rearrange("p (u w) -> p u w", u=4))\
                  .then_inc(pt_ready, 1)

            with act.Fori(0, iters) as i:
                act.wait_ge(v_turned, START + i + 1)
                act.wait_ge(out_ready, START + (i * outs if not single else i))
                if seg:
                    ins = nc.scalar.copy(v_use[:, :, :], v_bank[:, 0:256].rearrange("p (u e) -> p u e", u=16))
                elif single:
                    for half in range(2):
                        ins = nc.scalar.copy(v_use[:, 2 * half:2 * half + 2, :],
                                             core.psum[4 + 3 * half].rearrange("p (u f) -> p u f", u=2))
                else:
                    for c in range(chunk_n):
                        ins = nc.scalar.copy(v_use[:, c, :, 0:dh],
                                             v_bank[:, c * P:(c + 1) * P].rearrange("p (h f) -> p h f", h=hp))
                ins.then_inc(v_ready, 1)
                for n in range(quads):
                    if softmax:
                        exps(i, n)
                    if turns and n >= 1:
                        turned(i, n - 1)
                if turns:
                    turned(i, quads - 1)

        @block.vector
        def _(dve):
            def mask_quad(i, n):
                dve.wait_ge(scores_ready, START + i * quads + n + 1)
                sc = scores_bank(n).rearrange("p (u w) -> p u w", u=4)
                if not softmax:
                    dve.wait_ge(p_turned, START + i * quads + max(0, n - 1))
                    nc.vector.tensor_tensor(p[:, n % 2, :, :], sc, bcast(mask[:, :], 4), ALU.mult)\
                      .then_inc(masked, 1)
                    dve.wait_ge(masked, START + i * quads + n + 1)
                    dve.sem_inc(normed, 1)
                    return
                dve.wait_ge(exped, START + i * quads + max(0, n - 1))
                nc.vector.tensor_tensor(s[:, n % 2, :, :], sc, bcast(mask[:, :], 4), ALU.add).then_inc(masked, 1)
                dve.wait_ge(masked, START + i * quads + n + 1)
                nc.vector.tensor_reduce(top[:, n % 2, :], s[:, n % 2, :, :], AX, ALU.max).then_inc(topped, 1)
                dve.wait_ge(topped, START + i * quads + n + 1)
                nc.vector.tensor_scalar(neg[:, n % 2, :], top[:, n % 2, :], -scale, None, ALU.mult)\
                  .then_inc(negated, 1)

            def norm(i, n):
                dve.wait_ge(exped, START + i * quads + n + 1)
                nc.vector.reciprocal(inv[:, n % 2, :], total[:, n % 2, :]).then_inc(inverted, 1)
                dve.wait_ge(inverted, START + i * quads + n + 1)
                nc.vector.tensor_tensor(p[:, n % 2, :, :], p[:, n % 2, :, :], bcast(inv[:, n % 2, :], P, 2),
                                        ALU.mult).then_inc(normed, 1)

            def take(i, o):
                if single:
                    dve.wait_ge(out_ready, START + i + 1)
                    nc.vector.tensor_copy(out[:, :, blk(i)], core.banks8[:, 5:7, :]).then_inc(out_taken, 1)
                    return
                dve.wait_ge(out_ready, START + i * outs + o + 1)
                if seg:
                    dve.wait_ge(stored, START + 16 * i)
                    nc.vector.tensor_copy(
                        o_st[:, :, 32 * o:32 * o + 32].rearrange("e s (u t) -> e u s t", u=4),
                        out_bank(o)[0:16, :].rearrange("e (u s t) -> e u s t", u=4, t=8)).then_inc(out_taken, 1)
                else:
                    nc.vector.tensor_copy(out[:, o, blk(i, GT)], out_bank(o)[:, 0:GT]).then_inc(out_taken, 1)

            with dve.Fori(0, iters) as i:
                taken = 0
                for n in range(quads + 2):
                    if n < quads:
                        mask_quad(i, n)
                    if softmax and 1 <= n <= quads:
                        norm(i, n - 1)
                    while n >= 2 and not single and (taken + 1) * (1 if seg else hp) <= (n - 1) * (1 if seg else 4):
                        take(i, taken)
                        taken += 1
                if single:
                    take(i, 0)
                else:
                    assert taken == outs


def tail_values(core, wv, tails):
    nc = core.nc
    with ExitStack() as mem:
        last = mem.enter_context(nc.sbuf_tensor(f"last_{core.turn}", [P, KC, B], F32))
        v = mem.enter_context(nc.sbuf_tensor(f"v_last_{core.turn}", [B, D], F32))
        block, loaded, made, taken, kept = mem.enter_context(phase(core, "loaded", "made", "taken", "kept"))

        @block.sync
        def _(sp):
            sp.dma_start(last[:, :, :], chunks(core.dram["ctx_last_t"])).then_inc(loaded, 16)
            sp.wait_ge(taken, START + 1)
            sp.dma_start(tails, v[:, :]).then_inc(kept, 16)
            sp.wait_ge(kept, START + 16)

        @block.tensor
        def _(pe):
            pe.wait_ge(loaded, START + 16)
            for k in range(KC):
                ins = pe.matmul(core.psum[0][0:B, 0:D], last[:, k, :], wv[:, k, :], start=(k == 0),
                                stop=(k == KC - 1))
            ins.then_inc(made, 1)

        @block.vector
        def _(dve):
            dve.wait_ge(made, START + 1)
            nc.vector.tensor_copy(v[:, :], core.psum[0][0:B, 0:D]).then_inc(taken, 1)


def cross_attention(core, q, wk, wv, out, ctx_t, tails, mask=None, rel=None):
    nc = core.nc
    SC = 0.25
    masked = mask is not None
    with ExitStack() as mem:
        def sb(name, shape, dt=F32):
            return mem.enter_context(nc.sbuf_tensor(f"{name}_{core.turn}", shape, dt))
        ctx_sb = [sb(f"ctx{j}", [P, KC, M]) for j in range(2)]
        q_pad = [sb(f"q_pad{j}", [P, 16, S]) for j in range(2)]
        k_t = [sb(f"k_t{j}", [P, KC, M]) for j in range(2)]
        if masked:
            hide8 = [sb(f"hide8{j}", [P, M], U8) for j in range(2)]
            show = [sb(f"show{j}", [P, M]) for j in range(2)]
            hidden = [sb(f"hidden{j}", [P, M]) for j in range(2)]
            k_show = [sb(f"k_show{j}", [P, KC, M]) for j in range(2)]
        else:
            k_show = k_t
        v_tok = [sb(f"v_tok{j}", [P, 2, D]) for j in range(2)]
        v_last = [sb(f"v_last{j}", [P, D]) for j in range(2)]
        p_last = sb("p_last", [P, 4])
        s, p = sb("s", [P, 4, M]), sb("p", [P, 4, M])
        pt = sb("pt", [P, 2, 4 * P])
        last_part, own_inv, whole, om = (sb(n, [P, 4, 64]) for n in ("last_part", "own_inv", "whole", "om"))
        top, neg, total, inv = (sb(n, [P, 4]) for n in ("top", "neg", "total", "inv"))
        (block, loaded0, loaded1, tail0, tail1, padded, shown, k_made, v_made, k_ready, v_ready,
         scores_ready, biased, topped, negated, exped, inverted, p_turned, pt_act, pt_dve, result_ready,
         prepared, added, owned, out_made, out_taken, passed) = mem.enter_context(
            phase(core, "loaded0", "loaded1", "tail0", "tail1", "padded", "shown", "k_made", "v_made",
                  "k_ready", "v_ready", "scores_ready", "biased", "topped", "negated", "exped", "inverted",
                  "p_turned", "pt_act", "pt_dve", "result_ready", "prepared", "added", "owned", "out_made", "out_taken", "passed"))
        arrived, tail_in = [loaded0, loaded1], [tail0, tail1]
        loads = 32 if masked else 16
        banks = core.banks8
        halves = ((0, 2), (2, 4))

        def loop(eng, batch):
            with eng.Fori(0, B // 2 - 1) as r:
                for j in range(2):
                    batch(2 * r + j, j, 2)
            batch(B - 2, 0, 1)
            batch(B - 1, 1, 0)

        def of_parity(b, j, count):
            return START + (b - j) * (count // 2) + count

        @block.sync
        def _(sp):
            def fetch(b, j):
                sp.dma_start(ctx_sb[j][:, :, :], ctx_t[b, :, :].rearrange("(k p) m -> p k m", p=P))\
                  .then_inc(arrived[j], 16)
                if masked:
                    sp.dma_start(hide8[j][:, :], mask[b, :, :].broadcast_to([P, M])).then_inc(arrived[j], 16)

            def fetch_tail(b, j):
                sp.dma_start(v_last[j][:, :], tails[bass.ds(b, 1), :].broadcast_to([P, D])).then_inc(tail_in[j], 16)

            for j in range(2):
                fetch(j, j)
                fetch_tail(j, j)
            with sp.Fori(0, B // 2 - 1) as r:
                for j in range(2):
                    sp.wait_ge(k_made, START + 2 * r + j + 1)
                    sp.sem_inc(passed, 1)
                    if masked:
                        sp.wait_ge(shown, START + (2 * r + j + 1) * 3)
                    else:
                        sp.wait_ge(v_made, START + 2 * r + j + 1)
                    sp.sem_inc(passed, 1)
                    fetch(2 * r + j + 2, j)
                    sp.wait_ge(prepared, START + (2 * r + j + 1) * 2)
                    sp.sem_inc(passed, 1)
                    fetch_tail(2 * r + j + 2, j)

        @block.gpsimd
        def _(pool):
            def pad(b, j):
                for c in range(KC):
                    nc.gpsimd.tensor_tensor(q_pad[j][:, c * 8:c * 8 + 8, :], bcast(q[:, c, blk(b, S)], 8),
                                            bcast(core.consts["head_of_8"][:, :], S, 2), ALU.mult)\
                      .then_inc(padded, 1)

            def hide(b, j):
                pool.wait_ge(arrived[j], of_parity(b, j, loads))
                pool.sem_inc(passed, 1)
                nc.gpsimd.tensor_scalar(show[j][:, :], hide8[j][:, :], -1.0, 1.0, ALU.mult, ALU.add)\
                  .then_inc(shown, 1)
                nc.gpsimd.tensor_scalar(hidden[j][:, :], hide8[j][:, :], -1e9, None, ALU.mult)\
                  .then_inc(shown, 1)
                pool.wait_ge(k_ready, START + b + 1)
                pool.sem_inc(passed, 1)
                pool.wait_ge(shown, START + b * 3 + 2)
                nc.gpsimd.tensor_tensor(k_show[j][:, :, :], k_t[j][:, :, :], bcast(show[j][:, :], KC), ALU.mult)\
                  .then_inc(shown, 1)

            def prepare(b, j):
                pool.wait_ge(inverted, START + 2 * b + 2)
                pool.wait_ge(tail_in[j], of_parity(b, j, 16))
                pool.wait_ge(owned, START + b)
                nc.gpsimd.tensor_tensor(last_part[:, :, :], v_last[j][:, :].rearrange("p (n f) -> p n f", n=4),
                                        bcast(p_last[:, :], 64, 2), ALU.mult).then_inc(prepared, 1)
                nc.gpsimd.tensor_tensor(own_inv[:, :, :], bcast(core.consts["own_head"][:, :], 4),
                                        bcast(inv[:, :], 64, 2), ALU.mult).then_inc(prepared, 1)

            def batch(b, j, ahead):
                prepare(b, j)
                if ahead == 2:
                    pool.wait_ge(biased, START + 2 * b + 2)
                    pad(b + 2, j)
                    if masked:
                        hide(b + 2, j)

            for j in range(2):
                pad(j, j)
                if masked:
                    hide(j, j)
            loop(pool, batch)

        @block.tensor
        def _(pe):
            def keys(b, j):
                pe.wait_ge(arrived[j], of_parity(b, j, loads))
                for m in range(KC):
                    for k in range(KC):
                        ins = pe.matmul(banks[:, 4 + m, 0:M], wk[:, k, m * P:(m + 1) * P], ctx_sb[j][:, k, :],
                                        start=(k == 0), stop=(k == KC - 1))
                ins.then_inc(k_made, 1)

            def values(b, j):
                pe.wait_ge(v_ready, START + b)
                if masked:
                    pe.wait_ge(k_ready, START + b + 1)
                    for c in range(2):
                        for f in range(KC):
                            ins = pe.transpose(banks[:, 6, c * D + f * P:c * D + (f + 1) * P],
                                               k_t[j][:, f, c * P:(c + 1) * P], core.ident[:, :])
                else:
                    for c in range(2):
                        for k in range(KC):
                            ins = pe.matmul(banks[:, 6, c * D:(c + 1) * D], ctx_sb[j][:, k, c * P:(c + 1) * P],
                                            wv[:, k, :], start=(k == 0), stop=(k == KC - 1))
                ins.then_inc(v_made, 1)

            def scores(b, j):
                pe.wait_ge(padded, START + 2 * b + 2)
                if masked:
                    pe.wait_ge(shown, START + 3 * b + 3)
                else:
                    pe.wait_ge(k_ready, START + b + 1)
                pe.wait_ge(biased, START + 2 * b)
                for n in range(4):
                    ins = pe.matmul(banks[:, n, 0:M],
                                    q_pad[j][:, 4 * n:4 * n + 4, :].rearrange("p h s -> p (h s)"),
                                    k_show[j][:, n // 2, :], start=True, stop=True)
                    ins.then_inc(scores_ready, 1)

            def turn(b, ahead):
                pe.wait_ge(exped, START + b + 1)
                pe.wait_ge(k_ready, START + b + 1 + min(ahead, 1))
                for c in range(2):
                    for n in range(4):
                        ins = pe.transpose(banks[:, 4 + c, n * P:(n + 1) * P], p[:, n, c * P:(c + 1) * P],
                                           core.ident[:, :])
                ins.then_inc(p_turned, 1)

            def results(b, j):
                pe.wait_ge(pt_act, START + b + 1)
                pe.wait_ge(pt_dve, START + b + 1)
                pe.wait_ge(out_taken, START + b)
                pe.wait_ge(v_ready, START + b + 1)
                for n in range(4):
                    for c in range(2):
                        ins = pe.matmul(banks[:, 7, n * 64:(n + 1) * 64], pt[:, c, n * P:(n + 1) * P],
                                        v_tok[j][:, c, n * 64:(n + 1) * 64], start=(c == 0), stop=(c == 1))
                ins.then_inc(result_ready, 1)

            def output(b):
                pe.wait_ge(owned, START + b + 1)
                for c in range(KC):
                    ins = pe.matmul(banks[:, 7, 256 + c * S:256 + (c + 1) * S],
                                    om[:, 2 * c:2 * c + 2, :].rearrange("p n f -> p (n f)"),
                                    core.consts["query_sel"][:, :], start=True, stop=True)
                ins.then_inc(out_made, 1)

            def batch(b, j, ahead):
                turn(b, ahead)
                if ahead >= 1:
                    scores(b + 1, 1 - j)
                results(b, j)
                if ahead == 2:
                    keys(b + 2, j)
                output(b)
                if masked and ahead >= 1:
                    values(b + 1, 1 - j)
                elif ahead == 2:
                    values(b + 2, j)

            keys(0, 0)
            values(0, 0)
            scores(0, 0)
            pe.wait_ge(k_ready, START + 1)
            pe.wait_ge(v_ready, START + 1)
            keys(1, 1)
            if not masked:
                values(1, 1)
            loop(pe, batch)

        @block.scalar
        def _(act):
            def keys(b, j):
                act.wait_ge(k_made, START + b + 1)
                nc.scalar.copy(k_t[j][:, :, :], banks[:, 4:6, 0:M]).then_inc(k_ready, 1)

            def exps(b):
                act.wait_ge(p_turned, START + b)
                act.wait_ge(inverted, START + 2 * b)
                for h, (n0, n1) in enumerate(halves):
                    act.wait_ge(negated, START + 2 * b + h + 1)
                    for n in range(n0, n1):
                        ins = nc.scalar.activation(p[:, n, :], s[:, n, :], ACT.Exp, bias=neg[:, n:n + 1],
                                                   scale=SC if rel is None else 1.0, accum_out=total[:, n:n + 1])
                ins.then_inc(exped, 1)

            def batch(b, j, ahead):
                act.wait_ge(p_turned, START + b + 1)
                act.wait_ge(result_ready, START + b)
                nc.scalar.copy(pt[:, 0, :], banks[:, 4, :]).then_inc(pt_act, 1)
                if ahead >= 1:
                    exps(b + 1)
                if ahead == 2:
                    keys(b + 2, j)
                if masked and ahead >= 1:
                    values(b + 1, 1 - j)
                elif ahead == 2:
                    values(b + 2, j)

            def values(b, j):
                act.wait_ge(v_made, START + b + 1)
                nc.scalar.copy(v_tok[j][:, :, :], banks[:, 6, :].rearrange("p (c f) -> p c f", c=2))\
                  .then_inc(v_ready, 1)

            keys(0, 0)
            values(0, 0)
            exps(0)
            keys(1, 1)
            if not masked:
                values(1, 1)
            loop(act, batch)

        @block.vector
        def _(dve):
            def softmax(b, j, h):
                n0, n1 = halves[h]
                dve.wait_ge(scores_ready, START + b * 4 + n1)
                dve.wait_ge(exped, START + b)
                if masked:
                    nc.vector.tensor_tensor(s[:, n0:n1, :], banks[:, n0:n1, 0:M], bcast(hidden[j][:, :], 2),
                                            ALU.add).then_inc(biased, 1)
                else:
                    nc.vector.scalar_tensor_tensor(out=s[:, n0:n1, :], in0=banks[:, n0:n1, 0:M], scalar=SC,
                                                   in1=rel[:, n0:n1, :], op0=ALU.mult, op1=ALU.add)\
                      .then_inc(biased, 1)
                dve.wait_ge(biased, START + 2 * b + h + 1)
                nc.vector.tensor_reduce(top[:, n0:n1], s[:, n0:n1, :], AX, ALU.max).then_inc(topped, 1)
                dve.wait_ge(topped, START + 2 * b + h + 1)
                nc.vector.tensor_scalar(neg[:, n0:n1], top[:, n0:n1], -SC if rel is None else -1.0, None,
                                        ALU.mult).then_inc(negated, 1)

            def own(b):
                dve.wait_ge(prepared, START + 2 * b + 2)
                dve.wait_ge(result_ready, START + b + 1)
                nc.vector.tensor_tensor(whole[:, :, :], banks[:, 7, 0:D].rearrange("p (n f) -> p n f", n=4),
                                        last_part[:, :, :], ALU.add).then_inc(added, 1)
                dve.wait_ge(added, START + b + 1)
                nc.vector.tensor_tensor(om[:, :, :], whole[:, :, :], own_inv[:, :, :], ALU.mult).then_inc(owned, 1)

            def batch(b, j, ahead):
                dve.wait_ge(exped, START + b + 1)
                dve.wait_ge(prepared, START + 2 * b)
                nc.vector.reciprocal(inv[:, :], total[:, :]).then_inc(inverted, 1)
                nc.vector.tensor_copy(p_last[:, :], p[:, :, 2 * P]).then_inc(inverted, 1)
                dve.wait_ge(p_turned, START + b + 1)
                nc.vector.tensor_copy(pt[:, 1, :], banks[:, 5, :]).then_inc(pt_dve, 1)
                if ahead >= 1:
                    softmax(b + 1, 1 - j, 0)
                    softmax(b + 1, 1 - j, 1)
                own(b)
                dve.wait_ge(out_made, START + b + 1)
                nc.vector.tensor_copy(out[:, :, blk(b, S)],
                                      banks[:, 7, 256:256 + KC * S].rearrange("p (c s) -> p c s", c=KC))\
                  .then_inc(out_taken, 1)

            softmax(0, 0, 0)
            softmax(0, 0, 1)
            loop(dve, batch)


def cross_single(core, q, out, ctx_t, ctx_rows, row_w, row_src, row_bias, phi=None, phi_w=None, tops=None):
    nc = core.nc
    with ExitStack() as mem:
        def sb(name, shape):
            return mem.enter_context(nc.sbuf_tensor(f"{name}_{core.turn}", shape, F32))
        ctx_sb = [sb(f"ctx{j}", [P, KC, M]) for j in range(4)]
        rows_sb = [sb(f"rows{j}", [P, 3, D]) for j in range(4)]
        q_st, src_st = sb("q_st", [P, KC, GT]), sb("src_st", [P, KC, GT])
        phi_sb = sb("phi", [P, M])
        s, p = sb("s", [P, M]), sb("p", [P, M])
        pt = sb("pt", [P, 3, P])
        top, neg, total, inv, const = (sb(n, [P, 1]) for n in ("top", "neg", "total", "inv", "const"))
        (block, loaded_t, loaded_rows, loaded_phi, staged, scores_ready, summed, topped, negated, exped,
         inverted, normed, p_turned, pt_ready, out_ready, out_taken, passed) = mem.enter_context(
            phase(core, "loaded_t", "loaded_rows", "loaded_phi", "staged", "scores_ready", "summed", "topped",
                  "negated", "exped", "inverted", "normed", "p_turned", "pt_ready", "out_ready", "out_taken",
                  "passed"))
        sums = 3
        banks = core.banks8

        @block.sync
        def _(sp):
            with sp.Fori(0, NG) as g:
                sp.wait_ge(scores_ready, START + g)
                sp.sem_inc(passed, 1)
                for j in range(4):
                    sp.dma_start(ctx_sb[j][:, :, :], ctx_t[4 * g + j, :, :].rearrange("(k p) m -> p k m", p=P))\
                      .then_inc(loaded_t, 16)
                if phi is not None:
                    sp.wait_ge(summed, START + g * sums)
                    sp.sem_inc(passed, 1)
                    sp.dma_start(phi_sb[:, :], phi[blk(g, GT), :]).then_inc(loaded_phi, 16)
                sp.wait_ge(out_ready, START + g)
                sp.sem_inc(passed, 1)
                for j in range(4):
                    sp.dma_start(rows_sb[j][:, 0:2, :], ctx_rows[4 * g + j, 0:2 * P, :]
                                 .rearrange("(c p) f -> p c f", p=P)).then_inc(loaded_rows, 16)
                    sp.dma_start(rows_sb[j][0:1, 2, :], ctx_rows[4 * g + j, 2 * P:M, :]).then_inc(loaded_rows, 16)

        @block.gpsimd
        def _(pool):
            with pool.Fori(0, NG) as g:
                pool.wait_ge(scores_ready, START + g)
                pool.sem_inc(passed, 1)
                nc.gpsimd.tensor_copy(q_st[:, :, :], q[:, :, blk(g, GT)]).then_inc(staged, 1)
                nc.gpsimd.tensor_copy(src_st[:, :, :], row_src[:, :, blk(g, GT)]).then_inc(staged, 1)

        @block.tensor
        def _(pe):
            with pe.Fori(0, NG) as g:
                pe.wait_ge(loaded_t, START + (g + 1) * 64)
                pe.wait_ge(staged, START + 2 * g + 2)
                pe.wait_ge(summed, START + g * sums)
                for k in range(KC):
                    pe.matmul(banks[:, 1, 0:1], src_st[:, k, :], row_w[:, k:k + 1], start=(k == 0),
                              stop=(k == KC - 1))
                for j in range(4):
                    for k in range(KC):
                        ins = pe.matmul(banks[32 * j:32 * j + 32, 0, 0:M], q_st[:, k, 32 * j:32 * j + 32],
                                        ctx_sb[j][:, k, :], start=(k == 0), stop=(k == KC - 1))
                ins.then_inc(scores_ready, 1)
                pe.wait_ge(normed, START + g + 1)
                pe.wait_ge(pt_ready, START + g)
                for c, (at, m) in enumerate(KCH):
                    ins = pe.transpose(banks[0:m, 2, c * P:(c + 1) * P], p[:, at:at + m], core.ident[:, :])
                ins.then_inc(p_turned, 1)
                pe.wait_ge(pt_ready, START + g + 1)
                pe.wait_ge(loaded_rows, START + (g + 1) * 128)
                pe.wait_ge(out_taken, START + g)
                for j in range(4):
                    for f in range(KC):
                        for c, (at, m) in enumerate(KCH):
                            ins = pe.matmul(banks[:, 3, f * P + 32 * j:f * P + 32 * j + 32],
                                            rows_sb[j][0:m, c, f * P:(f + 1) * P], pt[0:m, c, 32 * j:32 * j + 32],
                                            start=(c == 0), stop=(c == 2))
                ins.then_inc(out_ready, 1)

        @block.scalar
        def _(act):
            with act.Fori(0, NG) as g:
                act.wait_ge(negated, START + g + 1)
                act.wait_ge(p_turned, START + g)
                nc.scalar.activation(p[:, :], s[:, :], ACT.Exp, bias=neg[:, 0:1], accum_out=total[:, 0:1])\
                  .then_inc(exped, 1)
                act.wait_ge(p_turned, START + g + 1)
                act.wait_ge(out_ready, START + g)
                nc.scalar.copy(pt[:, 0:2, :], banks[:, 2, 0:2 * P].rearrange("p (c w) -> p c w", c=2))
                nc.scalar.copy(pt[0:1, 2, :], banks[0:1, 2, 2 * P:3 * P]).then_inc(pt_ready, 1)

        @block.vector
        def _(dve):
            with dve.Fori(0, NG) as g:
                dve.wait_ge(scores_ready, START + g + 1)
                dve.wait_ge(exped, START + g)
                nc.vector.tensor_scalar(const[:, :], banks[:, 1, 0:1], row_bias, None, ALU.add).then_inc(summed, 1)
                if phi is not None:
                    dve.wait_ge(loaded_phi, START + (g + 1) * 16)
                    nc.vector.scalar_tensor_tensor(out=s[:, :], in0=phi_sb[:, :], scalar=phi_w,
                                                   in1=banks[:, 0, 0:M], op0=ALU.mult, op1=ALU.add).then_inc(summed, 1)
                else:
                    nc.vector.tensor_copy(s[:, :], banks[:, 0, 0:M]).then_inc(summed, 1)
                dve.wait_ge(summed, START + g * sums + 2)
                nc.vector.tensor_scalar(s[:, :], s[:, :], const[:, 0:1], None, ALU.add).then_inc(summed, 1)
                dve.wait_ge(summed, START + g * sums + 3)
                nc.vector.tensor_reduce(top[:, :], s[:, :], AX, ALU.max).then_inc(topped, 1)
                dve.wait_ge(topped, START + g + 1)
                if tops is not None:
                    nc.vector.tensor_copy(tops[:, bass.ds(g, 1)], top[:, :])
                nc.vector.tensor_scalar(neg[:, :], top[:, :], -1.0, None, ALU.mult).then_inc(negated, 1)
                dve.wait_ge(exped, START + g + 1)
                nc.vector.reciprocal(inv[:, :], total[:, :]).then_inc(inverted, 1)
                dve.wait_ge(inverted, START + g + 1)
                nc.vector.tensor_scalar(p[:, :], p[:, :], inv[:, 0:1], None, ALU.mult).then_inc(normed, 1)
                dve.wait_ge(out_ready, START + g + 1)
                nc.vector.tensor_copy(out[:, :, blk(g, GT)],
                                      banks[:, 3, 0:KC * P].rearrange("p (f n) -> p f n", f=KC)).then_inc(out_taken, 1)


def gates(core, x, w, bias, gate_rows, experts, shared=0):
    nc = core.nc
    E = experts
    with ExitStack() as mem:
        def sb(name, shape, dt=F32):
            return mem.enter_context(nc.sbuf_tensor(f"{name}_{core.turn}", shape, dt))
        z, e = sb("z", [P, NG, E]), sb("e", [P, NG, E])
        top, total, inv = (sb(n, [P, NG]) for n in ("top", "total", "inv"))
        best, which = sb("best", [P, NG, 8]), sb("which", [P, NG, 8], U32)
        at = sb("at", [P, NG, 8])
        first, second = sb("first", [P, NG, E]), sb("second", [P, NG, E])
        gate_t = sb("gate_t", [E, N])
        ones = sb("ones", [1, N])
        experts_at = core.consts["iota16"]
        (block, logits_ready, step, exped, found, turned, taken, kept, filled) = mem.enter_context(
            phase(core, "logits_ready", "step", "exped", "found", "turned", "taken", "kept", "filled"))

        @block.tensor
        def _(pe):
            for g in range(NG):
                for k in range(KC):
                    ins = pe.matmul(core.psum[0][:, g * E:(g + 1) * E], x[:, k, g * GT:(g + 1) * GT], w[:, k, :],
                                    start=(k == 0), stop=(k == KC - 1))
            ins.then_inc(logits_ready, 1)
            pe.wait_ge(found, START + 1)
            for g in range(NG):
                ins = pe.transpose(core.psum[4 + g // 4][0:E, (g % 4) * P:(g % 4 + 1) * P], second[:, g, :],
                                   core.ident[:, :])
            ins.then_inc(turned, 1)

        @block.scalar
        def _(act):
            act.wait_ge(step, START + 3)
            nc.scalar.activation(e[:, :, :], z[:, :, :], ACT.Exp).then_inc(exped, 1)

        @block.gpsimd
        def _(pool):
            nc.gpsimd.memset(ones[:, :], 1.0).then_inc(filled, 1)

        @block.sync
        def _(sp):
            sp.wait_ge(filled, START + 1)
            sp.wait_ge(taken, START + 1)
            sp.dma_start(gate_rows[0:E, :], gate_t[:, :]).then_inc(kept, 16)
            for j in range(shared):
                sp.dma_start(gate_rows[E + j:E + j + 1, :], ones[:, :]).then_inc(kept, 16)
            sp.wait_ge(kept, START + 16 * (1 + shared))

        @block.vector
        def _(dve):
            n = 0

            def then(ins):
                nonlocal n
                n += 1
                ins.then_inc(step, 1)
                dve.wait_ge(step, START + n)

            dve.wait_ge(logits_ready, START + 1)
            logits = core.psum[0][:, 0:NG * E].rearrange("p (g e) -> p g e", e=E)
            then(nc.vector.tensor_tensor(z[:, :, :], logits, bcast(bias[:, :], NG), ALU.add))
            then(nc.vector.tensor_reduce(top[:, :], z[:, :, :], AX, ALU.max))
            then(nc.vector.tensor_tensor(z[:, :, :], z[:, :, :], bcast(top[:, :], E, 2), ALU.subtract))
            dve.wait_ge(exped, START + 1)
            then(nc.vector.tensor_reduce(total[:, :], e[:, :, :], AX, ALU.add))
            then(nc.vector.reciprocal(inv[:, :], total[:, :]))
            then(nc.vector.tensor_tensor(e[:, :, :], e[:, :, :], bcast(inv[:, :], E, 2), ALU.mult))
            for g in range(NG):
                ins = nc.vector.max(best[:, g, :], e[:, g, :])
            then(ins)
            for g in range(NG):
                ins = nc.vector.max_index(which[:, g, :], best[:, g, :], e[:, g, :])
            then(ins)
            then(nc.vector.tensor_copy(at[:, :, :], which[:, :, :]))
            for g in range(NG):
                nc.vector.tensor_scalar(first[:, g, :], experts_at[:, 0:E], at[:, g, 0:1], best[:, g, 0:1],
                                        ALU.is_equal, ALU.mult)
                ins = nc.vector.tensor_scalar(second[:, g, :], experts_at[:, 0:E], at[:, g, 1:2],
                                              best[:, g, 1:2], ALU.is_equal, ALU.mult)
            then(ins)
            nc.vector.tensor_tensor(second[:, :, :], second[:, :, :], first[:, :, :], ALU.add).then_inc(found, 1)
            dve.wait_ge(turned, START + 1)
            nc.vector.tensor_copy(gate_t[:, :].rearrange("e (b n) -> e b n", b=4),
                                  core.banks8[0:E, 4:8, :]).then_inc(taken, 1)


def experts_sum(core, kind, x, acc, gate_rows, experts, w1, w2, b1=None, b2=None, hidden=None):
    nc = core.nc
    hc = hidden // P if hidden else 0
    hp = 2 * hc if kind == "glu" else hc
    with ExitStack() as mem:
        def sb(name, shape):
            return mem.enter_context(nc.sbuf_tensor(f"{name}_{core.turn}", shape, F32))
        w1_sb = [sb(f"w1_{j}", [P, KC, hp * P if hp else D]) for j in range(2)]
        w2_sb = [sb(f"w2_{j}", [P, hc, D]) for j in range(2)] if hc else None
        b1_sb = [sb(f"b1_{j}", [P, hc]) for j in range(2)] if b1 is not None else None
        b2_sb = [sb(f"b2_{j}", [P, KC]) for j in range(2)] if b2 is not None else None
        gate = [sb(f"gate_{j}", [P, N]) for j in range(2)]
        h = sb("h", [P, 2, hc, BLK]) if hc else None
        act_g = sb("act_g", [P, 2, BLK]) if kind == "glu" else None
        y = sb("y", [P, 2, KC, BLK])
        (block, loaded, h_made, h_ready, y_made, y_gated, added, glu_ready, loaded1, passed) = mem.enter_context(
            phase(core, "loaded", "h_made", "h_ready", "y_made", "y_gated", "added", "glu_ready", "loaded1",
                  "passed"))
        arrived = [loaded, loaded1]
        loads = 16 * (2 + bool(hc) + (b1 is not None) + (b2 is not None))
        banks = core.banks8
        y_at = 4
        credit = {"relu": hc, "plain": 0, "glu": 2}[kind]

        @block.sync
        def _(sp):
            def fetch(e, j):
                sp.dma_start(w1_sb[j][:, :, :], w1[e, :, :].rearrange("(k p) m -> p k m", p=P)).then_inc(arrived[j], 16)
                if hc:
                    sp.dma_start(w2_sb[j][:, :, :], w2[e, :, :].rearrange("(k p) m -> p k m", p=P))\
                      .then_inc(arrived[j], 16)
                if b1 is not None:
                    sp.dma_start(b1_sb[j][:, :], b1[e, :, :]).then_inc(arrived[j], 16)
                if b2 is not None:
                    sp.dma_start(b2_sb[j][:, :], b2[e, :, :]).then_inc(arrived[j], 16)
                sp.dma_start(gate[j][:, :], gate_rows[bass.ds(e, 1), :].broadcast_to([P, N])).then_inc(arrived[j], 16)

            fetch(0, 0)
            fetch(1, 1)
            if experts > 2:
                with sp.Fori(0, experts // 2 - 1) as r:
                    for j in range(2):
                        sp.wait_ge(y_gated, START + (2 * r + j + 1) * NB * KC)
                        sp.sem_inc(passed, 1)
                        fetch(2 * r + j + 2, j)

        @block.tensor
        def _(pe):
            def first(e, j, t):
                n = e * NB + t
                pe.wait_ge(arrived[j], START + (e - j) * (loads // 2) + loads)
                for m in range(hp):
                    bank = m if hc == 4 else 2 * (t % 2) + m
                    pe.wait_ge(h_ready, START + (n * hc + (m + 1 if kind == "relu" else 1)))
                    for k in range(KC):
                        ins = pe.matmul(banks[:, bank, :], w1_sb[j][:, k, m * P:(m + 1) * P], x[:, k, blk(t)],
                                        start=(k == 0), stop=(k == KC - 1))
                    ins.then_inc(h_made, 1)

            def second(e, j, t):
                n = e * NB + t
                if hc:
                    pe.wait_ge(h_ready, START + (n + 1) * hc + credit)
                else:
                    pe.wait_ge(arrived[j], START + (e - j) * (loads // 2) + loads)
                for m in range(KC):
                    pe.wait_ge(added, START + n * KC + m + 1)
                    bank = y_at + 2 * (t % 2) + m
                    if hc:
                        for k in range(hc):
                            ins = pe.matmul(banks[:, bank, :], w2_sb[j][:, k, m * P:(m + 1) * P],
                                            h[:, t % 2, k, :], start=(k == 0), stop=(k == hc - 1))
                    else:
                        for k in range(KC):
                            ins = pe.matmul(banks[:, bank, :], w1_sb[j][:, k, m * P:(m + 1) * P], x[:, k, blk(t)],
                                            start=(k == 0), stop=(k == KC - 1))
                    ins.then_inc(y_made, 1)

            if hc:
                first(0, 0, 0)
            with pe.Fori(0, experts // 2 - 1) as r:
                for j in range(2):
                    for t in range(NB):
                        if hc:
                            if t + 1 < NB:
                                first(2 * r + j, j, t + 1)
                            else:
                                first(2 * r + j + 1, 1 - j, 0)
                        second(2 * r + j, j, t)
            for j in range(2):
                for t in range(NB):
                    if hc:
                        if t + 1 < NB:
                            first(experts - 2 + j, j, t + 1)
                        elif j == 0:
                            first(experts - 1, 1, 0)
                    second(experts - 2 + j, j, t)

        @block.scalar
        def _(act):
            if kind == "plain":
                return
            act.sem_inc(h_ready, credit)
            with act.Fori(0, experts // 2) as r:
                for j in range(2):
                    for t in range(NB):
                        n = (2 * r + j) * NB + t
                        if kind == "relu":
                            for m in range(hc):
                                act.wait_ge(h_made, START + n * hp + m + 1)
                                act.wait_ge(y_made, START + (((n - 1) * KC) if t >= 1 else (2 * r + j) * NB * KC - KC * j))
                                nc.scalar.activation(h[:, t % 2, m, :], banks[:, m, :], ACT.Relu,
                                                     bias=b1_sb[j][:, m:m + 1]).then_inc(h_ready, 1)
                        else:
                            act.wait_ge(h_made, START + n * 2 + 1)
                            act.wait_ge(h_ready, START + n - 1 + credit)
                            nc.scalar.activation(act_g[:, t % 2, :], banks[:, 2 * (t % 2), :], ACT.Silu)\
                              .then_inc(glu_ready, 1)

        @block.vector
        def _(dve):
            dve.sem_inc(added, 4)
            with dve.Fori(0, experts // 2) as r:
                for j in range(2):
                    for t in range(NB):
                        n = (2 * r + j) * NB + t

                        def glu(n, t):
                            dve.wait_ge(glu_ready, START + n + 1)
                            dve.wait_ge(h_made, START + n * 2 + 2)
                            nc.vector.tensor_tensor(h[:, t % 2, 0, :], act_g[:, t % 2, :],
                                                    banks[:, 2 * (t % 2) + 1, :], ALU.mult).then_inc(h_ready, 1)

                        if kind == "glu":
                            glu(n, t)
                        for m in range(KC):
                            dve.wait_ge(y_made, START + n * KC + m + 1)
                            dve.wait_ge(arrived[j], START + (r + 1) * loads)
                            dve.wait_ge(added, START + n * KC + m + 1)
                            nc.vector.scalar_tensor_tensor(
                                out=y[:, t % 2, m, :], in0=banks[:, y_at + 2 * (t % 2) + m, :],
                                scalar=b2_sb[j][:, m:m + 1] if b2 is not None else 0.0,
                                in1=gate[j][:, blk(t)], op0=ALU.add, op1=ALU.mult).then_inc(y_gated, 1)
                            dve.wait_ge(y_gated, START + n * KC + m + 1)
                            nc.vector.tensor_tensor(acc[:, m, blk(t)], acc[:, m, blk(t)], y[:, t % 2, m, :],
                                                    ALU.add).then_inc(added, 1)


def rms_norm(core, t, w):
    nc = core.nc
    with ExitStack() as mem:
        def sb(name, shape):
            return mem.enter_context(nc.sbuf_tensor(f"{name}_{core.turn}", shape, F32))
        sq, std, inv = sb("sq", [P, 2, KC, BLK]), sb("std", [P, 2, KC, BLK]), sb("inv", [P, 2, KC, BLK])
        block, squared, mean_ready, std_ready, inverted, done = mem.enter_context(
            phase(core, "squared", "mean_ready", "std_ready", "inverted", "done"))

        @block.gpsimd
        def _(pool):
            for n in range(NB):
                if n >= 2:
                    pool.wait_ge(mean_ready, START + n - 1)
                nc.gpsimd.tensor_tensor(sq[:, n % 2, :, :], t[:, :, blk(n)], t[:, :, blk(n)], ALU.mult)\
                  .then_inc(squared, 1)

        @block.tensor
        def _(pe):
            for n in range(NB):
                pe.wait_ge(squared, START + n + 1)
                if n >= 2:
                    pe.wait_ge(std_ready, START + n - 1)
                for k in range(KC):
                    ins = pe.matmul(core.psum[2 * (n % 2) + k], core.consts["same_head"][:, :],
                                    sq[:, n % 2, k, :], start=True, stop=True)
                ins.then_inc(mean_ready, 1)

        @block.scalar
        def _(act):
            for n in range(NB):
                act.wait_ge(mean_ready, START + n + 1)
                if n >= 2:
                    act.wait_ge(inverted, START + n - 1)
                nc.scalar.activation(std[:, n % 2, :, :], core.banks8[:, 2 * (n % 2):2 * (n % 2) + 2, :], ACT.Sqrt,
                                     bias=core.eps[:, 1:2]).then_inc(std_ready, 1)

        @block.vector
        def _(dve):
            for n in range(NB):
                dve.wait_ge(std_ready, START + n + 1)
                nc.vector.reciprocal(inv[:, n % 2, :, :], std[:, n % 2, :, :]).then_inc(inverted, 1)
                dve.wait_ge(inverted, START + n + 1)
                dve.wait_ge(squared, START + n + 1)
                for k in range(KC):
                    nc.vector.scalar_tensor_tensor(out=t[:, k, blk(n)], in0=inv[:, n % 2, k, :],
                                                   scalar=w[:, k:k + 1], in1=t[:, k, blk(n)], op0=ALU.mult,
                                                   op1=ALU.mult).then_inc(done, 1)


def elementwise(core, *steps):
    with phase(core, "step") as (block, step):
        @block.vector
        def _(dve):
            for n, f in enumerate(steps):
                f().then_inc(step, 1)
                dve.wait_ge(step, START + n + 1)


def butterfly(core, w, row, stage_w, backwards):
    nc = core.nc
    hidden, stages = 4 * D, 10
    with ExitStack() as mem:
        def sb(name, shape):
            return mem.enter_context(nc.sbuf_tensor(f"{name}_{core.turn}", shape, F32))
        sw = [sb(f"sw{j}", [P, hidden * 2]) for j in range(2)]
        t = [sb(f"t{j}", [P, KC, hidden // 2]) for j in range(4)]
        tr = [sb(f"tr{j}", [1, hidden // 2]) for j in range(4)]
        block, loaded0, loaded1, step, used = mem.enter_context(phase(core, "loaded0", "loaded1", "step", "used"))
        arrived = [loaded0, loaded1]
        order = range(stages - 1, -1, -1) if backwards else range(stages)

        @block.sync
        def _(sp):
            for n, st in enumerate(order):
                if n >= 2:
                    sp.wait_ge(used, START + n - 1)
                sp.dma_start(sw[n % 2][:, :], stage_w[st:st + 1, :].broadcast_to([P, 2 * hidden]))\
                  .then_inc(arrived[n % 2], 16)

        @block.vector
        def _(dve):
            done = 0
            for n, st in enumerate(order):
                half = 2 ** st
                dve.wait_ge(arrived[n % 2], START + 16 * (n // 2 + 1))
                wv = sw[n % 2][:, :].rearrange("p (b s q) -> p b s q", s=half, q=4)
                both = []
                for c in range(KC):
                    v = w[:, c, :].rearrange("p (b h s) -> p b h s", h=2, s=half)
                    both.append((v[:, :, 0, :], v[:, :, 1, :], wv, [x[:, c, :] for x in t]))
                if row is not None:
                    v = row[:, :].rearrange("p (b h s) -> p b h s", h=2, s=half)
                    both.append((v[:, :, 0, :], v[:, :, 1, :], wv[0:1], [x[:, :] for x in tr]))
                order4 = [(0, 0), (2, 1), (1, 0), (3, 1)] if backwards else [(0, 0), (1, 1), (2, 0), (3, 1)]
                for a, b, ww, tt in both:
                    for i, (q, which) in enumerate(order4):
                        ins = nc.vector.tensor_tensor(tt[i].rearrange("p (b s) -> p b s", s=half),
                                                      (a, b)[which], ww[:, :, :, q], ALU.mult)
                        ins.then_inc(step, 1)
                        done += 1
                dve.wait_ge(step, START + done)
                for a, b, ww, tt in both:
                    for o, i in ((a, 0), (b, 2)):
                        tv = [x.rearrange("p (b s) -> p b s", s=half) for x in tt[i:i + 2]]
                        nc.vector.tensor_tensor(o, tv[0], tv[1], ALU.add).then_inc(step, 1)
                        done += 1
                dve.wait_ge(step, START + done)
                dve.sem_inc(used, 1)


def turn_weights(core, src, dst, row=None, row_dst=None):
    nc = core.nc
    with phase(core, "turned", "taken") as (block, turned, taken):
        @block.tensor
        def _(pe):
            for h in range(8):
                for c in range(KC):
                    ins = pe.transpose(core.psum[h % 4][:, c * P:(c + 1) * P] if h < 4 else
                                       core.psum[h % 4][:, (2 + c) * P:(3 + c) * P],
                                       src[:, c, h * P:(h + 1) * P], core.ident[:, :])
            if row is not None:
                for h in range(8):
                    ins = pe.transpose(core.psum[4][:, h:h + 1], row[:, h * P:(h + 1) * P], core.ident[0:1, 0:1])
            ins.then_inc(turned, 1)

        @block.vector
        def _(dve):
            dve.wait_ge(turned, START + 1)
            for half in range(2):
                nc.vector.tensor_copy(dst[:, 4 * half:4 * half + 4, :],
                                      core.banks8[:, 0:4, half * D:(half + 1) * D]).then_inc(taken, 1)
            if row is not None:
                nc.vector.tensor_copy(row_dst[:, :], core.psum[4][:, 0:8]).then_inc(taken, 1)


def context_mean(core, x, tops, mixed):
    nc = core.nc
    nb = BLK // S
    with ExitStack() as mem:
        def sb(name, shape):
            return mem.enter_context(nc.sbuf_tensor(f"{name}_{core.turn}", shape, F32))
        diag = sb("diag", [P, 4, P])
        z, e = sb("z", [P, nb, S]), sb("e", [P, nb, S])
        top, total, inv = (sb(n, [P, nb]) for n in ("top", "total", "inv"))
        wx, bar = sb("wx", [P, KC, BLK]), sb("bar", [P, KC * nb])
        block, diag_ready, spread, centred, exped, step = mem.enter_context(
            phase(core, "diag_ready", "spread", "centred", "exped", "step"))

        @block.tensor
        def _(pe):
            for t in range(NB):
                pe.wait_ge(diag_ready, START + t + 1)
                pe.matmul(core.psum[t], core.consts["ones"][:, :], diag[:, :, :].rearrange("p g w -> p (g w)"),
                          start=True, stop=True).then_inc(spread, 1)

        @block.gpsimd
        def _(pool):
            for t in range(NB):
                if t >= 1:
                    pool.wait_ge(spread, START + t)
                nc.gpsimd.tensor_tensor(diag[:, :, :], bcast(core.ident[:, :], 4),
                                        bcast(tops[:, 4 * t:4 * t + 4], P, 2), ALU.mult).then_inc(diag_ready, 1)

        @block.scalar
        def _(act):
            for t in range(NB):
                act.wait_ge(centred, START + t + 1)
                nc.scalar.activation(e[:, :, :], z[:, :, :], ACT.Exp).then_inc(exped, 1)

        @block.vector
        def _(dve):
            n = 0

            def then(ins):
                nonlocal n
                n += 1
                ins.then_inc(step, 1)
                dve.wait_ge(step, START + n)

            for t in range(NB):
                dve.wait_ge(spread, START + t + 1)
                m = core.psum[t].rearrange("p (b s) -> p b s", s=S)
                then(nc.vector.tensor_reduce(top[:, :], m, AX, ALU.max))
                nc.vector.tensor_tensor(z[:, :, :], m, bcast(top[:, :], S, 2), ALU.subtract).then_inc(centred, 1)
                dve.wait_ge(exped, START + t + 1)
                then(nc.vector.tensor_reduce(total[:, :], e[:, :, :], AX, ALU.add))
                then(nc.vector.reciprocal(inv[:, :], total[:, :]))
                then(nc.vector.tensor_tensor(e[:, :, :], e[:, :, :], bcast(inv[:, :], S, 2), ALU.mult))
                then(nc.vector.tensor_tensor(wx[:, :, :], x[:, :, blk(t)],
                                             bcast(e[:, :, :].rearrange("p b s -> p (b s)"), KC), ALU.mult))
                then(nc.vector.tensor_reduce(bar[:, :], wx[:, :, :].rearrange("p k (b s) -> p (k b) s", s=S), AX,
                                             ALU.add))
                for k in range(KC):
                    then(nc.vector.tensor_tensor(
                        mixed[:, k, blk(t)].rearrange("p (b s) -> p b s", s=S),
                        x[:, k, blk(t)].rearrange("p (b s) -> p b s", s=S),
                        bcast(bar[:, k * nb:(k + 1) * nb], S, 2), ALU.mult))


def perceiver(nc, dram, out, scratch, layers=12):
    with ExitStack() as ctx:
        core = Core(nc, ctx, dram)
        start(core)
        steps = [l0_xattn, l0_attn, l0_ffn, l1_xattn, l1_attn, l1_ffn, l2_xattn, l2_attn, l2_ffn, l3_xattn,
                 l3_attn, l3_ffn]
        for step in steps[:layers]:
            with ExitStack() as mem:
                turn = core.turn

                def sb(name, *shape):
                    return mem.enter_context(nc.sbuf_tensor(f"{name}_{turn}", list(shape), F32))
                step(core, sb, scratch)
        store(core, core.x, out)


def weights(core, sb, layer, mats, vecs=()):
    got, pairs = [], []
    for name in mats:
        d = core.dram[f"{layer}_{name}"]
        tile = sb(name, P, d.shape[0] // P, d.shape[1])
        pairs.append((tile[:, :, :], chunks(d)))
        got.append(tile)
    for name in vecs:
        d = core.dram[f"{layer}_{name}"]
        tile = sb(name, P, d.shape[1])
        pairs.append((tile[:, :], d if d.shape[0] == P else d.broadcast_to([P, d.shape[1]])))
        got.append(tile)
    load(core, *pairs)
    return got


def l0_xattn(core, sb, scratch):
    q1, k1, o1, q2, k2, o2, f1, f2, fb1, fb2, g1, b1, g2, b2, g3, b3 = weights(
        core, sb, "L0_xattn", ["q1W", "w1W", "o1W", "q2W", "w2W", "o2W", "ffW1", "ffW2"],
        ["ffb1", "ffb2", "g1", "b1", "g2", "b2", "g3", "b3"])
    xn, q, k, o = (sb(n, P, KC, N) for n in ("xn", "q", "k", "o"))
    layer_norm(core, core.x, xn)
    linear(core, q1, xn, q)
    linear(core, k1, xn, k)
    self_attention(core, "heads", q, k, k, o, KC, 0.25, core.consts["mask_block"])
    linear(core, o1, o, xn, kind="residual")
    layer_norm(core, xn, xn, (g1, b1))
    linear(core, q2, xn, q)
    tail_values(core, k2, scratch["tails"])
    cross_attention(core, q, k2, None, o, core.dram["ctx_t"], scratch["tails"], mask=core.dram["mask"])
    linear(core, o2, o, xn, kind="residual")
    layer_norm(core, xn, xn, (g2, b2))
    mlp(core, xn, f1, fb1, f2, fb2, xn)
    layer_norm(core, xn, core.x, (g3, b3), add=core.x)


def mlp(core, x, w1, b1, w2, b2, out):
    nc = core.nc
    HC = 8
    with ExitStack() as mem:
        h = mem.enter_context(nc.sbuf_tensor(f"h_{core.turn}", [P, 2, HC, BLK], F32))
        block, h_made, h_ready, y_made, y_taken = mem.enter_context(
            phase(core, "h_made", "h_ready", "y_made", "y_taken"))

        @block.tensor
        def _(pe):
            def first(t):
                for m in range(HC):
                    n = t * HC + m
                    if n >= 4:
                        pe.wait_ge(h_ready, START + n - 3)
                    for k in range(KC):
                        ins = pe.matmul(core.psum[m % 4], w1[:, k, m * P:(m + 1) * P], x[:, k, blk(t)],
                                        start=(k == 0), stop=(k == KC - 1))
                    ins.then_inc(h_made, 1)

            def second(t):
                pe.wait_ge(h_ready, START + (t + 1) * HC)
                for m in range(KC):
                    if t >= 2:
                        pe.wait_ge(y_taken, START + (t - 2) * KC + m + 1)
                    for k in range(HC):
                        ins = pe.matmul(core.psum[4 + 2 * (t % 2) + m], w2[:, k, m * P:(m + 1) * P],
                                        h[:, t % 2, k, :], start=(k == 0), stop=(k == HC - 1))
                    ins.then_inc(y_made, 1)

            first(0)
            for t in range(NB):
                if t + 1 < NB:
                    first(t + 1)
                second(t)

        @block.scalar
        def _(act):
            for t in range(NB):
                for m in range(HC):
                    act.wait_ge(h_made, START + t * HC + m + 1)
                    if t >= 2:
                        act.wait_ge(y_made, START + (t - 1) * KC)
                    nc.scalar.activation(h[:, t % 2, m, :], core.psum[m % 4], ACT.Gelu, bias=b1[:, m:m + 1])\
                      .then_inc(h_ready, 1)

        @block.vector
        def _(dve):
            for t in range(NB):
                dve.wait_ge(h_made, START + (t + 1) * HC)
                for m in range(KC):
                    dve.wait_ge(y_made, START + t * KC + m + 1)
                    nc.vector.scalar_tensor_tensor(out=out[:, m, blk(t)], in0=core.psum[4 + 2 * (t % 2) + m],
                                                   scalar=b2[:, m:m + 1], in1=out[:, m, blk(t)], op0=ALU.add,
                                                   op1=ALU.add).then_inc(y_taken, 1)


def l0_attn(core, sb, scratch):
    wqkv, wo, bqkv, bo = weights(core, sb, "L0_attn", ["W_qkv", "W_out"], ["b_qkv", "b_out"])
    parts = [scratch["qkv"][i * D:(i + 1) * D, :] for i in range(3)]
    with ExitStack() as mem:
        nc = core.nc
        xn = mem.enter_context(nc.sbuf_tensor("seg_xn", [P, KC, N], F32))
        qkv = mem.enter_context(nc.sbuf_tensor("seg_qkv", [P, 6, N], F32))
        layer_norm(core, core.x, xn)
        linear(core, wqkv, xn, qkv, bias=bqkv, mc=6)
        load(core, *[(chunks(parts[i]), qkv[:, 2 * i:2 * i + 2, :]) for i in range(3)])
    self_attention(core, "segments", *parts, scratch["seg_out"], KC, 512 ** -0.5, core.consts["mask_segments"])
    o = sb("o", P, KC, N)
    load(core, (o[:, :, :], chunks(scratch["seg_out"])))
    linear(core, wo, o, core.x, bias=bo, kind="residual")


def l0_ffn(core, sb, scratch):
    gw, gb = weights(core, sb, "L0_ffn", ["gate_w"], ["gate_b"])
    d = core.dram
    xn = sb("xn", P, KC, N)
    layer_norm(core, core.x, xn)
    gates(core, xn, gw, gb, scratch["gates"], 8)
    experts_sum(core, "relu", xn, core.x, scratch["gates"], 8, d["L0_ffn_w1"], d["L0_ffn_w2"], d["L0_ffn_b1"],
                d["L0_ffn_b2"], hidden=512)


def l1_xattn(core, sb, scratch):
    nc = core.nc
    wq, wk, wv, wo, w_rel = weights(core, sb, "L1_xattn", ["w_q", "w_k", "w_v", "w_proj"], ["w_rel"])
    xn, q, o, rel = sb("xn", P, KC, N), sb("q", P, KC, N), sb("o", P, KC, N), sb("rel", P, 4, M)
    layer_norm(core, core.x, xn)
    linear(core, wq, xn, q)
    elementwise(core, *[lambda n=n: nc.vector.tensor_scalar(rel[:, n, :], core.consts["positions"][:, :],
                                                            w_rel[:, n:n + 1], None, ALU.mult) for n in range(4)])
    tail_values(core, wv, scratch["tails"])
    cross_attention(core, q, wk, wv, o, core.dram["ctx_t"], scratch["tails"], rel=rel)
    linear(core, wo, o, core.x, kind="residual")


def l1_attn(core, sb, scratch):
    wq, wv, qw, vw = weights(core, sb, "L1_attn", ["Wq", "Wv"], ["q_norm_w", "v_norm_w"])
    xn, q, v, o = (sb(n, P, KC, N) for n in ("xn", "q", "v", "o"))
    layer_norm(core, core.x, xn)
    linear(core, wq, xn, q)
    linear(core, wv, xn, v)
    rms_norm(core, q, qw)
    rms_norm(core, v, vw)
    self_attention(core, "linear", q, xn, v, o, KC, mask=core.consts["mask_lower"])
    elementwise(core, lambda: core.nc.vector.tensor_tensor(core.x[:, :, :], core.x[:, :, :], o[:, :, :], ALU.add))


def l1_ffn(core, sb, scratch):
    nc = core.nc
    wq, wk, wv, wo, wg, bq, bk, bv, bo, g1, be1, g2, be2, bg = weights(
        core, sb, "L1_ffn", ["Wq", "Wk", "Wv", "Wo", "Wg"],
        ["bq", "bk", "bv", "bo", "g1", "be1", "g2", "be2", "bg"])
    xn, q, k, v, o = (sb(n, P, KC, N) for n in ("xn", "q", "k", "v", "o"))
    d = core.dram
    layer_norm(core, core.x, xn)
    linear(core, wq, xn, q, bias=bq)
    linear(core, wk, xn, k, bias=bk)
    linear(core, wv, xn, v, bias=bv)
    self_attention(core, "heads", q, k, v, o, KC, 0.25, core.consts["mask_block"])
    linear(core, wo, o, q, bias=bo)
    layer_norm(core, q, xn, (g1, be1), add=xn)
    gates(core, xn, wg, bg, scratch["gates"], 8)
    elementwise(core, lambda: nc.vector.memset(k[:, :, :], 0.0))
    experts_sum(core, "plain", xn, k, scratch["gates"], 8, d["L1_ffn_We"], None, b2=d["L1_ffn_bexp"])
    layer_norm(core, k, xn, (g2, be2), add=xn)
    elementwise(core, lambda: nc.vector.tensor_tensor(core.x[:, :, :], core.x[:, :, :], xn[:, :, :], ALU.add))


def l2_xattn(core, sb, scratch):
    nc = core.nc
    wqv, w_sim, b_sim, bqv = weights(core, sb, "L2_xattn", ["W_qv"], ["w_sim", "b_sim", "b_qv"])
    xn, q, hat, mixed, tops = (sb("xn", P, KC, N), sb("q", P, KC, N), sb("hat", P, KC, N),
                               sb("mixed", P, KC, N), sb("tops", P, NG))
    d = core.dram
    layer_norm(core, core.x, xn)
    elementwise(core, *[lambda k=k: nc.vector.tensor_scalar(q[:, k, :], xn[:, k, :], w_sim[:, 4 + k:5 + k],
                                                            w_sim[:, 2 + k:3 + k], ALU.mult, ALU.add)
                        for k in range(KC)])
    cross_single(core, q, hat, d["ctx_t"], d["ctx"], w_sim, xn, b_sim[:, 0:1], tops=tops)
    linear(core, wqv[:, 0:2, :], xn, core.x, bias=bqv, kind="residual")
    linear(core, wqv[:, 2:4, :], hat, core.x, kind="residual")
    elementwise(core, lambda: nc.vector.tensor_tensor(hat[:, :, :], hat[:, :, :], xn[:, :, :], ALU.mult))
    linear(core, wqv[:, 4:6, :], hat, core.x, kind="residual")
    context_mean(core, xn, tops, mixed)
    linear(core, wqv[:, 6:8, :], mixed, core.x, kind="residual")


def l2_attn(core, sb, scratch):
    wq, wk, wv = weights(core, sb, "L2_attn", ["W_Q", "W_K", "W_V"])
    xn, q, k, o = (sb(n, P, KC, N) for n in ("xn", "q", "k", "o"))
    layer_norm(core, core.x, xn)
    linear(core, wq, xn, q)
    linear(core, wk, xn, k)
    single_attention_old(core, "single", q, k, xn, o, KC, D ** -0.5, core.consts["mask_causal"], wv=wv)
    elementwise(core, lambda: core.nc.vector.tensor_tensor(core.x[:, :, :], core.x[:, :, :], o[:, :, :], ALU.add))


def l2_ffn(core, sb, scratch):
    nc = core.nc
    w_up, w_con_t, up_bias, b_con, down_bias = weights(
        core, sb, "L2_ffn", ["W_exp", "W_con_t"], ["up_bias", "b_con", "down_bias"])
    xn, w_down = sb("xn", P, KC, N), sb("w_down", P, 8, D)
    row, hb = sb("row", 1, 4 * D), sb("hb", P, 8)
    d = core.dram
    load(core, (row[:, :], d["L2_ffn_b_exp"]))
    butterfly(core, w_up, row, d["L2_ffn_up_weights"], False)
    butterfly(core, w_con_t, None, d["L2_ffn_down_weights"], True)
    turn_weights(core, w_con_t, w_down, row, hb)
    elementwise(core, lambda: nc.vector.tensor_tensor(hb[:, :], hb[:, :], up_bias[:, :], ALU.add),
                lambda: nc.vector.tensor_tensor(b_con[:, :], b_con[:, :], down_bias[:, :], ALU.add))
    layer_norm(core, core.x, xn)
    mlp(core, xn, w_up, hb, w_down, b_con, core.x)


def l3_xattn(core, sb, scratch):
    nc = core.nc
    wq, wk, wv, bq, bk, bv, betas = weights(core, sb, "L3_xattn", ["Wq", "Wk", "Wv"], ["bq", "bk", "bv", "betas"])
    xn, q, qk, o, phi_w, zero = (sb("xn", P, KC, N), sb("q", P, KC, N), sb("qk", P, KC, N), sb("o", P, KC, N),
                                 sb("phi_w", P, 1), sb("zero", P, 1))
    d = core.dram
    layer_norm(core, core.x, xn)
    linear(core, wq, xn, q, bias=bq)
    elementwise(core, lambda: nc.vector.tensor_scalar(q[:, :, :], q[:, :, :], D ** -0.5, None, ALU.mult),
                lambda: nc.vector.memset(zero[:, :], 0.0),
                lambda: nc.vector.tensor_tensor(phi_w[:, :], betas[:, 0:1], betas[:, 1:2], ALU.add),
                lambda: nc.vector.tensor_tensor(phi_w[:, :], phi_w[:, :], betas[:, 2:3], ALU.subtract))
    linear(core, wk, q, qk)
    cross_single(core, qk, o, d["ctx_t"], d["ctx"], bk, q, zero[:, 0:1], phi=d["fside"], phi_w=phi_w[:, 0:1])
    linear(core, wv, o, core.x, bias=bv, kind="residual")


def l3_attn(core, sb, scratch):
    lb, bq, bk, bv = weights(core, sb, "L3_attn", [], ["l_b", "q_b", "k_b", "v_b"])
    d = core.dram
    wq, wk, wv = (sb(n, P, KC, 512) for n in ("wq", "wk", "wv"))
    wl = sb("wl", P, 4, D)
    xn = sb("xn", P, KC, N)
    layer_norm(core, core.x, xn)
    q, k, v = (sb(n, P, 4, N) for n in ("q", "k", "v"))
    for half in range(2):
        cols = slice(half * 512, (half + 1) * 512)
        load(core, *[(t[:, :, :], chunks(d[f"L3_attn_{n}"][:, cols]))
                     for n, t in (("q_w", wq), ("k_w", wk), ("v_w", wv))],
             (wl[:, :, :], chunks(d["L3_attn_l_w"][cols, :])))
        for w, b, t in ((wq, bq, q), (wk, bk, k), (wv, bv, v)):
            linear(core, w, xn, t, bias=b[:, 4 * half:4 * half + 4], mc=4)
        self_attention(core, "columns", k, q, v, q, 4, 0.125, core.consts["mask_block"])
        linear(core, wl, q, core.x, bias=lb if half == 0 else None, kind="residual", kc=4)


def l3_ffn(core, sb, scratch):
    nc = core.nc
    (wr,) = weights(core, sb, "L3_ffn", ["Wr"])
    d = core.dram
    xn, no_bias = sb("xn", P, KC, N), sb("no_bias", P, 16)
    layer_norm(core, core.x, xn)
    elementwise(core, lambda: nc.vector.memset(no_bias[:, :], 0.0))
    gates(core, xn, wr, no_bias, scratch["gates"], 16, shared=2)
    experts_sum(core, "glu", xn, core.x, scratch["gates"], 18, d["L3_ffn_Wgu"], d["L3_ffn_Wd"], hidden=P)


def shape_constants():
    import numpy as np
    f, r = np.float32, np.arange(128)
    same = r[:, None] // 32 == r[None, :] // 32
    lower = same & (r[:, None] >= r[None, :])
    seg, tok = r // 8, r % 8
    at = tok % 2 * 16 + seg
    own = (tok[:, None] // 2 == tok[None, :] // 2) & (at[:, None] >= at[None, :])
    hide = f(-1e30)
    return {
        "ident": np.eye(128, dtype=f),
        "mask_block": np.where(same, f(0), hide),
        "mask_causal": np.where(lower, f(0), hide),
        "mask_lower": lower.astype(f),
        "mask_segments": np.where(own, f(0), hide),
        "head_of_8": (r[:, None] // 16 == np.arange(8)[None, :]).astype(f),
        "head_of_2": (r[:, None] // 64 == np.arange(2)[None, :]).astype(f),
        "own_head": (r[:, None] // 32 == np.arange(64)[None, :] // 16).astype(f),
        "query_sel": (r[:, None] % 32 == np.arange(32)[None, :]).astype(f),
        "same_head": (r[:, None] // 16 == r[None, :] // 16).astype(f) / 16,
        "iota16": np.tile(np.arange(16, dtype=f), (128, 1)),
        "ones": np.ones((128, 128), f),
        "positions": (r[:, None] % 32 - np.arange(257)[None, :]).astype(f),
    }


def laid_out(inputs):
    import numpy as np
    a = {k: np.asarray(v) for k, v in inputs.items()}

    def vec(b):
        return b.reshape(-1, 128).T

    def heads_cols(w):
        return w.reshape(-1, 16, 16).transpose(0, 2, 1).reshape(-1, 256)

    out = {"x": a["x"].reshape(2048, 256).T, "ctx": a["ctx_1024"], "ctx_t": a["ctx_1024"].transpose(0, 2, 1),
           "ctx_last_t": a["ctx_1024"][:, 256, :].T,
           "fside": a["fside_BxSxS2_0"].reshape(2048, 257),
           "mask": a["mask_Bx1xS2x1_bk0"].reshape(64, 1, 257)}
    n = "L0_xattn_"
    for w in ("q1W", "w1W", "q2W", "w2W"):
        out[n + w] = heads_cols(a[n + w])
    for w in ("o1W", "o2W"):
        out[n + w] = heads_cols(a[n + w].T).T
    for w in ("ffW1", "ffW2"):
        out[n + w] = a[n + w]
    for b in ("ffb1", "ffb2", "g1", "b1", "g2", "b2", "g3", "b3"):
        out[n + b] = vec(a[n + b])
    n = "L0_attn_"
    parts = a[n + "W_qkv"].reshape(256, 16, 3, 16).transpose(0, 2, 1, 3).reshape(256, 768)
    out[n + "W_qkv"] = parts
    out[n + "b_qkv"] = vec(a[n + "b_qkv"].reshape(16, 3, 16).transpose(1, 0, 2).reshape(768))
    out[n + "W_out"], out[n + "b_out"] = a[n + "W_out"], vec(a[n + "b_out"])
    n = "L0_ffn_"
    out[n + "gate_w"], out[n + "gate_b"] = a[n + "gate_w"], a[n + "gate_b"].reshape(1, 8)
    out[n + "w1"], out[n + "w2"] = a[n + "w1"], a[n + "w2"]
    out[n + "b1"] = a[n + "b1"].reshape(8, 4, 128).transpose(0, 2, 1)
    out[n + "b2"] = a[n + "b2"].reshape(8, 2, 128).transpose(0, 2, 1)
    n = "L1_xattn_"
    out[n + "w_q"], out[n + "w_proj"] = a[n + "w_q"], a[n + "w_proj"]
    out[n + "w_k"], out[n + "w_v"] = a[n + "w_kv"][:, :256], a[n + "w_kv"][:, 256:]
    out[n + "w_rel"] = np.repeat(a[n + "w_rel"].reshape(4, 4).T, 32, axis=0)
    n = "L1_attn_"
    out[n + "Wq"], out[n + "Wv"] = a[n + "Wq"].T, a[n + "Wv"].T
    out[n + "q_norm_w"], out[n + "v_norm_w"] = vec(a[n + "q_norm_w"].reshape(-1)), vec(a[n + "v_norm_w"].reshape(-1))
    n = "L1_ffn_"
    for w in ("Wq", "Wk", "Wv", "Wo", "Wg", "We"):
        out[n + w] = a[n + w]
    for b in ("bq", "bk", "bv", "bo", "g1", "be1", "g2", "be2"):
        out[n + b] = vec(a[n + b])
    out[n + "bg"] = a[n + "bg"].reshape(1, 8)
    out[n + "bexp"] = a[n + "bexp"].reshape(8, 2, 128).transpose(0, 2, 1)
    n = "L2_xattn_"
    out[n + "W_qv"], out[n + "w_sim"] = a[n + "W_qv"], vec(a[n + "w_sim"])
    out[n + "b_sim"], out[n + "b_qv"] = a[n + "b_sim"].reshape(1, 1), vec(a[n + "b_qv"])
    n = "L2_attn_"
    for w in ("W_Q", "W_K", "W_V"):
        out[n + w] = a[n + w]
    n = "L2_ffn_"
    out[n + "W_exp"], out[n + "W_con_t"] = a[n + "W_exp"], a[n + "W_con"].T
    out[n + "b_exp"] = a[n + "b_exp"].reshape(1, 1024)
    for w in ("up_weights", "down_weights"):
        out[n + w] = a[n + w].reshape(10, 2048)
    for b in ("up_bias", "b_con", "down_bias"):
        out[n + b] = vec(a[n + b])
    n = "L3_xattn_"
    out[n + "Wq"], out[n + "Wk"], out[n + "Wv"] = a[n + "Wq"].T, a[n + "Wk"], a[n + "Wv"].T
    for b in ("bq", "bk", "bv"):
        out[n + b] = vec(a[n + b])
    out[n + "betas"] = np.stack([a[n + "beta_risk"], a[n + "beta_prio"], a[n + "beta_impl"]]).reshape(1, 3)
    n = "L3_attn_"
    for w in "qkv":
        out[n + w + "_w"] = a[n + w + "_w"].reshape(1024, 256).T
        out[n + w + "_b"] = vec(a[n + w + "_b"].reshape(-1))
    out[n + "l_w"], out[n + "l_b"] = a[n + "l_w"].T, vec(a[n + "l_b"].reshape(-1))
    n = "L3_ffn_"
    out[n + "Wr"] = a[n + "Wr"]
    gate = np.concatenate([a[n + "Wg"], a[n + "Sg"].reshape(256, 2, 128).transpose(1, 0, 2)])
    up = np.concatenate([a[n + "Wu"], a[n + "Su"].reshape(256, 2, 128).transpose(1, 0, 2)])
    out[n + "Wgu"] = np.concatenate([gate, up], axis=2)
    out[n + "Wd"] = np.concatenate([a[n + "Wd"], a[n + "Sd"].reshape(2, 128, 256)])
    return {k: np.ascontiguousarray(v) for k, v in out.items()}


def kernel(**inputs):
    import numpy as np
    import concourse.bacc as bacc
    from concourse.bass_utils import run_bass_kernel_spmd

    arrays = {**laid_out(inputs), **shape_constants()}
    nc = bacc.Bacc("TRN2", target_bir_lowering=False, num_devices=1)
    dram = {k: nc.dram_tensor(f"in_{k}", v.shape, mybir.dt.from_np(v.dtype), kind="ExternalInput").ap()
            for k, v in arrays.items()}
    out = nc.dram_tensor("out_0_dram", (D, N), F32, kind="ExternalOutput").ap()
    scratch = {k: nc.dram_tensor(f"scratch_{k}", shape, F32, kind="Internal").ap()
               for k, shape in {"qkv": (3 * D, N), "seg_out": (D, N), "gates": (18, N), "tails": (B, D)}.items()}
    perceiver(nc, dram, out, scratch)
    r = run_bass_kernel_spmd(nc, [{f"in_{k}": v for k, v in arrays.items()}], core_ids=[0])
    return r.results[0]["out_0_dram"].T.reshape(B, S, D)
```

```python
import concourse.bass as bass
from concourse import mybir
from contextlib import ExitStack, contextmanager

P = 128
D = 256
KC = D // P
B = 64
S = 32
N = B * S
M = 257
BLK = 512
NB = N // BLK
GT = 128
NG = N // GT
KCH = [(0, 128), (128, 128), (256, 1)]
HALF = BLK // 2

START = 1

F32 = mybir.dt.float32
F32R = mybir.dt.float32r
U32 = mybir.dt.uint32
U8 = mybir.dt.uint8
ALU = mybir.AluOpType
ACT = mybir.ActivationFunctionType
AX = mybir.AxisListType.X


CONSTS = ["ident", "mask_block", "mask_causal", "mask_lower", "mask_segments", "head_of_8", "head_of_2",
          "own_head", "batch_of_4", "query_sel", "same_head",
          "iota16", "ones", "positions"]




class Core:

    BANK = 30

    def __init__(self, nc, ctx, dram):
        self.nc, self.ctx, self.dram = nc, ctx, dram
        self.banks = [[ctx.enter_context(nc.semaphore(f"bank{b}_{i}")) for i in range(self.BANK)]
                      for b in range(2)]
        self.turn = 0
        self.pending = []
        self.used = [self.BANK, self.BANK]
        with nc.Block(no_gpsimd_drain=True) as block:
            @block.gpsimd
            def _(pool):
                for s in self.banks[0]:
                    pool.sem_inc(s, START)
        self.banks8 = ctx.enter_context(nc.psum_tensor("banks8", [P, 8, BLK], F32))
        self.psum = [self.banks8[:, i, :] for i in range(8)]
        self.x = self.keep("x_T", [P, KC, N])
        self.consts = {name: self.keep(name, list(dram[name].shape)) for name in CONSTS}
        self.ident = self.consts["ident"]
        self.mean_w = self.keep("mean_w", [P, P])
        self.eps = self.keep("eps", [P, 2])

    def keep(self, name, shape, dt=F32):
        return self.ctx.enter_context(self.nc.sbuf_tensor(f"sb_{name}", shape, dt))


@contextmanager
def phase(core, *names):
    nc = core.nc
    assert len(names) <= core.BANK
    bank, old = core.banks[core.turn % 2], core.banks[(core.turn + 1) % 2]
    stale = old if core.turn == 0 else old[:core.used[(core.turn + 1) % 2]]
    core.used[core.turn % 2] = max(len(names), 1)
    with nc.Block(no_gpsimd_drain=True) as block:
        @block.gpsimd
        def _(pool):
            for s in stale:
                if core.turn:
                    pool.sem_clear(s)
                pool.sem_inc(s, START)
        yield (block, *bank[:len(names)])
    core.turn += 1


def bcast(ap, n, at=1):
    a = ap.unsqueeze(at)
    shape = list(a.shape)
    shape[at] = n
    return a.broadcast_to(shape)


def blk(t, width=BLK):
    return bass.ds(t * width, width)




def low_part(nc, low, x, high):
    return nc.vector.tensor_tensor(low, x, high.bitcast(F32), ALU.subtract)


def split_products(pe, to, weights, streams):
    last = 3 * len(weights) - 1
    n = 0
    for (w_high, w_low), (x_high, x_low) in zip(weights, streams):
        for w, x in ((w_high, x_high), (w_high, x_low), (w_low, x_high)):
            ins = pe.matmul(to, w, x, start=(n == 0), stop=(n == last))
            n += 1
    return ins


def layer_norm(core, src, dst, scale_shift=None, add=None, jobs=(), mc=KC):
    nc = core.nc
    assert not jobs or (scale_shift is None and add is None)
    pairs = core.pending
    products = [(w, out, bias, m) for w, out, bias in jobs for m in range(mc)]
    PER = len(products)
    with ExitStack() as mem:
        def sb(name, shape):
            return mem.enter_context(nc.sbuf_tensor(f"{name}_{core.turn}", shape, F32))
        cen, sq, diag = sb("cen", [P, KC, N]), sb("sq", [P, 2, KC, BLK]), sb("diag", [P, 2, 4, P])
        std, rstd = sb("std", [P, NG]), sb("rstd", [P, NG])
        (block, mean_ready, centred, squared, var_ready, std_ready, rstd_ready, diag_ready, spread, scaled,
         done, loaded, product_ready, taken_act, taken_dve) = mem.enter_context(
            phase(core, "mean_ready", "centred", "squared", "var_ready", "std_ready", "rstd_ready",
                  "diag_ready", "spread", "scaled", "done", "loaded", "product_ready", "taken_act", "taken_dve"))
        load_pending(core, block, loaded)

        def spread_bank(t):
            return core.psum[3 if jobs else 4 + t]

        def take(eng, taken, which, t):
            for n, (w, out, bias, m) in enumerate(products):
                i = t * PER + n
                if n % 2 != which:
                    continue
                eng.wait_ge(product_ready, START + i + 1)
                b = 0.0 if bias is None else bias[:, m:m + 1]
                if which == 0:
                    ins = nc.scalar.activation(out[:, m, blk(t)], core.psum[4 + i % 4], ACT.Identity, bias=b)
                else:
                    ins = nc.vector.tensor_scalar(out[:, m, blk(t)], core.psum[4 + i % 4], b, None, ALU.add)
                ins.then_inc(taken, 1)

        @block.tensor
        def _(pe):
            def project(t):
                pe.wait_ge(scaled, START + t + 1)
                pe.wait_ge(loaded, START + 16 * len(pairs))
                for n, (w, out, bias, m) in enumerate(products):
                    i = t * PER + n
                    if i >= 4:
                        pe.wait_ge(taken_act if i % 2 == 0 else taken_dve, START + (i - 4) // 2 + 1)
                    for k in range(KC):
                        ins = pe.matmul(core.psum[4 + i % 4], w[:, k, m * P:(m + 1) * P], dst[:, k, blk(t)],
                                        start=(k == 0), stop=(k == KC - 1))
                    ins.then_inc(product_ready, 1)

            def mean(t):
                if t >= 2:
                    pe.wait_ge(centred, START + t - 1)
                for k in range(KC):
                    ins = pe.matmul(core.psum[t % 2], core.mean_w[:, :], src[:, k, blk(t)], start=(k == 0),
                                    stop=(k == KC - 1))
                ins.then_inc(mean_ready, 1)

            def variance(t):
                pe.wait_ge(squared, START + t + 1)
                if t >= 1:
                    pe.wait_ge(std_ready, START + t)
                for g in range(4):
                    for k in range(KC):
                        ins = pe.matmul(core.psum[2][:, g:g + 1], sq[:, t % 2, k, g * P:(g + 1) * P],
                                        core.mean_w[:, 0:1], start=(k == 0), stop=(k == KC - 1))
                ins.then_inc(var_ready, 1)

            def spread_out(t):
                pe.wait_ge(diag_ready, START + t + 1)
                if jobs and t >= 1:
                    pe.wait_ge(scaled, START + t)
                pe.matmul(spread_bank(t), core.consts["ones"][:, :],
                          diag[:, t % 2, :, :].rearrange("p g w -> p (g w)"), start=True, stop=True)\
                  .then_inc(spread, 1)

            mean(0)
            mean(1)
            for t in range(NB):
                variance(t)
                if t + 2 < NB:
                    mean(t + 2)
                if t >= 1:
                    spread_out(t - 1)
                if jobs and t >= 2:
                    project(t - 2)
            spread_out(NB - 1)
            if jobs:
                project(NB - 2)
                project(NB - 1)

        @block.scalar
        def _(act):
            def square(t):
                act.wait_ge(centred, START + t + 1)
                if t >= 2:
                    act.wait_ge(var_ready, START + t - 1)
                nc.scalar.activation(sq[:, t % 2, :, :], cen[:, :, blk(t)], ACT.Square).then_inc(squared, 1)

            def shift(t):
                for k in range(KC):
                    act.wait_ge(scaled, START + t * KC + k + 1)
                    nc.scalar.activation(dst[:, k, blk(t)], cen[:, k, blk(t)], ACT.Identity,
                                         bias=scale_shift[1][:, k:k + 1]).then_inc(done, 1)

            square(0)
            square(1)
            for t in range(NB):
                act.wait_ge(var_ready, START + t + 1)
                nc.scalar.activation(std[:, 4 * t:4 * t + 4], core.psum[2][:, 0:4], ACT.Sqrt,
                                     bias=core.eps[:, 0:1]).then_inc(std_ready, 1)
                if t + 2 < NB:
                    square(t + 2)
                if t >= 2 and scale_shift is not None and add is None:
                    shift(t - 2)
                if t >= 2:
                    take(act, taken_act, 0, t - 2)
            for t in (NB - 2, NB - 1):
                take(act, taken_act, 0, t)
            if scale_shift is not None and add is None:
                shift(NB - 2)
                shift(NB - 1)

        @block.gpsimd
        def _(pool):
            for t in range(NB):
                pool.wait_ge(rstd_ready, START + t + 1)
                if t >= 2:
                    pool.wait_ge(spread, START + t - 1)
                nc.gpsimd.tensor_tensor(diag[:, t % 2, :, :], bcast(core.ident[:, :], 4),
                                        bcast(rstd[:, 4 * t:4 * t + 4], P, 2), ALU.mult).then_inc(diag_ready, 1)

        @block.vector
        def _(dve):
            def centre(t):
                dve.wait_ge(mean_ready, START + t + 1)
                nc.vector.tensor_tensor(cen[:, :, blk(t)], src[:, :, blk(t)], bcast(core.psum[t % 2], KC),
                                        ALU.subtract).then_inc(centred, 1)

            def scale(t):
                dve.wait_ge(centred, START + t + 1)
                dve.wait_ge(spread, START + t + 1)
                if scale_shift is None:
                    out = dst if add is None else cen
                    nc.vector.tensor_tensor(out[:, :, blk(t)], cen[:, :, blk(t)], bcast(spread_bank(t), KC),
                                            ALU.mult).then_inc(scaled, 1)
                    return
                g, b = scale_shift
                for k in range(KC):
                    nc.vector.scalar_tensor_tensor(out=cen[:, k, blk(t)], in0=spread_bank(t),
                                                   scalar=g[:, k:k + 1], in1=cen[:, k, blk(t)], op0=ALU.mult,
                                                   op1=ALU.mult).then_inc(scaled, 1)
                    if add is not None:
                        dve.wait_ge(scaled, START + t * KC + k + 1)
                        nc.vector.scalar_tensor_tensor(out=dst[:, k, blk(t)], in0=cen[:, k, blk(t)],
                                                       scalar=b[:, k:k + 1], in1=add[:, k, blk(t)], op0=ALU.add,
                                                       op1=ALU.add).then_inc(done, 1)

            centre(0)
            centre(1)
            for t in range(NB):
                dve.wait_ge(std_ready, START + t + 1)
                nc.vector.reciprocal(rstd[:, 4 * t:4 * t + 4], std[:, 4 * t:4 * t + 4]).then_inc(rstd_ready, 1)
                if t + 2 < NB:
                    centre(t + 2)
                if t >= 1:
                    scale(t - 1)
                if t >= 2:
                    take(dve, taken_dve, 1, t - 2)
            scale(NB - 1)
            for t in (NB - 2, NB - 1):
                take(dve, taken_dve, 1, t)


def linear(core, w, src, dst, bias=None, kind="copy", kc=KC, mc=KC):
    linears(core, (w, src, dst, bias), kind=kind, kc=kc, mc=mc)


def linears(core, *jobs, kind="copy", kc=KC, mc=KC):
    nc = core.nc
    takers = {"copy": 2, "residual": 1}[kind]
    unroll = 2 if mc <= 4 else 1
    products = NB * mc
    per = unroll * mc // takers
    with phase(core, "product_ready", "free_act", "free_dve", "loaded") as (block, ready, free_act, free_dve, loaded):
        load_pending(core, block, loaded)

        @block.tensor
        def _(pe):
            for i, (w, src, dst, bias) in enumerate(jobs):
                with pe.Fori(0, NB // unroll) as r:
                    for n in range(unroll * mc):
                        u, m = n // mc, n % mc
                        free = free_act if takers == 2 and n % 2 == 0 else free_dve
                        pe.wait_ge(free, START + r * per + n // takers + 1 + i * products // takers)
                        for k in range(kc):
                            x = src[k // KC][:, k % KC, blk(r * unroll + u)] if isinstance(src, tuple) else \
                                src[:, k, blk(r * unroll + u)]
                            ins = pe.matmul(core.psum[n][:, :], w[:, k, m * P:(m + 1) * P], x, start=(k == 0),
                                            stop=(k == kc - 1))
                        ins.then_inc(ready, 1)

        def take(eng, which, free):
            eng.sem_inc(free, per)
            for i, (w, src, dst, bias) in enumerate(jobs):
                with eng.Fori(0, NB // unroll) as r:
                    for n in range(unroll * mc):
                        u, m = n // mc, n % mc
                        if takers == 2 and n % 2 != which:
                            continue
                        eng.wait_ge(ready, START + r * unroll * mc + n + 1 + i * products)
                        out, got = dst[:, m, blk(r * unroll + u)], core.psum[n][:, :]
                        b = 0.0 if bias is None else bias[:, m:m + 1]
                        if which == 0:
                            ins = nc.scalar.activation(out, got, ACT.Identity, bias=b)
                        elif kind == "residual":
                            ins = nc.vector.scalar_tensor_tensor(out=out, in0=got, scalar=b, in1=out,
                                                                 op0=ALU.add, op1=ALU.add)
                        else:
                            ins = nc.vector.tensor_scalar(out, got, b, None, ALU.add)
                        ins.then_inc(free, 1)

        if kind != "residual":
            @block.scalar
            def _(act):
                take(act, 0, free_act)

        @block.vector
        def _(dve):
            take(dve, 1, free_dve)


def start(core):
    nc = core.nc
    with phase(core, "loaded", "set") as (block, loaded, done):
        @block.sync
        def _(sp):
            sp.dma_start(core.x[:, :, :], core.dram["x"].rearrange("(k p) n -> p k n", p=P)).then_inc(loaded, 16)
            for i, (name, tile) in enumerate(core.consts.items()):
                sp.dma_start(tile[:, :], core.dram[name]).then_inc(loaded, 16)
            sp.wait_ge(loaded, START + 16 * (1 + len(core.consts)))

        @block.gpsimd
        def _(pool):
            nc.gpsimd.memset(core.mean_w[:, :], 1.0 / D).then_inc(done, 1)
            nc.gpsimd.memset(core.eps[:, 0:1], 1e-5).then_inc(done, 1)
            nc.gpsimd.memset(core.eps[:, 1:2], 1e-8).then_inc(done, 1)
            pool.wait_ge(done, START + 3)


def load(core, *pairs):
    with phase(core, "loaded") as (block, loaded):
        @block.sync
        def _(sp):
            for tile, source in pairs:
                sp.dma_start(tile, source).then_inc(loaded, 16)
            sp.wait_ge(loaded, START + 16 * len(pairs))


def load_pending(core, block, loaded):
    pairs, core.pending = core.pending, []

    @block.sync
    def _(sp):
        for tile, source in pairs:
            sp.dma_start(tile, source).then_inc(loaded, 16)
        if pairs:
            sp.wait_ge(loaded, START + 16 * len(pairs))


def chunks(ap):
    return ap.rearrange("(k p) n -> p k n", p=P)


def store(core, src, out):
    with phase(core, "stored") as (block, stored):
        @block.sync
        def _(sp):
            sp.dma_start(chunks(out), src[:, :, :]).then_inc(stored, 16)
            sp.wait_ge(stored, START + 16)


def self_attention(core, kind, still, moving, v, out, chunk_n, scale=1.0, mask=None, residual=False):
    nc = core.nc
    seg = kind == "segments"
    dh = {"heads": 16, "linear": 16, "columns": 64}.get(kind, 0)
    hp = P // dh if dh else 0
    units = 16 if seg else chunk_n * hp
    Q = units // 4
    softmax, turns = kind != "linear", kind != "columns"
    outs = Q if seg else chunk_n
    AHEAD, TOTAL = 3, NG * Q
    with ExitStack() as mem:
        def sb(name, shape):
            return mem.enter_context(nc.sbuf_tensor(f"{name}_{core.turn}", shape, F32))
        if seg:
            q_e, v_e = sb("q_e", [16, 16, GT]), sb("v_e", [16, 16, GT])
            k_e, o_e = ([sb(f"{n}{j}", [16, 16, GT]) for j in range(2)] for n in ("k_e", "o_e"))
            a_st, v_st = ([sb(f"{n}{j}", [16, 16, 16, 8]) for j in range(2)] for n in ("q_rows", "v_cols"))
            v_use = [sb(f"v_rows{j}", [P, 16, 16]) for j in range(2)]
        else:
            a_st = [sb(f"a_pad{j}", [P, units, GT]) for j in range(2)]
            v_st = [sb(f"v_st{j}", [P, chunk_n, GT]) for j in range(2)]
            v_use = [sb(f"v_pad{j}", [P, chunk_n, hp, P + dh]) for j in range(2)]
        s = sb("s", [P, 4, 4, P]) if softmax else None
        p = sb("p", [P, 4, 4, P])
        pt = sb("pt", [P, 2, 4, P]) if turns else None
        top, neg, total, inv = (sb(n, [P, 4, 4]) for n in ("top", "neg", "total", "inv"))
        (block, staged, v_staged, zeroed, v_turned, v_ready, scores_ready, masked, topped, negated, exped,
         inverted, normed, p_turned, pt_ready, out_ready, out_taken, stored0, stored1, arrived, passed) = \
            mem.enter_context(phase(
                core, "staged", "v_staged", "zeroed", "v_turned", "v_ready", "scores_ready", "masked",
                "topped", "negated", "exped", "inverted", "normed", "p_turned", "pt_ready", "out_ready",
                "out_taken", "stored0", "stored1", "arrived", "passed"))
        stored = [stored0, stored1]
        n_staged = 1 if seg else chunk_n
        heads_of = core.consts["head_of_8" if dh == 16 else "head_of_2"]
        normal = masked if kind == "linear" else normed
        v_bank = core.psum[7]

        def rounds(eng, step):
            with eng.Fori(0, NG // 2 - 1) as r:
                for j in range(2):
                    for n in range(Q):
                        step(2 * r + j, j, n, False)
            for j in range(2):
                for n in range(Q):
                    step(NG - 2 + j, j, n, True)

        def ahead(i, j, n, by, last):
            d, n2 = (n + by) // Q, (n + by) % Q
            return None if last and i + d >= NG else (i + d, (j + d) % 2, n2)

        def slot(j, n, of=4):
            return (j * Q + n) % of

        def finished(n):
            return [n] if seg else [c for c in range(chunk_n) if (c + 1) * hp - 1 in range(4 * n, 4 * n + 4)]

        if not seg:
            load_pending(core, block, arrived)
        if seg:
            @block.sync
            def _(sp):
                def part(d, g):
                    return d.rearrange("(s e) n -> e s n", e=16)[:, :, blk(g, GT)]

                def fetch(g, j):
                    for tile, d in ((q_e, still), (k_e[j], moving), (v_e, v)):
                        sp.dma_start(tile[:, :, :], part(d, g)).then_inc(arrived, 16)

                def keep(g, j):
                    sp.wait_ge(out_taken, START + (g + 1) * Q)
                    sp.sem_inc(passed, 1)
                    sp.dma_start(part(out, g), o_e[j][:, :, :]).then_inc(stored[j], 16)

                fetch(0, 0)
                sp.wait_ge(staged, START + 1)
                sp.wait_ge(v_staged, START + 1)
                fetch(1, 1)
                with sp.Fori(0, NG // 2 - 1) as r:
                    for j in range(2):
                        g = 2 * r + j
                        sp.wait_ge(staged, START + g + 2)
                        sp.sem_inc(passed, 1)
                        sp.wait_ge(v_staged, START + g + 2)
                        sp.sem_inc(passed, 1)
                        sp.wait_ge(scores_ready, START + (g + 1) * Q)
                        sp.sem_inc(passed, 1)
                        fetch(g + 2, j)
                        keep(g, j)
                for j in range(2):
                    keep(NG - 2 + j, j)
                for j in range(2):
                    sp.wait_ge(stored[j], START + 16 * (NG // 2))

            @block.gpsimd
            def _(pool):
                def stage(g, j):
                    pool.wait_ge(arrived, START + (g + 1) * 48)
                    pool.sem_inc(passed, 1)
                    nc.gpsimd.tensor_copy(a_st[j][:, :, :, :],
                                          q_e[:, :, :].rearrange("e s (u t) -> e u s t", t=8)).then_inc(staged, 1)

                for j in range(2):
                    stage(j, j)
                with pool.Fori(0, NG // 2 - 1) as r:
                    for j in range(2):
                        pool.wait_ge(scores_ready, START + (2 * r + j + 1) * Q)
                        stage(2 * r + j + 2, j)
        else:
            @block.gpsimd
            def _(pool):
                def stage(g, j):
                    nc.gpsimd.tensor_copy(v_st[j][:, :, :], v[:, :, blk(g, GT)]).then_inc(v_staged, 1)
                    for c in range(chunk_n):
                        nc.gpsimd.tensor_tensor(
                            a_st[j][:, c * hp:(c + 1) * hp, :], bcast(still[:, c, blk(g, GT)], hp),
                            bcast(heads_of[:, 0:hp], GT, 2), ALU.mult).then_inc(staged, 1)

                stage(0, 0)
                for j in range(2):
                    nc.gpsimd.memset(v_use[j][:, :, :, :], 0.0).then_inc(zeroed, 1)
                stage(1, 1)
                with pool.Fori(0, NG // 2 - 1) as r:
                    for j in range(2):
                        pool.wait_ge(scores_ready, START + (2 * r + j + 1) * Q)
                        pool.wait_ge(v_turned, START + 2 * r + j + 1)
                        pool.sem_inc(passed, 1)
                        stage(2 * r + j + 2, j)

        @block.tensor
        def _(pe):
            def values(g, j):
                pe.wait_ge(v_staged, START + g + 1)
                pe.wait_ge(v_ready, START + g)
                if seg:
                    for u in range(units):
                        ins = pe.matmul(v_bank[:, u * 16:(u + 1) * 16],
                                        v_st[j][:, u, :, :].rearrange("e s t -> e (s t)"),
                                        core.ident[0:16, 0:16], start=True, stop=True)
                else:
                    for c in range(chunk_n):
                        ins = pe.transpose(v_bank[:, c * P:(c + 1) * P], v_st[j][:, c, :], core.ident[:, :])
                ins.then_inc(v_turned, 1)

            def scores(g, j, n):
                pe.wait_ge(staged, START + (g + 1) * n_staged)
                for u in range(4 * n, 4 * n + 4):
                    to = core.psum[slot(j, n)][:, (u % 4) * P:(u % 4 + 1) * P]
                    if seg:
                        ins = pe.matmul(to, a_st[j][:, u, :, :].rearrange("e s t -> e (s t)"),
                                        k_e[j][:, :, 8 * u:8 * u + 8], start=True, stop=True)
                    else:
                        ins = pe.matmul(to, a_st[j][:, u, :], moving[:, u // hp, blk(g, GT)], start=True,
                                        stop=True)
                ins.then_inc(scores_ready, 1)

            def result(g, j, n, last):
                if turns:
                    pe.wait_ge(pt_ready, START + g * Q + n + 1)
                else:
                    pe.wait_ge(normal, START + g * Q + n + 1)
                if n == 0:
                    pe.wait_ge(v_ready, START + g + 1)
                for u in range(4 * n, 4 * n + 4):
                    pu = pt[:, slot(j, n, 2), u % 4, :] if turns else p[:, slot(j, n), u % 4, :]
                    o = n if seg else u // hp
                    first = u % 4 == 0 if seg else u % hp == 0
                    if first:
                        pe.wait_ge(out_taken, START + g * outs + max(0, o - 1))
                        if o == 1 and not (last and g == NG - 1):
                            pe.wait_ge(v_ready, START + g + 2)
                    if seg:
                        ins = pe.matmul(core.psum[6 + o % 2][0:16, (u % 4) * P:(u % 4 + 1) * P],
                                        v_use[j][:, u, :], pu, start=True, stop=True)
                        done = u % 4 == 3
                    else:
                        h = u % hp
                        at = o * hp * (P + dh) + h * P
                        flat = v_use[j][:, :, :, :].rearrange("p c h w -> p (c h w)")
                        ins = pe.matmul(core.psum[6 + o % 2][:, 0:GT], flat[:, at:at + P], pu, start=(h == 0),
                                        stop=(h == hp - 1))
                        done = h == hp - 1
                    if done:
                        ins.then_inc(out_ready, 1)

            def step(i, j, n, last):
                if turns:
                    pe.wait_ge(normal, START + i * Q + n + 1)
                    for u in range(4):
                        ins = pe.transpose(core.psum[4 + slot(j, n, 2)][:, u * P:(u + 1) * P],
                                           p[:, slot(j, n), u, :], core.ident[:, :])
                    ins.then_inc(p_turned, 1)
                later = ahead(i, j, n, AHEAD, last)
                if later:
                    pe.wait_ge(masked, START + i * Q + n)
                    scores(*later)
                if n == 0 and not (last and i == NG - 1):
                    pe.wait_ge(out_taken, START + i * outs)
                    values(i + 1, 1 - j)
                result(i, j, n, last)

            values(0, 0)
            for m in range(AHEAD):
                scores(m // Q, m // Q % 2, m % Q)
            rounds(pe, step)

        @block.scalar
        def _(act):
            def values(g, j):
                act.wait_ge(v_turned, START + g + 1)
                if seg:
                    ins = nc.scalar.copy(v_use[j][:, :, :], v_bank[:, 0:256].rearrange("p (u e) -> p u e", u=16))
                else:
                    for c in range(chunk_n):
                        ins = nc.scalar.copy(v_use[j][:, c, :, 0:dh],
                                             v_bank[:, c * P:(c + 1) * P].rearrange("p (h f) -> p h f", h=hp))
                ins.then_inc(v_ready, 1)

            def arrange(g, j):
                act.wait_ge(arrived, START + (g + 1) * 48)
                nc.scalar.copy(v_st[j][:, :, :, :], v_e[:, :, :].rearrange("e s (u t) -> e u s t", t=8))\
                  .then_inc(v_staged, 1)

            def exps(g, j, n):
                act.wait_ge(negated, START + g * Q + n + 1)
                sl = slot(j, n)
                for u in range(4):
                    ins = nc.scalar.activation(p[:, sl, u, :], s[:, sl, u, :], ACT.Exp, bias=neg[:, sl, u:u + 1],
                                               scale=scale, accum_out=total[:, sl, u:u + 1])
                ins.then_inc(exped, 1)

            def step(i, j, n, last):
                if turns:
                    act.wait_ge(p_turned, START + i * Q + n + 1)
                    nc.scalar.copy(pt[:, slot(j, n, 2), :, :],
                                   core.psum[4 + slot(j, n, 2)].rearrange("p (u w) -> p u w", u=4))\
                      .then_inc(pt_ready, 1)
                if n == 0 and not (last and i == NG - 1):
                    values(i + 1, 1 - j)
                later = ahead(i, j, n, 2, last)
                if softmax and later:
                    exps(*later)
                if seg and n == 2 and not last:
                    arrange(i + 2, j)

            if seg:
                arrange(0, 0)
            else:
                act.wait_ge(zeroed, START + 2)
            values(0, 0)
            if seg:
                arrange(1, 1)
            if softmax:
                for m in range(2):
                    exps(m // Q, m // Q % 2, m % Q)
            rounds(act, step)

        @block.vector
        def _(dve):
            def mask_quad(g, j, n):
                dve.wait_ge(scores_ready, START + g * Q + n + 1)
                sl = slot(j, n)
                sc = core.psum[sl].rearrange("p (u w) -> p u w", u=4)
                if not softmax:
                    nc.vector.tensor_tensor(p[:, sl, :, :], sc, bcast(mask[:, :], 4), ALU.mult)\
                      .then_inc(masked, 1)
                    return
                nc.vector.tensor_tensor(s[:, sl, :, :], sc, bcast(mask[:, :], 4), ALU.add).then_inc(masked, 1)
                dve.wait_ge(masked, START + g * Q + n + 1)
                nc.vector.tensor_reduce(top[:, sl, :], s[:, sl, :, :], AX, ALU.max).then_inc(topped, 1)
                dve.wait_ge(topped, START + g * Q + n + 1)
                nc.vector.tensor_scalar(neg[:, sl, :], top[:, sl, :], -scale, None, ALU.mult)\
                  .then_inc(negated, 1)

            def norm(g, j, n):
                sl = slot(j, n)
                dve.wait_ge(exped, START + g * Q + n + 1)
                nc.vector.reciprocal(inv[:, sl, :], total[:, sl, :]).then_inc(inverted, 1)
                dve.wait_ge(inverted, START + g * Q + n + 1)
                nc.vector.tensor_tensor(p[:, sl, :, :], p[:, sl, :, :], bcast(inv[:, sl, :], P, 2), ALU.mult)\
                  .then_inc(normed, 1)

            def take(g, j, o):
                dve.wait_ge(out_ready, START + g * outs + o + 1)
                bank = core.psum[6 + o % 2]
                if seg:
                    if o == 0:
                        dve.wait_ge(stored[j], START + (g - j) * 8)
                    nc.vector.tensor_copy(
                        o_e[j][:, :, 32 * o:32 * o + 32].rearrange("e s (u t) -> e u s t", u=4),
                        bank[0:16, :].rearrange("e (u s t) -> e u s t", u=4, t=8)).then_inc(out_taken, 1)
                elif residual:
                    nc.vector.tensor_tensor(out[:, o, blk(g, GT)], out[:, o, blk(g, GT)], bank[:, 0:GT], ALU.add)\
                      .then_inc(out_taken, 1)
                else:
                    nc.vector.tensor_copy(out[:, o, blk(g, GT)], bank[:, 0:GT]).then_inc(out_taken, 1)

            def step(i, j, n, last):
                later = ahead(i, j, n, 2, last)
                if later:
                    mask_quad(*later)
                later = ahead(i, j, n, 1, last)
                if softmax and later:
                    norm(*later)
                for o in finished(n):
                    take(i, j, o)

            for m in range(2):
                mask_quad(m // Q, m // Q % 2, m % Q)
            if softmax:
                norm(0, 0, 0)
            rounds(dve, step)


def single_attention(core, q, k, x, wv, out, scale, mask):
    nc = core.nc
    with ExitStack() as mem:
        def sb(name, *shape):
            return [mem.enter_context(nc.sbuf_tensor(f"{name}{j}_{core.turn}", list(shape), F32)) for j in range(2)]
        v_tok, s, p, pt = sb("v_tok", P, 4, D), sb("s", P, 4, P), sb("p", P, 4, P), sb("pt", P, 4, P)
        top, neg, total, inv = (sb(n, P, 4) for n in ("top", "neg", "total", "inv"))
        (block, v_made, v_ready, scores_ready, masked, topped, negated, exped, inverted, normed, p_turned,
         pt_ready, out_ready, out_taken, loaded) = mem.enter_context(
            phase(core, "v_made", "v_ready", "scores_ready", "masked", "topped", "negated", "exped", "inverted",
                  "normed", "p_turned", "pt_ready", "out_ready", "out_taken", "loaded"))
        load_pending(core, block, loaded)

        def tokens(t, u):
            return slice(t * BLK + u * P, t * BLK + (u + 1) * P)

        @block.tensor
        def _(pe):
            def scores(t):
                if t >= 2:
                    pe.wait_ge(masked, START + t - 1)
                for u in range(4):
                    for c in range(KC):
                        ins = pe.matmul(core.psum[t % 2][:, u * P:(u + 1) * P], q[:, c, tokens(t, u)],
                                        k[:, c, tokens(t, u)], start=(c == 0), stop=(c == KC - 1))
                ins.then_inc(scores_ready, 1)

            def values(t):
                if t >= 1:
                    pe.wait_ge(v_ready, START + t)
                for u in range(4):
                    for c in range(KC):
                        ins = pe.matmul(core.psum[4 + u // 2][:, u % 2 * D:(u % 2 + 1) * D], x[:, c, tokens(t, u)],
                                        wv[:, c, :], start=(c == 0), stop=(c == KC - 1))
                ins.then_inc(v_made, 1)

            def result(t):
                pe.wait_ge(normed, START + t + 1)
                for u in range(4):
                    ins = pe.transpose(core.psum[2 + t % 2][:, u * P:(u + 1) * P], p[t % 2][:, u, :],
                                       core.ident[:, :])
                ins.then_inc(p_turned, 1)
                if t + 2 < NB:
                    scores(t + 2)
                if t + 1 < NB:
                    values(t + 1)
                pe.wait_ge(pt_ready, START + t + 1)
                pe.wait_ge(v_ready, START + t + 1)
                if t >= 1:
                    pe.wait_ge(out_taken, START + t)
                for f in range(KC):
                    for u in range(4):
                        ins = pe.matmul(core.psum[6 + f][:, u * P:(u + 1) * P], v_tok[t % 2][:, u, f * P:(f + 1) * P],
                                        pt[t % 2][:, u, :], start=True, stop=True)
                ins.then_inc(out_ready, 1)

            scores(0)
            scores(1)
            values(0)
            for t in range(NB):
                result(t)

        @block.scalar
        def _(act):
            def exps(t):
                act.wait_ge(negated, START + t + 1)
                if t >= 2:
                    act.wait_ge(p_turned, START + t - 1)
                for u in range(4):
                    ins = nc.scalar.activation(p[t % 2][:, u, :], s[t % 2][:, u, :], ACT.Exp,
                                               bias=neg[t % 2][:, u:u + 1], scale=scale,
                                               accum_out=total[t % 2][:, u:u + 1])
                ins.then_inc(exped, 1)

            def values(t):
                act.wait_ge(v_made, START + t + 1)
                if t >= 2:
                    act.wait_ge(out_ready, START + t - 1)
                nc.scalar.copy(v_tok[t % 2][:, :, :], core.banks8[:, 4:6, :].rearrange("p b (u f) -> p (b u) f", u=2))\
                  .then_inc(v_ready, 1)

            exps(0)
            values(0)
            exps(1)
            for t in range(NB):
                act.wait_ge(p_turned, START + t + 1)
                nc.scalar.copy(pt[t % 2][:, :, :], core.psum[2 + t % 2].rearrange("p (u w) -> p u w", u=4))\
                  .then_inc(pt_ready, 1)
                if t + 1 < NB:
                    values(t + 1)
                if t + 2 < NB:
                    exps(t + 2)

        @block.vector
        def _(dve):
            def softmax(t):
                dve.wait_ge(scores_ready, START + t + 1)
                if t >= 2:
                    dve.wait_ge(exped, START + t - 1)
                j = t % 2
                nc.vector.tensor_tensor(s[j][:, :, :], core.psum[j].rearrange("p (u w) -> p u w", u=4),
                                        bcast(mask[:, :], 4), ALU.add).then_inc(masked, 1)
                dve.wait_ge(masked, START + t + 1)
                nc.vector.tensor_reduce(top[j][:, :], s[j][:, :, :], AX, ALU.max).then_inc(topped, 1)
                dve.wait_ge(topped, START + t + 1)
                nc.vector.tensor_scalar(neg[j][:, :], top[j][:, :], -scale, None, ALU.mult).then_inc(negated, 1)

            def norm(t):
                dve.wait_ge(exped, START + t + 1)
                j = t % 2
                nc.vector.reciprocal(inv[j][:, :], total[j][:, :]).then_inc(inverted, 1)
                dve.wait_ge(inverted, START + t + 1)
                nc.vector.tensor_tensor(p[j][:, :, :], p[j][:, :, :], bcast(inv[j][:, :], P, 2), ALU.mult)\
                  .then_inc(normed, 1)

            softmax(0)
            softmax(1)
            norm(0)
            for t in range(NB):
                if t + 1 < NB:
                    norm(t + 1)
                if t + 2 < NB:
                    softmax(t + 2)
                dve.wait_ge(out_ready, START + t + 1)
                nc.vector.tensor_tensor(out[:, :, blk(t)], out[:, :, blk(t)], core.banks8[:, 6:8, :], ALU.add)\
                  .then_inc(out_taken, 1)



def tail_values(core, wv, tails):
    nc = core.nc
    with ExitStack() as mem:
        last = mem.enter_context(nc.sbuf_tensor(f"last_{core.turn}", [P, KC, B], F32))
        v = mem.enter_context(nc.sbuf_tensor(f"v_last_{core.turn}", [B, D], F32))
        block, loaded, made, taken, kept = mem.enter_context(phase(core, "loaded", "made", "taken", "kept"))

        @block.sync
        def _(sp):
            sp.dma_start(last[:, :, :], chunks(core.dram["ctx_last_t"])).then_inc(loaded, 16)
            sp.wait_ge(taken, START + 1)
            sp.dma_start(tails, v[:, :]).then_inc(kept, 16)
            sp.wait_ge(kept, START + 16)

        @block.tensor
        def _(pe):
            pe.wait_ge(loaded, START + 16)
            for k in range(KC):
                ins = pe.matmul(core.psum[0][0:B, 0:D], last[:, k, :], wv[:, k, :], start=(k == 0),
                                stop=(k == KC - 1))
            ins.then_inc(made, 1)

        @block.vector
        def _(dve):
            dve.wait_ge(made, START + 1)
            nc.vector.tensor_copy(v[:, :], core.psum[0][0:B, 0:D]).then_inc(taken, 1)


def cross_attention(core, q, wk, wv, out, ctx_t, tails, mask=None, rel=None):
    nc = core.nc
    SC = 0.25
    masked = mask is not None
    with ExitStack() as mem:
        def sb(name, shape, dt=F32):
            return mem.enter_context(nc.sbuf_tensor(f"{name}_{core.turn}", shape, dt))
        ctx_sb = [sb(f"ctx{j}", [P, KC, M]) for j in range(2)]
        q_pad = [sb(f"q_pad{j}", [P, 16, S]) for j in range(2)]
        k_t = [sb(f"k_t{j}", [P, KC, M]) for j in range(2)]
        if masked:
            hide8 = [sb(f"hide8{j}", [P, M], U8) for j in range(2)]
            show = [sb(f"show{j}", [P, M]) for j in range(2)]
            hidden = [sb(f"hidden{j}", [P, M]) for j in range(2)]
            k_show = [sb(f"k_show{j}", [P, KC, M]) for j in range(2)]
        else:
            k_show = k_t
        v_tok = [sb(f"v_tok{j}", [P, 2, D]) for j in range(2)]
        v_last = [sb(f"v_last{j}", [P, D]) for j in range(2)]
        p_last = sb("p_last", [P, 4])
        s, p = sb("s", [P, 4, M]), sb("p", [P, 4, M])
        pt = sb("pt", [P, 2, 4 * P])
        last_part, own_inv, whole, om = (sb(n, [P, 4, 64]) for n in ("last_part", "own_inv", "whole", "om"))
        top, neg, total, inv = (sb(n, [P, 4]) for n in ("top", "neg", "total", "inv"))
        (block, loaded0, loaded1, tail0, tail1, padded, shown, k_made, v_made, k_ready, v_ready,
         scores_ready, biased, topped, negated, exped, inverted, p_turned, pt_act, pt_dve, result_ready,
         prepared, added, owned, out_made, out_taken, passed) = mem.enter_context(
            phase(core, "loaded0", "loaded1", "tail0", "tail1", "padded", "shown", "k_made", "v_made",
                  "k_ready", "v_ready", "scores_ready", "biased", "topped", "negated", "exped", "inverted",
                  "p_turned", "pt_act", "pt_dve", "result_ready", "prepared", "added", "owned",
                  "out_made", "out_taken", "passed"))
        arrived, tail_in = [loaded0, loaded1], [tail0, tail1]
        loads = 32 if masked else 16
        banks = core.banks8
        halves = ((0, 2), (2, 4))

        def loop(eng, batch):
            with eng.Fori(0, B // 2 - 1) as r:
                for j in range(2):
                    batch(2 * r + j, j, 2)
            batch(B - 2, 0, 1)
            batch(B - 1, 1, 0)

        def of_parity(b, j, count):
            return START + (b - j) * (count // 2) + count

        @block.sync
        def _(sp):
            def fetch(b, j):
                sp.dma_start(ctx_sb[j][:, :, :], ctx_t[b, :, :].rearrange("(k p) m -> p k m", p=P))\
                  .then_inc(arrived[j], 16)
                if masked:
                    sp.dma_start(hide8[j][:, :], mask[b, :, :].broadcast_to([P, M])).then_inc(arrived[j], 16)

            def fetch_tail(b, j):
                sp.dma_start(v_last[j][:, :], tails[bass.ds(b, 1), :].broadcast_to([P, D])).then_inc(tail_in[j], 16)

            for j in range(2):
                fetch(j, j)
                fetch_tail(j, j)
            with sp.Fori(0, B // 2 - 1) as r:
                for j in range(2):
                    sp.wait_ge(k_made, START + 2 * r + j + 1)
                    sp.sem_inc(passed, 1)
                    if masked:
                        sp.wait_ge(shown, START + (2 * r + j + 1) * 3)
                    else:
                        sp.wait_ge(v_made, START + 2 * r + j + 1)
                    sp.sem_inc(passed, 1)
                    fetch(2 * r + j + 2, j)
                    sp.wait_ge(prepared, START + (2 * r + j + 1) * 2)
                    sp.sem_inc(passed, 1)
                    fetch_tail(2 * r + j + 2, j)

        @block.gpsimd
        def _(pool):
            def pad(b, j):
                for c in range(KC):
                    nc.gpsimd.tensor_tensor(q_pad[j][:, c * 8:c * 8 + 8, :], bcast(q[:, c, blk(b, S)], 8),
                                            bcast(core.consts["head_of_8"][:, :], S, 2), ALU.mult)\
                      .then_inc(padded, 1)

            def hide(b, j):
                pool.wait_ge(arrived[j], of_parity(b, j, loads))
                pool.sem_inc(passed, 1)
                nc.gpsimd.tensor_scalar(show[j][:, :], hide8[j][:, :], -1.0, 1.0, ALU.mult, ALU.add)\
                  .then_inc(shown, 1)
                nc.gpsimd.tensor_scalar(hidden[j][:, :], hide8[j][:, :], -1e9, None, ALU.mult)\
                  .then_inc(shown, 1)
                pool.wait_ge(k_ready, START + b + 1)
                pool.sem_inc(passed, 1)
                pool.wait_ge(shown, START + b * 3 + 2)
                nc.gpsimd.tensor_tensor(k_show[j][:, :, :], k_t[j][:, :, :], bcast(show[j][:, :], KC), ALU.mult)\
                  .then_inc(shown, 1)

            def prepare(b, j):
                pool.wait_ge(inverted, START + 2 * b + 2)
                pool.wait_ge(tail_in[j], of_parity(b, j, 16))
                pool.wait_ge(owned, START + b)
                nc.gpsimd.tensor_tensor(last_part[:, :, :], v_last[j][:, :].rearrange("p (n f) -> p n f", n=4),
                                        bcast(p_last[:, :], 64, 2), ALU.mult).then_inc(prepared, 1)
                nc.gpsimd.tensor_tensor(own_inv[:, :, :], bcast(core.consts["own_head"][:, :], 4),
                                        bcast(inv[:, :], 64, 2), ALU.mult).then_inc(prepared, 1)

            def batch(b, j, ahead):
                prepare(b, j)
                if ahead == 2:
                    pool.wait_ge(biased, START + 2 * b + 2)
                    pad(b + 2, j)
                    if masked:
                        hide(b + 2, j)

            for j in range(2):
                pad(j, j)
                if masked:
                    hide(j, j)
            loop(pool, batch)

        @block.tensor
        def _(pe):
            def keys(b, j):
                pe.wait_ge(arrived[j], of_parity(b, j, loads))
                for m in range(KC):
                    for k in range(KC):
                        ins = pe.matmul(banks[:, 4 + m, 0:M], wk[:, k, m * P:(m + 1) * P], ctx_sb[j][:, k, :],
                                        start=(k == 0), stop=(k == KC - 1))
                ins.then_inc(k_made, 1)

            def values(b, j):
                pe.wait_ge(v_ready, START + b)
                if masked:
                    pe.wait_ge(k_ready, START + b + 1)
                    for c in range(2):
                        for f in range(KC):
                            ins = pe.transpose(banks[:, 6, c * D + f * P:c * D + (f + 1) * P],
                                               k_t[j][:, f, c * P:(c + 1) * P], core.ident[:, :])
                else:
                    for c in range(2):
                        for k in range(KC):
                            ins = pe.matmul(banks[:, 6, c * D:(c + 1) * D], ctx_sb[j][:, k, c * P:(c + 1) * P],
                                            wv[:, k, :], start=(k == 0), stop=(k == KC - 1))
                ins.then_inc(v_made, 1)

            def scores(b, j):
                pe.wait_ge(padded, START + 2 * b + 2)
                if masked:
                    pe.wait_ge(shown, START + 3 * b + 3)
                else:
                    pe.wait_ge(k_ready, START + b + 1)
                pe.wait_ge(biased, START + 2 * b)
                for n in range(4):
                    ins = pe.matmul(banks[:, n, 0:M],
                                    q_pad[j][:, 4 * n:4 * n + 4, :].rearrange("p h s -> p (h s)"),
                                    k_show[j][:, n // 2, :], start=True, stop=True)
                    ins.then_inc(scores_ready, 1)

            def turn(b, ahead):
                pe.wait_ge(exped, START + b + 1)
                pe.wait_ge(k_ready, START + b + 1 + min(ahead, 1))
                for c in range(2):
                    for n in range(4):
                        ins = pe.transpose(banks[:, 4 + c, n * P:(n + 1) * P], p[:, n, c * P:(c + 1) * P],
                                           core.ident[:, :])
                ins.then_inc(p_turned, 1)

            def results(b, j):
                pe.wait_ge(pt_act, START + b + 1)
                pe.wait_ge(pt_dve, START + b + 1)
                pe.wait_ge(out_taken, START + b)
                pe.wait_ge(v_ready, START + b + 1)
                for n in range(4):
                    for c in range(2):
                        ins = pe.matmul(banks[:, 7, n * 64:(n + 1) * 64], pt[:, c, n * P:(n + 1) * P],
                                        v_tok[j][:, c, n * 64:(n + 1) * 64], start=(c == 0), stop=(c == 1))
                ins.then_inc(result_ready, 1)

            def output(b):
                pe.wait_ge(owned, START + b + 1)
                for c in range(KC):
                    ins = pe.matmul(banks[:, 7, 256 + c * S:256 + (c + 1) * S],
                                    om[:, 2 * c:2 * c + 2, :].rearrange("p n f -> p (n f)"),
                                    core.consts["query_sel"][:, :], start=True, stop=True)
                ins.then_inc(out_made, 1)

            def batch(b, j, ahead):
                turn(b, ahead)
                if ahead >= 1:
                    scores(b + 1, 1 - j)
                results(b, j)
                if ahead == 2:
                    keys(b + 2, j)
                output(b)
                if masked and ahead >= 1:
                    values(b + 1, 1 - j)
                elif ahead == 2:
                    values(b + 2, j)

            keys(0, 0)
            values(0, 0)
            scores(0, 0)
            pe.wait_ge(k_ready, START + 1)
            pe.wait_ge(v_ready, START + 1)
            keys(1, 1)
            if not masked:
                values(1, 1)
            loop(pe, batch)

        @block.scalar
        def _(act):
            def keys(b, j):
                act.wait_ge(k_made, START + b + 1)
                nc.scalar.copy(k_t[j][:, :, :], banks[:, 4:6, 0:M]).then_inc(k_ready, 1)

            def exps(b):
                act.wait_ge(p_turned, START + b)
                act.wait_ge(inverted, START + 2 * b)
                for h, (n0, n1) in enumerate(halves):
                    act.wait_ge(negated, START + 2 * b + h + 1)
                    for n in range(n0, n1):
                        ins = nc.scalar.activation(p[:, n, :], s[:, n, :], ACT.Exp, bias=neg[:, n:n + 1],
                                                   scale=SC if rel is None else 1.0, accum_out=total[:, n:n + 1])
                ins.then_inc(exped, 1)

            def batch(b, j, ahead):
                act.wait_ge(p_turned, START + b + 1)
                act.wait_ge(result_ready, START + b)
                nc.scalar.copy(pt[:, 0, :], banks[:, 4, :]).then_inc(pt_act, 1)
                if ahead >= 1:
                    exps(b + 1)
                if ahead == 2:
                    keys(b + 2, j)
                if masked and ahead >= 1:
                    values(b + 1, 1 - j)
                elif ahead == 2:
                    values(b + 2, j)

            def values(b, j):
                act.wait_ge(v_made, START + b + 1)
                nc.scalar.copy(v_tok[j][:, :, :], banks[:, 6, :].rearrange("p (c f) -> p c f", c=2))\
                  .then_inc(v_ready, 1)

            keys(0, 0)
            values(0, 0)
            exps(0)
            keys(1, 1)
            if not masked:
                values(1, 1)
            loop(act, batch)

        @block.vector
        def _(dve):
            def softmax(b, j, h):
                n0, n1 = halves[h]
                dve.wait_ge(scores_ready, START + b * 4 + n1)
                dve.wait_ge(exped, START + b)
                if masked:
                    nc.vector.tensor_tensor(s[:, n0:n1, :], banks[:, n0:n1, 0:M], bcast(hidden[j][:, :], 2),
                                            ALU.add).then_inc(biased, 1)
                else:
                    nc.vector.scalar_tensor_tensor(out=s[:, n0:n1, :], in0=banks[:, n0:n1, 0:M], scalar=SC,
                                                   in1=rel[:, n0:n1, :], op0=ALU.mult, op1=ALU.add)\
                      .then_inc(biased, 1)
                dve.wait_ge(biased, START + 2 * b + h + 1)
                nc.vector.tensor_reduce(top[:, n0:n1], s[:, n0:n1, :], AX, ALU.max).then_inc(topped, 1)
                dve.wait_ge(topped, START + 2 * b + h + 1)
                nc.vector.tensor_scalar(neg[:, n0:n1], top[:, n0:n1], -SC if rel is None else -1.0, None,
                                        ALU.mult).then_inc(negated, 1)

            def own(b):
                dve.wait_ge(prepared, START + 2 * b + 2)
                dve.wait_ge(result_ready, START + b + 1)
                nc.vector.tensor_tensor(whole[:, :, :], banks[:, 7, 0:D].rearrange("p (n f) -> p n f", n=4),
                                        last_part[:, :, :], ALU.add).then_inc(added, 1)
                dve.wait_ge(added, START + b + 1)
                nc.vector.tensor_tensor(om[:, :, :], whole[:, :, :], own_inv[:, :, :], ALU.mult).then_inc(owned, 1)

            def batch(b, j, ahead):
                dve.wait_ge(exped, START + b + 1)
                dve.wait_ge(prepared, START + 2 * b)
                nc.vector.reciprocal(inv[:, :], total[:, :]).then_inc(inverted, 1)
                nc.vector.tensor_copy(p_last[:, :], p[:, :, 2 * P]).then_inc(inverted, 1)
                dve.wait_ge(p_turned, START + b + 1)
                nc.vector.tensor_copy(pt[:, 1, :], banks[:, 5, :]).then_inc(pt_dve, 1)
                if ahead >= 1:
                    softmax(b + 1, 1 - j, 0)
                    softmax(b + 1, 1 - j, 1)
                own(b)
                dve.wait_ge(out_made, START + b + 1)
                nc.vector.tensor_copy(out[:, :, blk(b, S)],
                                      banks[:, 7, 256:256 + KC * S].rearrange("p (c s) -> p c s", c=KC))\
                  .then_inc(out_taken, 1)

            softmax(0, 0, 0)
            softmax(0, 0, 1)
            loop(dve, batch)


def cross_single(core, q, out, ctx_t, ctx_rows, row_w, row_src, row_bias, phi=None, phi_w=None, tops=None):
    nc = core.nc
    CONST = BLK - 1
    with ExitStack() as mem:
        def sb(name, *shape):
            return [mem.enter_context(nc.sbuf_tensor(f"{name}{j}_{core.turn}", list(shape), F32)) for j in range(2)]
        ctx_sb, rows_sb, last_sb = sb("ctx", P, 4, KC, M), sb("rows", P, 4, 2, D), sb("last", 4, D)
        q_st, src_st = sb("q_st", P, KC, GT), sb("src_st", P, KC, GT)
        phi_sb = sb("phi", P, M) if phi is not None else None
        s, p, pt = sb("s", P, M), sb("p", P, M), sb("pt", P, 3, P)
        p_last, om = sb("p_last", P, 4), sb("om", P, D)
        top, neg, total, inv, const = (sb(n, P, 1) for n in ("top", "neg", "total", "inv", "const"))
        (block, t_in0, t_in1, rows_in0, rows_in1, phi_in0, phi_in1, staged, scores_ready, const_ready, summed,
         topped, negated, exped, inverted, normed, p_turned, pt_ready, result_ready, om_ready, out_ready,
         out_taken, passed) = mem.enter_context(
            phase(core, "t_in0", "t_in1", "rows_in0", "rows_in1", "phi_in0", "phi_in1", "staged", "scores_ready",
                  "const_ready", "summed", "topped", "negated", "exped", "inverted", "normed", "p_turned",
                  "pt_ready", "result_ready", "om_ready", "out_ready", "out_taken", "passed"))
        t_in, rows_in, phi_in = [t_in0, t_in1], [rows_in0, rows_in1], [phi_in0, phi_in1]
        T_LOADS, ROW_LOADS = 4 * 16, 5 * 16
        banks = core.banks8

        def of_parity(g, j, count):
            return START + (g - j) * (count // 2) + count

        def loop(eng, step):
            with eng.Fori(0, NG // 2 - 1) as r:
                for j in range(2):
                    step(2 * r + j, j, 2)
            step(NG - 2, 0, 1)
            step(NG - 1, 1, 0)

        @block.sync
        def _(sp):
            def fetch_t(g, j):
                for b in range(4):
                    sp.dma_start(ctx_sb[j][:, b, :, :], ctx_t[4 * g + b, :, :].rearrange("(k p) m -> p k m", p=P))\
                      .then_inc(t_in[j], 16)
                if phi is not None:
                    sp.dma_start(phi_sb[j][:, :], phi[blk(g, GT), :]).then_inc(phi_in[j], 16)

            def fetch_rows(g, j):
                for b in range(4):
                    sp.dma_start(rows_sb[j][:, b, :, :], ctx_rows[4 * g + b, 0:2 * P, :]
                                 .rearrange("(c p) f -> p c f", p=P)).then_inc(rows_in[j], 16)
                sp.dma_start(last_sb[j][:, :], ctx_rows[bass.ds(4 * g, 4), 2 * P:M, :]
                             .rearrange("b o f -> (b o) f")).then_inc(rows_in[j], 16)

            def next_t(g, j):
                sp.wait_ge(summed, START + g - 1)
                sp.sem_inc(passed, 1)
                fetch_t(g, j)

            def next_rows(g, j):
                sp.wait_ge(out_ready, START + g - 1)
                sp.sem_inc(passed, 1)
                fetch_rows(g, j)

            for j in range(2):
                fetch_t(j, j)
                fetch_rows(j, j)
            for j in range(2):
                next_t(2 + j, j)
            with sp.Fori(0, NG // 2 - 2) as r:
                for j in range(2):
                    next_rows(2 * r + j + 2, j)
                    next_t(2 * r + j + 4, j)
            for j in range(2):
                next_rows(NG - 2 + j, j)

        @block.gpsimd
        def _(pool):
            def stage(g, j):
                nc.gpsimd.tensor_copy(q_st[j][:, :, :], q[:, :, blk(g, GT)]).then_inc(staged, 1)
                nc.gpsimd.tensor_copy(src_st[j][:, :, :], row_src[:, :, blk(g, GT)]).then_inc(staged, 1)

            stage(0, 0)
            stage(1, 1)
            with pool.Fori(0, NG // 2 - 1) as r:
                for j in range(2):
                    pool.wait_ge(scores_ready, START + 2 * r + j + 1)
                    pool.sem_inc(passed, 1)
                    stage(2 * r + j + 2, j)

        @block.tensor
        def _(pe):
            def scores(g, j):
                pe.wait_ge(t_in[j], of_parity(g, j, T_LOADS))
                pe.wait_ge(staged, START + 2 * g + 2)
                if not isinstance(g, int):
                    pe.wait_ge(summed, START + g - 1)
                for k in range(KC):
                    pe.matmul(banks[:, j, CONST:CONST + 1], src_st[j][:, k, :], row_w[:, k:k + 1], start=(k == 0),
                              stop=(k == KC - 1))
                for b in range(4):
                    for k in range(KC):
                        ins = pe.matmul(banks[32 * b:32 * b + 32, j, 0:M], q_st[j][:, k, 32 * b:32 * b + 32],
                                        ctx_sb[j][:, b, k, :], start=(k == 0), stop=(k == KC - 1))
                ins.then_inc(scores_ready, 1)

            def turn(g, j):
                pe.wait_ge(normed, START + g + 1)
                if not isinstance(g, int) or g >= 2:
                    pe.wait_ge(pt_ready, START + g - 1)
                for c in range(2):
                    pe.transpose(banks[:, 2 + j, c * P:(c + 1) * P], p[j][:, c * P:(c + 1) * P], core.ident[:, :])
                pe.transpose(banks[0:4, 2 + j, 2 * P:3 * P], p_last[j][:, :], core.ident[:, :])\
                  .then_inc(p_turned, 1)

            def result(g, j):
                pe.wait_ge(pt_ready, START + g + 1)
                pe.wait_ge(rows_in[j], of_parity(g, j, ROW_LOADS))
                if not isinstance(g, int) or g >= 2:
                    pe.wait_ge(out_taken, START + g - 1)
                pe.matmul(banks[:, 4 + j, 0:D], pt[j][0:4, 2, :], last_sb[j][:, :], start=True, stop=False)
                for b in range(4):
                    for c in range(2):
                        ins = pe.matmul(banks[32 * b:32 * b + 32, 4 + j, 0:D], pt[j][:, c, 32 * b:32 * b + 32],
                                        rows_sb[j][:, b, c, :], start=False, stop=(c == 1))
                ins.then_inc(result_ready, 1)

            def output(g, j):
                pe.wait_ge(om_ready, START + g + 1)
                for f in range(KC):
                    ins = pe.transpose(banks[:, 4 + j, D + f * P:D + (f + 1) * P], om[j][:, f * P:(f + 1) * P],
                                       core.ident[:, :])
                ins.then_inc(out_ready, 1)

            def step(i, j, ahead):
                result(i, j)
                if ahead == 2:
                    scores(i + 2, j)
                output(i, j)
                if ahead >= 1:
                    turn(i + 1, 1 - j)

            scores(0, 0)
            scores(1, 1)
            turn(0, 0)
            loop(pe, step)

        @block.scalar
        def _(act):
            def exps(g, j):
                act.wait_ge(negated, START + g + 1)
                if not isinstance(g, int) or g >= 2:
                    act.wait_ge(p_turned, START + g - 1)
                nc.scalar.activation(p[j][:, :], s[j][:, :], ACT.Exp, bias=neg[j][:, 0:1],
                                     accum_out=total[j][:, 0:1]).then_inc(exped, 1)

            def turned(g, j):
                act.wait_ge(p_turned, START + g + 1)
                if not isinstance(g, int) or g >= 2:
                    act.wait_ge(result_ready, START + g - 1)
                nc.scalar.copy(pt[j][:, 0:2, :], banks[:, 2 + j, 0:2 * P].rearrange("p (c w) -> p c w", c=2))
                nc.scalar.copy(pt[j][0:4, 2, :], banks[0:4, 2 + j, 2 * P:3 * P]).then_inc(pt_ready, 1)

            def step(i, j, ahead):
                if ahead == 2:
                    exps(i + 2, j)
                if ahead >= 1:
                    turned(i + 1, 1 - j)

            exps(0, 0)
            exps(1, 1)
            turned(0, 0)
            loop(act, step)

        @block.vector
        def _(dve):
            def scored(g, j):
                dve.wait_ge(scores_ready, START + g + 1)
                if not isinstance(g, int) or g >= 2:
                    dve.wait_ge(exped, START + g - 1)
                nc.vector.tensor_scalar(const[j][:, :], banks[:, j, CONST:CONST + 1], row_bias, None, ALU.add)\
                  .then_inc(const_ready, 1)
                dve.wait_ge(const_ready, START + g + 1)
                if phi is not None:
                    dve.wait_ge(phi_in[j], of_parity(g, j, 16))
                    nc.vector.tensor_scalar(s[j][:, :], phi_sb[j][:, :], phi_w, const[j][:, 0:1], ALU.mult,
                                            ALU.add).then_inc(topped, 1)
                    dve.wait_ge(topped, START + 2 * g + 1)
                    nc.vector.tensor_tensor(s[j][:, :], s[j][:, :], banks[:, j, 0:M], ALU.add).then_inc(summed, 1)
                else:
                    nc.vector.tensor_scalar(s[j][:, :], banks[:, j, 0:M], const[j][:, 0:1], None, ALU.add)\
                      .then_inc(summed, 1)
                dve.wait_ge(summed, START + g + 1)
                nc.vector.tensor_reduce(top[j][:, :], s[j][:, :], AX, ALU.max).then_inc(topped, 1)
                dve.wait_ge(topped, START + (2 * g + 2 if phi is not None else g + 1))
                if tops is not None:
                    nc.vector.tensor_copy(tops[:, bass.ds(g, 1)], top[j][:, :])
                nc.vector.tensor_scalar(neg[j][:, :], top[j][:, :], -1.0, None, ALU.mult).then_inc(negated, 1)

            def sums(g, j):
                dve.wait_ge(exped, START + g + 1)
                nc.vector.reciprocal(inv[j][:, :], total[j][:, :]).then_inc(inverted, 1)
                if not isinstance(g, int) or g >= 2:
                    dve.wait_ge(p_turned, START + g - 1)
                nc.vector.tensor_scalar(p_last[j][:, :], core.consts["batch_of_4"][:, :], p[j][:, 2 * P:M], None,
                                        ALU.mult).then_inc(normed, 1)

            def step(i, j, ahead):
                dve.wait_ge(result_ready, START + i + 1)
                dve.wait_ge(inverted, START + i + 1)
                nc.vector.tensor_scalar(om[j][:, :], banks[:, 4 + j, 0:D], inv[j][:, 0:1], None, ALU.mult)\
                  .then_inc(om_ready, 1)
                if ahead == 2:
                    scored(i + 2, j)
                    sums(i + 2, j)
                dve.wait_ge(out_ready, START + i + 1)
                nc.vector.tensor_copy(out[:, :, blk(i, GT)],
                                      banks[:, 4 + j, D:2 * D].rearrange("p (f n) -> p f n", f=KC))\
                  .then_inc(out_taken, 1)

            scored(0, 0)
            scored(1, 1)
            sums(0, 0)
            sums(1, 1)
            loop(dve, step)


def gates(core, x, parts, w, bias, gate_rows, experts, shared=0, aside=()):
    nc = core.nc
    E = experts
    with ExitStack() as mem:
        def sb(name, shape, dt=F32):
            return mem.enter_context(nc.sbuf_tensor(f"{name}_{core.turn}", shape, dt))
        z, e = sb("z", [P, NG, E]), sb("e", [P, NG, E])
        top, total, inv = (sb(n, [P, NG]) for n in ("top", "total", "inv"))
        best, which = sb("best", [P, NG, 8]), sb("which", [P, NG, 8], U32)
        at = sb("at", [P, NG, 8])
        first, second = sb("first", [P, NG, E]), sb("second", [P, NG, E])
        gate_t = sb("gate_t", [E, N])
        ones = sb("ones", [1, N])
        experts_at = core.consts["iota16"]
        (block, logits_ready, step, exped, found, turned, taken, kept, filled, aside_done, highs) = mem.enter_context(
            phase(core, "logits_ready", "step", "exped", "found", "turned", "taken", "kept", "filled",
                  "aside_done", "highs"))

        @block.tensor
        def _(pe):
            for g in range(NG):
                for k in range(KC):
                    ins = pe.matmul(core.psum[0][:, g * E:(g + 1) * E], x[:, k, g * GT:(g + 1) * GT], w[:, k, :],
                                    start=(k == 0), stop=(k == KC - 1))
            ins.then_inc(logits_ready, 1)
            pe.wait_ge(found, START + 1)
            for g in range(NG):
                ins = pe.transpose(core.psum[4 + g // 4][0:E, (g % 4) * P:(g % 4 + 1) * P], second[:, g, :],
                                   core.ident[:, :])
            ins.then_inc(turned, 1)

        @block.scalar
        def _(act):
            for t in range(NB):
                nc.scalar.copy(parts[0][:, :, blk(t)], x[:, :, blk(t)]).then_inc(highs, 1)
            act.wait_ge(step, START + 3)
            nc.scalar.activation(e[:, :, :], z[:, :, :], ACT.Exp).then_inc(exped, 1)

        @block.gpsimd
        def _(pool):
            nc.gpsimd.memset(ones[:, :], 1.0).then_inc(filled, 1)
            for n, f in enumerate(aside):
                f().then_inc(aside_done, 1)
            if aside:
                pool.wait_ge(aside_done, START + len(aside))

        @block.sync
        def _(sp):
            sp.wait_ge(filled, START + 1)
            sp.wait_ge(taken, START + 1)
            sp.dma_start(gate_rows[0:E, :], gate_t[:, :]).then_inc(kept, 16)
            for j in range(shared):
                sp.dma_start(gate_rows[E + j:E + j + 1, :], ones[:, :]).then_inc(kept, 16)
            sp.wait_ge(kept, START + 16 * (1 + shared))

        @block.vector
        def _(dve):
            n = 0

            def then(ins):
                nonlocal n
                n += 1
                ins.then_inc(step, 1)
                dve.wait_ge(step, START + n)

            for t in range(NB):
                dve.wait_ge(highs, START + t + 1)
                low_part(nc, parts[1][:, :, blk(t)], x[:, :, blk(t)], parts[0][:, :, blk(t)])
            dve.wait_ge(logits_ready, START + 1)
            logits = core.psum[0][:, 0:NG * E].rearrange("p (g e) -> p g e", e=E)
            then(nc.vector.tensor_tensor(z[:, :, :], logits, bcast(bias[:, :], NG), ALU.add))
            then(nc.vector.tensor_reduce(top[:, :], z[:, :, :], AX, ALU.max))
            then(nc.vector.tensor_tensor(z[:, :, :], z[:, :, :], bcast(top[:, :], E, 2), ALU.subtract))
            dve.wait_ge(exped, START + 1)
            then(nc.vector.tensor_reduce(total[:, :], e[:, :, :], AX, ALU.add))
            then(nc.vector.reciprocal(inv[:, :], total[:, :]))
            then(nc.vector.tensor_tensor(e[:, :, :], e[:, :, :], bcast(inv[:, :], E, 2), ALU.mult))
            for g in range(NG):
                ins = nc.vector.max(best[:, g, :], e[:, g, :])
            then(ins)
            for g in range(NG):
                ins = nc.vector.max_index(which[:, g, :], best[:, g, :], e[:, g, :])
            then(ins)
            then(nc.vector.tensor_copy(at[:, :, :], which[:, :, :]))
            for g in range(NG):
                nc.vector.tensor_scalar(first[:, g, :], experts_at[:, 0:E], at[:, g, 0:1], best[:, g, 0:1],
                                        ALU.is_equal, ALU.mult)
                ins = nc.vector.tensor_scalar(second[:, g, :], experts_at[:, 0:E], at[:, g, 1:2],
                                              best[:, g, 1:2], ALU.is_equal, ALU.mult)
            then(ins)
            nc.vector.tensor_tensor(second[:, :, :], second[:, :, :], first[:, :, :], ALU.add).then_inc(found, 1)
            dve.wait_ge(turned, START + 1)
            nc.vector.tensor_copy(gate_t[:, :].rearrange("e (b n) -> e b n", b=4),
                                  core.banks8[0:E, 4:8, :]).then_inc(taken, 1)


def experts_sum(core, kind, x, acc, gate_rows, experts, w1, w2, b1=None, b2=None, hidden=None,
                aside=None):
    nc = core.nc
    hc = hidden // P if hidden else 0
    hp = 2 * hc if kind == "glu" else hc
    with ExitStack() as mem:
        def sb(name, shape, dt=F32):
            return mem.enter_context(nc.sbuf_tensor(f"{name}_{core.turn}", shape, dt))
        x_high, x_low = x
        shapes = [[P, KC, hp * P if hp else D]] + ([[P, hc, D]] if hc else [])
        mats = len(shapes)
        w_in = [sb(f"w{i}", shape) for i, shape in enumerate(shapes)]
        w_high, w_low = ([[sb(f"w{i}_{part}_{j}", shape, F32R) for i, shape in enumerate(shapes)] for j in range(2)]
                         for part in ("high", "low"))
        b1_sb = [sb(f"b1_{j}", [P, hc]) for j in range(2)] if b1 is not None else None
        b2_sb = [sb(f"b2_{j}", [P, KC]) for j in range(2)] if b2 is not None else None
        gate = [sb(f"gate_{j}", [P, N]) for j in range(2)]
        h = sb("h", [P, 2, BLK]) if hc else None
        h_high, h_low = (sb(f"h_{part}", [P, 2, hc, BLK], F32R) if hc else None for part in ("high", "low"))
        act_g = sb("act_g", [P, 2, BLK]) if kind == "glu" else None
        y = sb("y", [P, 2, KC, BLK])
        (block, loaded0, loaded1, w_loaded, h_made, h_ready, y_made, y_gated, added, glu_ready, passed, w_highs,
         w_lows, h_highs, h_lows) = mem.enter_context(
            phase(core, "loaded0", "loaded1", "w_loaded", "h_made", "h_ready", "y_made", "y_gated", "added",
                  "glu_ready", "passed", "w_highs", "w_lows", "h_highs", "h_lows"))
        arrived = [loaded0, loaded1]
        loads = 16 * (1 + (b1 is not None) + (b2 is not None))
        banks = core.banks8
        y_at = 4
        credit = {"relu": hc, "plain": 0, "glu": 2}[kind]
        low_credit = 2 if kind == "relu" else 0

        def of_parity(e, j):
            return START + (e - j) * (loads // 2) + loads

        def rounds(eng, step):
            with eng.Fori(0, experts // 2 - 1) as r:
                for j in range(2):
                    for t in range(NB):
                        step(2 * r + j, j, t, False)
            for j in range(2):
                for t in range(NB):
                    step(experts - 2 + j, j, t, True)

        def next_block(e, j, t, last):
            if t + 1 < NB:
                return e, j, t + 1
            return None if last and j == 1 else (e + 1, 1 - j, 0)

        if aside:
            @block.gpsimd
            def _(pool):
                aside.fetch_source(pool)
                for n in range(2):
                    aside.fetch_stage(pool, n)
                for n in range(aside.STAGES):
                    aside.stage(pool, nc.gpsimd, n)
                    if n + 2 < aside.STAGES:
                        pool.wait_ge(aside.step, aside.done)
                        aside.fetch_stage(pool, n + 2)
                aside.keep_result(pool)

        @block.sync
        def _(sp):
            def fetch_weights(e):
                for tile, d in zip(w_in, (w1, w2)):
                    sp.dma_start(tile[:, :, :], d[e, :, :].rearrange("(k p) m -> p k m", p=P)).then_inc(w_loaded, 16)

            def fetch_rest(e, j):
                if b1 is not None:
                    sp.dma_start(b1_sb[j][:, :], b1[e, :, :]).then_inc(arrived[j], 16)
                if b2 is not None:
                    sp.dma_start(b2_sb[j][:, :], b2[e, :, :]).then_inc(arrived[j], 16)
                sp.dma_start(gate[j][:, :], gate_rows[bass.ds(e, 1), :].broadcast_to([P, N])).then_inc(arrived[j], 16)

            fetch_weights(0)
            for j in range(2):
                fetch_rest(j, j)
            sp.wait_ge(w_lows, START + mats)
            fetch_weights(1)
            with sp.Fori(0, experts // 2 - 1) as r:
                for j in range(2):
                    sp.wait_ge(w_lows, START + (2 * r + j + 2) * mats)
                    sp.sem_inc(passed, 1)
                    fetch_weights(2 * r + j + 2)
                    sp.wait_ge(y_gated, START + (2 * r + j + 1) * NB * KC)
                    sp.sem_inc(passed, 1)
                    fetch_rest(2 * r + j + 2, j)

        @block.tensor
        def _(pe):
            def of_x(t):
                return [(x_high[:, k, blk(t)], x_low[:, k, blk(t)]) for k in range(KC)]

            def of_weights(i, j, m, chunks_n):
                return [(w_high[j][i][:, k, m * P:(m + 1) * P], w_low[j][i][:, k, m * P:(m + 1) * P])
                        for k in range(chunks_n)]

            def first(e, j, t):
                n = e * NB + t
                pe.wait_ge(w_lows, START + (e + 1) * mats)
                for m in range(hp):
                    bank = m if hc == 4 else 2 * (t % 2) + m
                    pe.wait_ge(h_ready, START + (n * hc + (m + 1 if kind == "relu" else 1)))
                    split_products(pe, banks[:, bank, :], of_weights(0, j, m, KC), of_x(t)).then_inc(h_made, 1)

            def second(e, j, t):
                n = e * NB + t
                if hc:
                    pe.wait_ge(h_lows, START + low_credit + (n + 1) * hc)
                else:
                    pe.wait_ge(w_lows, START + (e + 1) * mats)
                for m in range(KC):
                    pe.wait_ge(added, START + n * KC + m + 1)
                    xs = [(h_high[:, t % 2, k, :], h_low[:, t % 2, k, :]) for k in range(hc)] if hc else of_x(t)
                    split_products(pe, banks[:, y_at + 2 * (t % 2) + m, :], of_weights(mats - 1, j, m, hc or KC), xs)\
                        .then_inc(y_made, 1)

            def step(e, j, t, last):
                following = next_block(e, j, t, last)
                if hc and following:
                    first(*following)
                second(e, j, t)

            if hc:
                first(0, 0, 0)
            rounds(pe, step)

        @block.scalar
        def _(act):
            def weights_high(e, j):
                act.wait_ge(w_loaded, START + (e + 1) * mats * 16)
                for high, whole in zip(w_high[j], w_in):
                    nc.scalar.copy(high[:, :, :], whole[:, :, :]).then_inc(w_highs, 1)

            def hidden_features(e, j, t, last):
                n = e * NB + t
                used = n - 1 if last or t or j else n
                if kind == "relu":
                    for m in range(hc):
                        act.wait_ge(h_made, START + n * hp + m + 1)
                        act.wait_ge(arrived[j], of_parity(e, j))
                        act.wait_ge(y_made, START + used * KC)
                        nc.scalar.activation(h_high[:, t % 2, m, :], banks[:, m, :], ACT.Relu,
                                             bias=b1_sb[j][:, m:m + 1]).then_inc(h_highs, 1)
                        act.wait_ge(h_lows, START + n * hc + m + 1)
                        nc.scalar.activation(h[:, m % 2, :], banks[:, m, :], ACT.Relu,
                                             bias=b1_sb[j][:, m:m + 1]).then_inc(h_ready, 1)
                else:
                    act.wait_ge(h_made, START + n * 2 + 1)
                    act.wait_ge(h_ready, START + n - 1 + credit)
                    nc.scalar.activation(act_g[:, t % 2, :], banks[:, 2 * (t % 2), :], ACT.Silu)\
                      .then_inc(glu_ready, 1)
                    act.wait_ge(h_ready, START + n + 1 + credit)
                    act.wait_ge(y_made, START + used * KC)
                    nc.scalar.copy(h_high[:, t % 2, 0, :], h[:, t % 2, :]).then_inc(h_highs, 1)

            def step(e, j, t, last):
                if hc:
                    hidden_features(e, j, t, last)
                if t == 1 and not (last and j == 1):
                    act.wait_ge(y_made, START + e * NB * KC)
                    weights_high(e + 1, 1 - j)

            act.sem_inc(h_ready, max(credit, 1))
            weights_high(0, 0)
            rounds(act, step)

        @block.vector
        def _(dve):
            def weights_low(e, j):
                for i in range(mats):
                    dve.wait_ge(w_highs, START + e * mats + i + 1)
                    low_part(nc, w_low[j][i][:, :, :], w_in[i][:, :, :], w_high[j][i][:, :, :]).then_inc(w_lows, 1)

            def gated_unit(e, j, t):
                n = e * NB + t
                dve.wait_ge(glu_ready, START + n + 1)
                dve.wait_ge(h_made, START + n * 2 + 2)
                nc.vector.tensor_tensor(h[:, t % 2, :], act_g[:, t % 2, :], banks[:, 2 * (t % 2) + 1, :],
                                        ALU.mult).then_inc(h_ready, 1)

            def hidden_low(e, j, t):
                n = e * NB + t
                for m in range(hc):
                    dve.wait_ge(h_ready, START + n * hc + m + 1 + credit)
                    dve.wait_ge(h_highs, START + n * hc + m + 1)
                    low_part(nc, h_low[:, t % 2, m, :], h[:, (m if kind == "relu" else t) % 2, :],
                             h_high[:, t % 2, m, :]).then_inc(h_lows, 1)

            def outputs(e, j, t):
                n = e * NB + t
                for m in range(KC):
                    dve.wait_ge(y_made, START + n * KC + m + 1)
                    dve.wait_ge(arrived[j], of_parity(e, j))
                    dve.wait_ge(added, START + n * KC + m + 1)
                    nc.vector.scalar_tensor_tensor(
                        out=y[:, t % 2, m, :], in0=banks[:, y_at + 2 * (t % 2) + m, :],
                        scalar=b2_sb[j][:, m:m + 1] if b2 is not None else 0.0,
                        in1=gate[j][:, blk(t)], op0=ALU.add, op1=ALU.mult).then_inc(y_gated, 1)
                    dve.wait_ge(y_gated, START + n * KC + m + 1)
                    nc.vector.tensor_tensor(acc[:, m, blk(t)], acc[:, m, blk(t)], y[:, t % 2, m, :],
                                            ALU.add).then_inc(added, 1)

            def step(e, j, t, last):
                if t == 2 and not (last and j == 1):
                    weights_low(e + 1, 1 - j)
                following = next_block(e, j, t, last)
                if kind == "relu" and following:
                    hidden_low(*following)
                if kind == "glu" and following:
                    gated_unit(*following)
                outputs(e, j, t)
                if kind == "glu" and following:
                    hidden_low(*following)

            dve.sem_inc(added, 4)
            if low_credit:
                dve.sem_inc(h_lows, low_credit)
            weights_low(0, 0)
            if kind == "glu":
                gated_unit(0, 0, 0)
            if hc:
                hidden_low(0, 0, 0)
            rounds(dve, step)


def rms_norm(core, t, w):
    nc = core.nc
    with ExitStack() as mem:
        def sb(name, shape):
            return mem.enter_context(nc.sbuf_tensor(f"{name}_{core.turn}", shape, F32))
        sq, std, inv = sb("sq", [P, 2, KC, BLK]), sb("std", [P, 2, KC, BLK]), sb("inv", [P, 2, KC, BLK])
        block, squared, mean_ready, std_ready, inverted, done = mem.enter_context(
            phase(core, "squared", "mean_ready", "std_ready", "inverted", "done"))

        @block.gpsimd
        def _(pool):
            for n in range(NB):
                if n >= 2:
                    pool.wait_ge(mean_ready, START + n - 1)
                nc.gpsimd.tensor_tensor(sq[:, n % 2, :, :], t[:, :, blk(n)], t[:, :, blk(n)], ALU.mult)\
                  .then_inc(squared, 1)

        @block.tensor
        def _(pe):
            for n in range(NB):
                pe.wait_ge(squared, START + n + 1)
                if n >= 2:
                    pe.wait_ge(std_ready, START + n - 1)
                for k in range(KC):
                    ins = pe.matmul(core.psum[2 * (n % 2) + k], core.consts["same_head"][:, :],
                                    sq[:, n % 2, k, :], start=True, stop=True)
                ins.then_inc(mean_ready, 1)

        @block.scalar
        def _(act):
            for n in range(NB):
                act.wait_ge(mean_ready, START + n + 1)
                if n >= 2:
                    act.wait_ge(inverted, START + n - 1)
                nc.scalar.activation(std[:, n % 2, :, :], core.banks8[:, 2 * (n % 2):2 * (n % 2) + 2, :], ACT.Sqrt,
                                     bias=core.eps[:, 1:2]).then_inc(std_ready, 1)

        @block.vector
        def _(dve):
            for n in range(NB):
                dve.wait_ge(std_ready, START + n + 1)
                nc.vector.reciprocal(inv[:, n % 2, :, :], std[:, n % 2, :, :]).then_inc(inverted, 1)
                dve.wait_ge(inverted, START + n + 1)
                dve.wait_ge(squared, START + n + 1)
                for k in range(KC):
                    nc.vector.scalar_tensor_tensor(out=t[:, k, blk(n)], in0=inv[:, n % 2, k, :],
                                                   scalar=w[:, k:k + 1], in1=t[:, k, blk(n)], op0=ALU.mult,
                                                   op1=ALU.mult).then_inc(done, 1)


def elementwise(core, *steps):
    with phase(core, "step") as (block, step):
        @block.vector
        def _(dve):
            for n, f in enumerate(steps):
                f().then_inc(step, 1)
                dve.wait_ge(step, START + n + 1)


class Butterfly:

    HIDDEN, STAGES = 4 * D, 10

    def __init__(self, core, mem, name, stage_w, backwards, source, result, row_source=None, row_result=None):
        self.core, self.stage_w, self.backwards = core, stage_w, backwards
        self.source, self.result, self.row_source, self.row_result = source, result, row_source, row_result

        def sb(n, *shape):
            return mem.enter_context(core.nc.sbuf_tensor(f"{name}_{n}", list(shape), F32))
        self.w = sb("w", P, KC, self.HIDDEN)
        self.row = sb("row", 1, self.HIDDEN) if row_source is not None else None
        self.sw = [sb(f"stage{j}", P, 2 * self.HIDDEN) for j in range(2)]
        self.t = [sb(f"t{j}", P, KC, self.HIDDEN // 2) for j in range(4)]
        self.tr = [sb(f"tr{j}", 1, self.HIDDEN // 2) for j in range(4)] if self.row is not None else None
        self.order = list(range(self.STAGES - 1, -1, -1) if backwards else range(self.STAGES))
        self.stage_in0, self.stage_in1, self.step, self.source_in, self.kept = (
            core.ctx.enter_context(core.nc.semaphore(f"{name}_{n}"))
            for n in ("stage_in0", "stage_in1", "step", "source_in", "kept"))
        self.stage_in = [self.stage_in0, self.stage_in1]
        self.done, self.n_in = 0, 1 + (self.row is not None)

    def fetch_source(self, queue):
        queue.dma_start(self.w[:, :, :], chunks(self.source)).then_inc(self.source_in, 16)
        if self.row is not None:
            queue.dma_start(self.row[:, :], self.row_source).then_inc(self.source_in, 16)

    def fetch_stage(self, queue, n):
        st = self.order[n]
        queue.dma_start(self.sw[n % 2][:, :], self.stage_w[st:st + 1, :].broadcast_to([P, 2 * self.HIDDEN]))\
             .then_inc(self.stage_in[n % 2], 16)

    def per_stage(self):
        return 6 * (KC + (self.row is not None))

    def stage(self, eng, ops, n):
        half = 2 ** self.order[n]
        eng.wait_ge(self.source_in, 16 * self.n_in)
        eng.wait_ge(self.stage_in[n % 2], 16 * (n // 2 + 1))
        wv = self.sw[n % 2][:, :].rearrange("p (b s q) -> p b s q", s=half, q=4)
        both = []
        for c in range(KC):
            v = self.w[:, c, :].rearrange("p (b h s) -> p b h s", h=2, s=half)
            both.append((v[:, :, 0, :], v[:, :, 1, :], wv, [x[:, c, :] for x in self.t]))
        if self.row is not None:
            v = self.row[:, :].rearrange("p (b h s) -> p b h s", h=2, s=half)
            both.append((v[:, :, 0, :], v[:, :, 1, :], wv[0:1], [x[:, :] for x in self.tr]))
        terms = [(0, 0), (2, 1), (1, 0), (3, 1)] if self.backwards else [(0, 0), (1, 1), (2, 0), (3, 1)]
        if n:
            eng.wait_ge(self.step, self.done)
        for a, b, ww, tt in both:
            for i, (q, which) in enumerate(terms):
                ops.tensor_tensor(tt[i].rearrange("p (b s) -> p b s", s=half), (a, b)[which], ww[:, :, :, q],
                                  ALU.mult).then_inc(self.step, 1)
                self.done += 1
        eng.wait_ge(self.step, self.done)
        for a, b, ww, tt in both:
            for o, i in ((a, 0), (b, 2)):
                tv = [x.rearrange("p (b s) -> p b s", s=half) for x in tt[i:i + 2]]
                ops.tensor_tensor(o, tv[0], tv[1], ALU.add).then_inc(self.step, 1)
                self.done += 1

    def keep_result(self, queue):
        queue.wait_ge(self.step, self.STAGES * self.per_stage())
        queue.dma_start(chunks(self.result), self.w[:, :, :]).then_inc(self.kept, 16)
        if self.row is not None:
            queue.dma_start(self.row_result, self.row[:, :]).then_inc(self.kept, 16)
        queue.wait_ge(self.kept, 16 * self.n_in)


def turn_weights(core, src, dst, row=None, row_dst=None):
    nc = core.nc
    with phase(core, "turned", "taken") as (block, turned, taken):
        @block.tensor
        def _(pe):
            for h in range(8):
                for c in range(KC):
                    ins = pe.transpose(core.psum[h % 4][:, c * P:(c + 1) * P] if h < 4 else
                                       core.psum[h % 4][:, (2 + c) * P:(3 + c) * P],
                                       src[:, c, h * P:(h + 1) * P], core.ident[:, :])
            if row is not None:
                for h in range(8):
                    ins = pe.transpose(core.psum[4][:, h:h + 1], row[:, h * P:(h + 1) * P], core.ident[0:1, 0:1])
            ins.then_inc(turned, 1)

        @block.vector
        def _(dve):
            dve.wait_ge(turned, START + 1)
            for half in range(2):
                nc.vector.tensor_copy(dst[:, 4 * half:4 * half + 4, :],
                                      core.banks8[:, 0:4, half * D:(half + 1) * D]).then_inc(taken, 1)
            if row is not None:
                nc.vector.tensor_copy(row_dst[:, :], core.psum[4][:, 0:8]).then_inc(taken, 1)


def context_mean(core, x, tops, mixed, product):
    nc = core.nc
    nb = BLK // S
    with ExitStack() as mem:
        def sb(name, shape):
            return mem.enter_context(nc.sbuf_tensor(f"{name}_{core.turn}", shape, F32))
        diag = sb("diag", [P, 4, P])
        z, e = sb("z", [P, nb, S]), sb("e", [P, nb, S])
        top, total, inv = (sb(n, [P, nb]) for n in ("top", "total", "inv"))
        wx, bar = sb("wx", [P, KC, BLK]), sb("bar", [P, KC * nb])
        block, diag_ready, spread, centred, exped, step, product_made = mem.enter_context(
            phase(core, "diag_ready", "spread", "centred", "exped", "step", "product_made"))

        @block.tensor
        def _(pe):
            for t in range(NB):
                pe.wait_ge(diag_ready, START + t + 1)
                pe.matmul(core.psum[t], core.consts["ones"][:, :], diag[:, :, :].rearrange("p g w -> p (g w)"),
                          start=True, stop=True).then_inc(spread, 1)

        @block.gpsimd
        def _(pool):
            for t in range(NB):
                if t >= 1:
                    pool.wait_ge(spread, START + t)
                nc.gpsimd.tensor_tensor(diag[:, :, :], bcast(core.ident[:, :], 4),
                                        bcast(tops[:, 4 * t:4 * t + 4], P, 2), ALU.mult).then_inc(diag_ready, 1)
            nc.gpsimd.tensor_tensor(product[0][:, :, :], product[1][:, :, :], product[2][:, :, :], ALU.mult)\
              .then_inc(product_made, 1)
            pool.wait_ge(product_made, START + 1)

        @block.scalar
        def _(act):
            for t in range(NB):
                act.wait_ge(centred, START + t + 1)
                nc.scalar.activation(e[:, :, :], z[:, :, :], ACT.Exp).then_inc(exped, 1)

        @block.vector
        def _(dve):
            n = 0

            def then(ins):
                nonlocal n
                n += 1
                ins.then_inc(step, 1)
                dve.wait_ge(step, START + n)

            for t in range(NB):
                dve.wait_ge(spread, START + t + 1)
                m = core.psum[t].rearrange("p (b s) -> p b s", s=S)
                then(nc.vector.tensor_reduce(top[:, :], m, AX, ALU.max))
                nc.vector.tensor_tensor(z[:, :, :], m, bcast(top[:, :], S, 2), ALU.subtract).then_inc(centred, 1)
                dve.wait_ge(exped, START + t + 1)
                then(nc.vector.tensor_reduce(total[:, :], e[:, :, :], AX, ALU.add))
                then(nc.vector.reciprocal(inv[:, :], total[:, :]))
                then(nc.vector.tensor_tensor(e[:, :, :], e[:, :, :], bcast(inv[:, :], S, 2), ALU.mult))
                then(nc.vector.tensor_tensor(wx[:, :, :], x[:, :, blk(t)],
                                             bcast(e[:, :, :].rearrange("p b s -> p (b s)"), KC), ALU.mult))
                then(nc.vector.tensor_reduce(bar[:, :], wx[:, :, :].rearrange("p k (b s) -> p (k b) s", s=S), AX,
                                             ALU.add))
                for k in range(KC):
                    then(nc.vector.tensor_tensor(
                        mixed[:, k, blk(t)].rearrange("p (b s) -> p b s", s=S),
                        x[:, k, blk(t)].rearrange("p (b s) -> p b s", s=S),
                        bcast(bar[:, k * nb:(k + 1) * nb], S, 2), ALU.mult))


def perceiver(nc, dram, out, scratch, layers=12):
    with ExitStack() as ctx:
        core = Core(nc, ctx, dram)
        start(core)
        steps = [l0_xattn, l0_attn, l0_ffn, l1_xattn, l1_attn, l1_ffn, l2_xattn, l2_attn, l2_ffn, l3_xattn,
                 l3_attn, l3_ffn]
        for step in steps[:layers]:
            with ExitStack() as mem:
                turn = core.turn

                def sb(name, *shape, dt=F32):
                    return mem.enter_context(nc.sbuf_tensor(f"{name}_{turn}", list(shape), dt))
                step(core, sb, scratch)
        store(core, core.x, out)


def weights(core, sb, layer, mats, vecs=()):
    got, pairs = [], []
    for name in mats:
        d = core.dram[f"{layer}_{name}"]
        tile = sb(name, P, d.shape[0] // P, d.shape[1])
        pairs.append((tile[:, :, :], chunks(d)))
        got.append(tile)
    for name in vecs:
        d = core.dram[f"{layer}_{name}"]
        tile = sb(name, P, d.shape[1])
        pairs.append((tile[:, :], d if d.shape[0] == P else d.broadcast_to([P, d.shape[1]])))
        got.append(tile)
    core.pending += pairs
    return got


def split_tiles(core, sb):
    return sb("x_high", P, KC, N, dt=F32R), sb("x_low", P, KC, N, dt=F32R)


def l0_xattn(core, sb, scratch):
    q1, k1, o1, q2, k2, o2, f1, f2, fb1, fb2, g1, b1, g2, b2, g3, b3 = weights(
        core, sb, "L0_xattn", ["q1W", "w1W", "o1W", "q2W", "w2W", "o2W", "ffW1", "ffW2"],
        ["ffb1", "ffb2", "g1", "b1", "g2", "b2", "g3", "b3"])
    xn, q, k, o = (sb(n, P, KC, N) for n in ("xn", "q", "k", "o"))
    layer_norm(core, core.x, xn, jobs=((q1, q, None), (k1, k, None)))
    self_attention(core, "heads", q, k, k, o, KC, 0.25, core.consts["mask_block"])
    linear(core, o1, o, xn, kind="residual")
    layer_norm(core, xn, xn, (g1, b1))
    linear(core, q2, xn, q)
    tail_values(core, k2, scratch["tails"])
    cross_attention(core, q, k2, None, o, core.dram["ctx_t"], scratch["tails"], mask=core.dram["mask"])
    linear(core, o2, o, xn, kind="residual")
    layer_norm(core, xn, xn, (g2, b2))
    with ExitStack() as mem:
        d = core.dram
        down = Butterfly(core, mem, "down", d["L2_ffn_down_weights"], True, d["L2_ffn_W_con_t"], scratch["w_down"])
        mlp(core, xn, f1, fb1, f2, fb2, xn, aside=down)
    layer_norm(core, xn, core.x, (g3, b3), add=core.x)


def mlp(core, x, w1, b1, w2, b2, out, aside=None):
    nc = core.nc
    HC = 8
    with ExitStack() as mem:
        h = mem.enter_context(nc.sbuf_tensor(f"h_{core.turn}", [P, 2, HC, BLK], F32))
        block, h_made, h_ready, y_made, y_taken = mem.enter_context(
            phase(core, "h_made", "h_ready", "y_made", "y_taken"))
        if aside:
            @block.sync
            def _(sp):
                aside.fetch_source(sp)
                for n in range(aside.STAGES):
                    if n >= 2:
                        sp.wait_ge(aside.step, (n - 1) * aside.per_stage())
                    aside.fetch_stage(sp, n)
                aside.keep_result(sp)

        @block.tensor
        def _(pe):
            def first(t):
                for m in range(HC):
                    n = t * HC + m
                    if n >= 4:
                        pe.wait_ge(h_ready, START + n - 3)
                    for k in range(KC):
                        ins = pe.matmul(core.psum[m % 4], w1[:, k, m * P:(m + 1) * P], x[:, k, blk(t)],
                                        start=(k == 0), stop=(k == KC - 1))
                    ins.then_inc(h_made, 1)

            def second(t):
                pe.wait_ge(h_ready, START + (t + 1) * HC)
                for m in range(KC):
                    if t >= 2:
                        pe.wait_ge(y_taken, START + (t - 2) * KC + m + 1)
                    for k in range(HC):
                        ins = pe.matmul(core.psum[4 + 2 * (t % 2) + m], w2[:, k, m * P:(m + 1) * P],
                                        h[:, t % 2, k, :], start=(k == 0), stop=(k == HC - 1))
                    ins.then_inc(y_made, 1)

            first(0)
            for t in range(NB):
                if t + 1 < NB:
                    first(t + 1)
                second(t)

        @block.scalar
        def _(act):
            for t in range(NB):
                for m in range(HC):
                    act.wait_ge(h_made, START + t * HC + m + 1)
                    if t >= 2:
                        act.wait_ge(y_made, START + (t - 1) * KC)
                    nc.scalar.activation(h[:, t % 2, m, :], core.psum[m % 4], ACT.Gelu, bias=b1[:, m:m + 1])\
                      .then_inc(h_ready, 1)

        @block.vector
        def _(dve):
            stages = [range(0, 4), range(4, 7), range(7, 10), ()]
            if aside:
                for n in stages[0]:
                    aside.stage(dve, nc.vector, n)
            for t in range(NB):
                dve.wait_ge(h_made, START + (t + 1) * HC)
                for m in range(KC):
                    dve.wait_ge(y_made, START + t * KC + m + 1)
                    nc.vector.scalar_tensor_tensor(out=out[:, m, blk(t)], in0=core.psum[4 + 2 * (t % 2) + m],
                                                   scalar=b2[:, m:m + 1], in1=out[:, m, blk(t)], op0=ALU.add,
                                                   op1=ALU.add).then_inc(y_taken, 1)
                if aside and t + 1 < NB:
                    for n in stages[t + 1]:
                        aside.stage(dve, nc.vector, n)


def l0_attn(core, sb, scratch):
    wqkv, wo, bqkv, bo = weights(core, sb, "L0_attn", ["W_qkv", "W_out"], ["b_qkv", "b_out"])
    parts = [scratch["qkv"][i * D:(i + 1) * D, :] for i in range(3)]
    with ExitStack() as mem:
        nc = core.nc
        xn = mem.enter_context(nc.sbuf_tensor("seg_xn", [P, KC, N], F32))
        qkv = mem.enter_context(nc.sbuf_tensor("seg_qkv", [P, 6, N], F32))
        layer_norm(core, core.x, xn, jobs=((wqkv, qkv, bqkv),), mc=6)
        load(core, *[(chunks(parts[i]), qkv[:, 2 * i:2 * i + 2, :]) for i in range(3)])
    self_attention(core, "segments", *parts, scratch["seg_out"], KC, 512 ** -0.5, core.consts["mask_segments"])
    o = sb("o", P, KC, N)
    load(core, (o[:, :, :], chunks(scratch["seg_out"])))
    linear(core, wo, o, core.x, bias=bo, kind="residual")


def l0_ffn(core, sb, scratch):
    gw, gb = weights(core, sb, "L0_ffn", ["gate_w"], ["gate_b"])
    d = core.dram
    parts = split_tiles(core, sb)
    with ExitStack() as mem:
        xn = mem.enter_context(core.nc.sbuf_tensor("l0_ffn_xn", [P, KC, N], F32))
        layer_norm(core, core.x, xn)
        gates(core, xn, parts, gw, gb, scratch["gates"], 8)
    with ExitStack() as mem:
        up = Butterfly(core, mem, "up", d["L2_ffn_up_weights"], False, d["L2_ffn_W_exp"], scratch["w_up"],
                       d["L2_ffn_b_exp"], scratch["b_up"])
        experts_sum(core, "relu", parts, core.x, scratch["gates"], 8, d["L0_ffn_w1"], d["L0_ffn_w2"], d["L0_ffn_b1"],
                    d["L0_ffn_b2"], hidden=512, aside=up)


def l1_xattn(core, sb, scratch):
    nc = core.nc
    wq, wk, wv, wo, w_rel = weights(core, sb, "L1_xattn", ["w_q", "w_k", "w_v", "w_proj"], ["w_rel"])
    xn, q, o, rel = sb("xn", P, KC, N), sb("q", P, KC, N), sb("o", P, KC, N), sb("rel", P, 4, M)
    layer_norm(core, core.x, xn, jobs=((wq, q, None),))
    elementwise(core, *[lambda n=n: nc.vector.tensor_scalar(rel[:, n, :], core.consts["positions"][:, :],
                                                            w_rel[:, n:n + 1], None, ALU.mult) for n in range(4)])
    tail_values(core, wv, scratch["tails"])
    cross_attention(core, q, wk, wv, o, core.dram["ctx_t"], scratch["tails"], rel=rel)
    linear(core, wo, o, core.x, kind="residual")


def l1_attn(core, sb, scratch):
    wq, wv, qw, vw = weights(core, sb, "L1_attn", ["Wq", "Wv"], ["q_norm_w", "v_norm_w"])
    xn, q, v = (sb(n, P, KC, N) for n in ("xn", "q", "v"))
    layer_norm(core, core.x, xn, jobs=((wq, q, None), (wv, v, None)))
    rms_norm(core, q, qw)
    rms_norm(core, v, vw)
    self_attention(core, "linear", q, xn, v, core.x, KC, mask=core.consts["mask_lower"], residual=True)


def l1_ffn(core, sb, scratch):
    nc = core.nc
    wq, wk, wv, wo, wg, bq, bk, bv, bo, g1, be1, g2, be2, bg = weights(
        core, sb, "L1_ffn", ["Wq", "Wk", "Wv", "Wo", "Wg"],
        ["bq", "bk", "bv", "bo", "g1", "be1", "g2", "be2", "bg"])
    xn, q, k, v, o = (sb(n, P, KC, N) for n in ("xn", "q", "k", "v", "o"))
    d = core.dram
    layer_norm(core, core.x, xn, jobs=((wq, q, bq), (wk, k, bk), (wv, v, bv)))
    self_attention(core, "heads", q, k, v, o, KC, 0.25, core.consts["mask_block"])
    linear(core, wo, o, q, bias=bo)
    layer_norm(core, q, xn, (g1, be1), add=xn)
    parts = split_tiles(core, sb)
    gates(core, xn, parts, wg, bg, scratch["gates"], 8,
          aside=(lambda: nc.gpsimd.memset(k[:, :, :], 0.0),
                 lambda: nc.gpsimd.tensor_tensor(core.x[:, :, :], core.x[:, :, :], xn[:, :, :], ALU.add)))
    experts_sum(core, "plain", parts, k, scratch["gates"], 8, d["L1_ffn_We"], None, b2=d["L1_ffn_bexp"])
    layer_norm(core, k, core.x, (g2, be2), add=core.x)


def l2_xattn(core, sb, scratch):
    nc = core.nc
    wqv, w_sim, b_sim, bqv = weights(core, sb, "L2_xattn", ["W_qv"], ["w_sim", "b_sim", "b_qv"])
    xn, q, hat, mixed, tops = (sb("xn", P, KC, N), sb("q", P, KC, N), sb("hat", P, KC, N),
                               sb("mixed", P, KC, N), sb("tops", P, NG))
    d = core.dram
    layer_norm(core, core.x, xn)
    elementwise(core, *[lambda k=k: nc.vector.tensor_scalar(q[:, k, :], xn[:, k, :], w_sim[:, 4 + k:5 + k],
                                                            w_sim[:, 2 + k:3 + k], ALU.mult, ALU.add)
                        for k in range(KC)])
    cross_single(core, q, hat, d["ctx_t"], d["ctx"], w_sim, xn, b_sim[:, 0:1], tops=tops)
    context_mean(core, xn, tops, mixed, (q, hat, xn))
    linear(core, wqv, (xn, hat, q, mixed), core.x, bias=bqv, kind="residual", kc=8)


def l2_attn(core, sb, scratch):
    wq, wk, wv = weights(core, sb, "L2_attn", ["W_Q", "W_K", "W_V"])
    xn, q, k = (sb(n, P, KC, N) for n in ("xn", "q", "k"))
    layer_norm(core, core.x, xn, jobs=((wq, q, None), (wk, k, None)))
    single_attention(core, q, k, xn, wv, core.x, D ** -0.5, core.consts["mask_causal"])


def l2_ffn(core, sb, scratch):
    nc = core.nc
    up_bias, b_con, down_bias = weights(core, sb, "L2_ffn", [], ["up_bias", "b_con", "down_bias"])
    w_up, w_con_t, row = sb("w_up", P, KC, 4 * D), sb("w_con_t", P, KC, 4 * D), sb("row", 1, 4 * D)
    xn, w_down, hb = sb("xn", P, KC, N), sb("w_down", P, 8, D), sb("hb", P, 8)
    core.pending += [(w_up[:, :, :], chunks(scratch["w_up"])), (w_con_t[:, :, :], chunks(scratch["w_down"])),
                     (row[:, :], scratch["b_up"])]
    layer_norm(core, core.x, xn)
    turn_weights(core, w_con_t, w_down, row, hb)
    elementwise(core, lambda: nc.vector.tensor_tensor(hb[:, :], hb[:, :], up_bias[:, :], ALU.add),
                lambda: nc.vector.tensor_tensor(b_con[:, :], b_con[:, :], down_bias[:, :], ALU.add))
    mlp(core, xn, w_up, hb, w_down, b_con, core.x)


def l3_xattn(core, sb, scratch):
    nc = core.nc
    wq, wk, wv, bq, bk, bv, betas = weights(core, sb, "L3_xattn", ["Wq", "Wk", "Wv"], ["bq", "bk", "bv", "betas"])
    xn, q, qk, o, phi_w, zero = (sb("xn", P, KC, N), sb("q", P, KC, N), sb("qk", P, KC, N), sb("o", P, KC, N),
                                 sb("phi_w", P, 1), sb("zero", P, 1))
    d = core.dram
    layer_norm(core, core.x, xn, jobs=((wq, q, bq),))
    elementwise(core, lambda: nc.vector.tensor_scalar(q[:, :, :], q[:, :, :], D ** -0.5, None, ALU.mult),
                lambda: nc.vector.memset(zero[:, :], 0.0),
                lambda: nc.vector.tensor_tensor(phi_w[:, :], betas[:, 0:1], betas[:, 1:2], ALU.add),
                lambda: nc.vector.tensor_tensor(phi_w[:, :], phi_w[:, :], betas[:, 2:3], ALU.subtract))
    linear(core, wk, q, qk)
    cross_single(core, qk, o, d["ctx_t"], d["ctx"], bk, q, zero[:, 0:1], phi=d["fside"], phi_w=phi_w[:, 0:1])
    linear(core, wv, o, core.x, bias=bv, kind="residual")


def l3_attn(core, sb, scratch):
    lb, bq, bk, bv = weights(core, sb, "L3_attn", [], ["l_b", "q_b", "k_b", "v_b"])
    d = core.dram
    wq, wk, wv = (sb(n, P, KC, 512) for n in ("wq", "wk", "wv"))
    wl = sb("wl", P, 8, D)

    def fetch(half):
        return [(t[:, :, :], chunks(d[f"L3_attn_{n}"][:, half * 512:(half + 1) * 512]))
                for n, t in (("q_w", wq), ("k_w", wk), ("v_w", wv))]

    core.pending += fetch(0) + [(wl[:, :, :], chunks(d["L3_attn_l_w"]))]
    xn = sb("xn", P, KC, N)
    q, k, v = (sb(n, P, 4, N) for n in ("q", "k", "v"))
    for half in range(2):
        jobs = [(w, t, b[:, 4 * half:4 * half + 4]) for w, b, t in ((wq, bq, q), (wk, bk, k), (wv, bv, v))]
        if half == 0:
            layer_norm(core, core.x, xn, jobs=jobs, mc=4)
        else:
            linears(core, *[(w, xn, t, b) for w, t, b in jobs], mc=4)
        if half == 0:
            core.pending += fetch(1)
        self_attention(core, "columns", k, q, v, q, 4, 0.125, core.consts["mask_block"])
        linear(core, wl[:, 4 * half:4 * half + 4, :], q, core.x, bias=lb if half == 0 else None, kind="residual",
               kc=4)


def l3_ffn(core, sb, scratch):
    nc = core.nc
    (wr,) = weights(core, sb, "L3_ffn", ["Wr"])
    d = core.dram
    xn, no_bias = sb("xn", P, KC, N), sb("no_bias", P, 16)
    layer_norm(core, core.x, xn)
    elementwise(core, lambda: nc.vector.memset(no_bias[:, :], 0.0))
    parts = split_tiles(core, sb)
    gates(core, xn, parts, wr, no_bias, scratch["gates"], 16, shared=2)
    experts_sum(core, "glu", parts, core.x, scratch["gates"], 18, d["L3_ffn_Wgu"], d["L3_ffn_Wd"], hidden=P)


def shape_constants():
    import numpy as np
    f, r = np.float32, np.arange(128)
    same = r[:, None] // 32 == r[None, :] // 32
    lower = same & (r[:, None] >= r[None, :])
    seg, tok = r // 8, r % 8
    at = tok % 2 * 16 + seg
    own = (tok[:, None] // 2 == tok[None, :] // 2) & (at[:, None] >= at[None, :])
    hide = f(-1e30)
    return {
        "ident": np.eye(128, dtype=f),
        "mask_block": np.where(same, f(0), hide),
        "mask_causal": np.where(lower, f(0), hide),
        "mask_lower": lower.astype(f),
        "mask_segments": np.where(own, f(0), hide),
        "head_of_8": (r[:, None] // 16 == np.arange(8)[None, :]).astype(f),
        "head_of_2": (r[:, None] // 64 == np.arange(2)[None, :]).astype(f),
        "own_head": (r[:, None] // 32 == np.arange(64)[None, :] // 16).astype(f),
        "batch_of_4": (r[:, None] // 32 == np.arange(4)[None, :]).astype(f),
        "query_sel": (r[:, None] % 32 == np.arange(32)[None, :]).astype(f),
        "same_head": (r[:, None] // 16 == r[None, :] // 16).astype(f) / 16,
        "iota16": np.tile(np.arange(16, dtype=f), (128, 1)),
        "ones": np.ones((128, 128), f),
        "positions": (r[:, None] % 32 - np.arange(257)[None, :]).astype(f),
    }


def laid_out(inputs):
    import numpy as np
    a = {k: np.asarray(v) for k, v in inputs.items()}

    def vec(b):
        return b.reshape(-1, 128).T

    def heads_cols(w):
        return w.reshape(-1, 16, 16).transpose(0, 2, 1).reshape(-1, 256)

    out = {"x": a["x"].reshape(2048, 256).T, "ctx": a["ctx_1024"], "ctx_t": a["ctx_1024"].transpose(0, 2, 1),
           "ctx_last_t": a["ctx_1024"][:, 256, :].T,
           "fside": a["fside_BxSxS2_0"].reshape(2048, 257),
           "mask": a["mask_Bx1xS2x1_bk0"].reshape(64, 1, 257)}
    n = "L0_xattn_"
    for w in ("q1W", "w1W", "q2W", "w2W"):
        out[n + w] = heads_cols(a[n + w])
    for w in ("o1W", "o2W"):
        out[n + w] = heads_cols(a[n + w].T).T
    for w in ("ffW1", "ffW2"):
        out[n + w] = a[n + w]
    for b in ("ffb1", "ffb2", "g1", "b1", "g2", "b2", "g3", "b3"):
        out[n + b] = vec(a[n + b])
    n = "L0_attn_"
    parts = a[n + "W_qkv"].reshape(256, 16, 3, 16).transpose(0, 2, 1, 3).reshape(256, 768)
    out[n + "W_qkv"] = parts
    out[n + "b_qkv"] = vec(a[n + "b_qkv"].reshape(16, 3, 16).transpose(1, 0, 2).reshape(768))
    out[n + "W_out"], out[n + "b_out"] = a[n + "W_out"], vec(a[n + "b_out"])
    n = "L0_ffn_"
    out[n + "gate_w"], out[n + "gate_b"] = a[n + "gate_w"], a[n + "gate_b"].reshape(1, 8)
    out[n + "w1"], out[n + "w2"] = a[n + "w1"], a[n + "w2"]
    out[n + "b1"] = a[n + "b1"].reshape(8, 4, 128).transpose(0, 2, 1)
    out[n + "b2"] = a[n + "b2"].reshape(8, 2, 128).transpose(0, 2, 1)
    n = "L1_xattn_"
    out[n + "w_q"], out[n + "w_proj"] = a[n + "w_q"], a[n + "w_proj"]
    out[n + "w_k"], out[n + "w_v"] = a[n + "w_kv"][:, :256], a[n + "w_kv"][:, 256:]
    out[n + "w_rel"] = np.repeat(a[n + "w_rel"].reshape(4, 4).T, 32, axis=0)
    n = "L1_attn_"
    out[n + "Wq"], out[n + "Wv"] = a[n + "Wq"].T, a[n + "Wv"].T
    out[n + "q_norm_w"], out[n + "v_norm_w"] = vec(a[n + "q_norm_w"].reshape(-1)), vec(a[n + "v_norm_w"].reshape(-1))
    n = "L1_ffn_"
    for w in ("Wq", "Wk", "Wv", "Wo", "Wg", "We"):
        out[n + w] = a[n + w]
    for b in ("bq", "bk", "bv", "bo", "g1", "be1", "g2", "be2"):
        out[n + b] = vec(a[n + b])
    out[n + "bg"] = a[n + "bg"].reshape(1, 8)
    out[n + "bexp"] = a[n + "bexp"].reshape(8, 2, 128).transpose(0, 2, 1)
    n = "L2_xattn_"
    out[n + "W_qv"], out[n + "w_sim"] = a[n + "W_qv"], vec(a[n + "w_sim"])
    out[n + "b_sim"], out[n + "b_qv"] = a[n + "b_sim"].reshape(1, 1), vec(a[n + "b_qv"])
    n = "L2_attn_"
    for w in ("W_Q", "W_K", "W_V"):
        out[n + w] = a[n + w]
    n = "L2_ffn_"
    out[n + "W_exp"], out[n + "W_con_t"] = a[n + "W_exp"], a[n + "W_con"].T
    out[n + "b_exp"] = a[n + "b_exp"].reshape(1, 1024)
    for w in ("up_weights", "down_weights"):
        out[n + w] = a[n + w].reshape(10, 2048)
    for b in ("up_bias", "b_con", "down_bias"):
        out[n + b] = vec(a[n + b])
    n = "L3_xattn_"
    out[n + "Wq"], out[n + "Wk"], out[n + "Wv"] = a[n + "Wq"].T, a[n + "Wk"], a[n + "Wv"].T
    for b in ("bq", "bk", "bv"):
        out[n + b] = vec(a[n + b])
    out[n + "betas"] = np.stack([a[n + "beta_risk"], a[n + "beta_prio"], a[n + "beta_impl"]]).reshape(1, 3)
    n = "L3_attn_"
    for w in "qkv":
        out[n + w + "_w"] = a[n + w + "_w"].reshape(1024, 256).T
        out[n + w + "_b"] = vec(a[n + w + "_b"].reshape(-1))
    out[n + "l_w"], out[n + "l_b"] = a[n + "l_w"].T, vec(a[n + "l_b"].reshape(-1))
    n = "L3_ffn_"
    out[n + "Wr"] = a[n + "Wr"]
    gate = np.concatenate([a[n + "Wg"], a[n + "Sg"].reshape(256, 2, 128).transpose(1, 0, 2)])
    up = np.concatenate([a[n + "Wu"], a[n + "Su"].reshape(256, 2, 128).transpose(1, 0, 2)])
    out[n + "Wgu"] = np.concatenate([gate, up], axis=2)
    out[n + "Wd"] = np.concatenate([a[n + "Wd"], a[n + "Sd"].reshape(2, 128, 256)])
    return {k: np.ascontiguousarray(v) for k, v in out.items()}


def kernel(**inputs):
    import numpy as np
    import concourse.bacc as bacc
    from concourse.bass_utils import run_bass_kernel_spmd

    arrays = {**laid_out(inputs), **shape_constants()}
    nc = bacc.Bacc("TRN2", target_bir_lowering=False, num_devices=1)
    dram = {k: nc.dram_tensor(f"in_{k}", v.shape, mybir.dt.from_np(v.dtype), kind="ExternalInput").ap()
            for k, v in arrays.items()}
    out = nc.dram_tensor("out_0_dram", (D, N), F32, kind="ExternalOutput").ap()
    scratch = {k: nc.dram_tensor(f"scratch_{k}", shape, F32, kind="Internal").ap()
               for k, shape in {"qkv": (3 * D, N), "seg_out": (D, N), "gates": (18, N), "tails": (B, D), "w_up": (D, 4 * D),
                                "w_down": (D, 4 * D), "b_up": (1, 4 * D)}.items()}
    perceiver(nc, dram, out, scratch)
    r = run_bass_kernel_spmd(nc, [{f"in_{k}": v for k, v in arrays.items()}], core_ids=[0])
    return r.results[0]["out_0_dram"].T.reshape(B, S, D)
```
